# Optimizing a Trainium2 kernel written in Bass

```python
import numpy as np
import jax
import jax.numpy as jnp

def _softmax(x, axis=-1):
    return jax.nn.softmax(x, axis=axis)

def _gelu(x):
    return jax.nn.gelu(x, approximate=True)

def _silu(x):
    return jax.nn.silu(x)

def _sigmoid(x):
    return jax.nn.sigmoid(x)

def _layernorm(x, axis=-1, eps=1e-05):
    m = jnp.mean(x, axis=axis, keepdims=True)
    v = jnp.var(x, axis=axis, keepdims=True)
    return (x - m) / jnp.sqrt(v + eps)

def _scatter_add(tgt, idx, src, axis=0):
    return tgt.at[idx].add(src)

def _segment_sum(src, seg, n):
    return jax.ops.segment_sum(src, seg, n)
kernel_name = 'mk_macaron_d1_jaxref_r8_5dbe2b'

def setup_inputs(seed: int=0):
    np.random.seed(seed)
    _w = jnp.asarray

    def _L0_attn_setup():
        import jax, jax.numpy as jnp
        import numpy as np
        from jax import lax
        BATCH, SEQ, DMODEL = (2, 256, 128)
        EXPAND, HEADDIM, DSTATE, DCONV, MLP_INNER = (2, 64, 64, 4, 512)
        DIN = EXPAND * DMODEL
        NH = DIN // HEADDIM
        CONV_DIM = DIN + 2 * DSTATE
        DPROJ = 2 * DIN + 2 * DSTATE + NH
        EPS = 1e-05

        def rmsnorm(x, w):
            return x * lax.rsqrt(jnp.mean(x * x, axis=-1, keepdims=True) + EPS) * w

        def _mamba2(x, W_in, conv_w, conv_b, dt_bias, A_log, D_param, norm_w, W_out):
            b, l, _ = x.shape
            zxbcdt = x @ W_in
            z = zxbcdt[..., :DIN]
            xBC = zxbcdt[..., DIN:DIN + CONV_DIM]
            dt = zxbcdt[..., DIN + CONV_DIM:]
            xt = jnp.pad(xBC, ((0, 0), (DCONV - 1, 0), (0, 0))).transpose(0, 2, 1)
            conv = lax.conv_general_dilated(xt, conv_w[:, None, :], (1,), 'VALID', feature_group_count=CONV_DIM, dimension_numbers=('NCH', 'OIH', 'NCH'))
            xBC = jax.nn.silu(conv.transpose(0, 2, 1) + conv_b)
            xs = xBC[..., :DIN].reshape(b, l, NH, HEADDIM)
            Bc = xBC[..., DIN:DIN + DSTATE]
            Cc = xBC[..., DIN + DSTATE:]
            dt = jax.nn.softplus(dt + dt_bias)
            A = -jnp.exp(A_log)
            dA = jnp.exp(dt * A)
            dtx = dt[..., None] * xs

            def step(h, inp):
                dA_t, dtx_t, B_t, C_t = inp
                h = dA_t[..., None, None] * h + dtx_t[..., None] * B_t[:, None, None, :]
                y = jnp.einsum('bhpn,bn->bhp', h, C_t)
                return (h, y)
            h0 = jnp.zeros((b, NH, HEADDIM, DSTATE), x.dtype)
            _, ys = lax.scan(step, h0, (dA.transpose(1, 0, 2), dtx.transpose(1, 0, 2, 3), Bc.transpose(1, 0, 2), Cc.transpose(1, 0, 2)))
            y = ys.transpose(1, 0, 2, 3) + D_param[None, None, :, None] * xs
            y = y.reshape(b, l, DIN)
            y = rmsnorm(y * jax.nn.silu(z), norm_w)
            return y @ W_out
        key = jax.random.key(seed)
        ks = jax.random.split(key, 12)
        n = lambda i, shape, scale: jax.random.normal(ks[i], shape, jnp.float32) * scale
        return {'hidden_tokens': n(0, (BATCH, SEQ, DMODEL), 1.0), 'W_in': n(1, (DMODEL, DPROJ), DMODEL ** (-0.5)), 'conv_w': n(2, (CONV_DIM, DCONV), 0.2), 'conv_b': jnp.zeros((CONV_DIM,), jnp.float32), 'dt_bias': jax.random.uniform(ks[3], (NH,), jnp.float32, -4.0, -1.0), 'A_log': jnp.log(jax.random.uniform(ks[4], (NH,), jnp.float32, 1.0, 16.0)), 'D_param': n(5, (NH,), 1.0), 'norm_w': jnp.ones((DIN,), jnp.float32), 'W_out': n(6, (DIN, DMODEL), DIN ** (-0.5)), 'rms_w': jnp.ones((DMODEL,), jnp.float32), 'mlp_w1': n(7, (DMODEL, MLP_INNER), DMODEL ** (-0.5)), 'mlp_b1': jnp.zeros((MLP_INNER,), jnp.float32), 'mlp_w2': n(8, (MLP_INNER, DMODEL), MLP_INNER ** (-0.5)), 'mlp_b2': jnp.zeros((DMODEL,), jnp.float32)}
    _L0_attn_in = _L0_attn_setup()

    def _L0_ffn_setup():
        import jax, jax.numpy as jnp
        import numpy as np
        EPS = 1e-05

        def _layernorm(x, w, b):
            mu = jnp.mean(x, axis=-1, keepdims=True)
            var = jnp.mean((x - mu) ** 2, axis=-1, keepdims=True)
            return (x - mu) * jax.lax.rsqrt(var + EPS) * w + b

        def _rope_tables(T, D, base=10000.0):
            inv_freq = 1.0 / base ** (jnp.arange(0, D, 2, dtype=jnp.float32) / D)
            t = jnp.arange(T, dtype=jnp.float32)
            freqs = jnp.einsum('i,j->ij', t, inv_freq)
            emb = jnp.concatenate([freqs, freqs], axis=-1)
            return (jnp.cos(emb), jnp.sin(emb))

        def _rotate_half(x):
            x1, x2 = (x[..., :x.shape[-1] // 2], x[..., x.shape[-1] // 2:])
            return jnp.concatenate([-x2, x1], axis=-1)

        def _attn(x, ln_w, ln_b, conv_w, attn_w, proj_w, n_head):
            B, T, C = x.shape
            D = C // n_head
            h = _layernorm(x, ln_w, ln_b)
            hc = jnp.transpose(h, (0, 2, 1))
            hc = jnp.pad(hc, ((0, 0), (0, 0), (2, 0)))
            hc = jax.lax.conv_general_dilated(hc, conv_w, window_strides=(1,), padding='VALID', dimension_numbers=('NCH', 'OIH', 'NCH'), feature_group_count=C)
            h = jnp.transpose(hc, (0, 2, 1))
            qkv = h @ attn_w
            q, k, v = jnp.split(qkv, 3, axis=-1)
            q = q.reshape(B, T, n_head, D)
            k = k.reshape(B, T, n_head, D)
            v = v.reshape(B, T, n_head, D)
            cos, sin = _rope_tables(T, D)
            cos = cos[None, :, None, :]
            sin = sin[None, :, None, :]
            q = q * cos + _rotate_half(q) * sin
            k = k * cos + _rotate_half(k) * sin
            scores = jnp.einsum('bqhd,bkhd->bhqk', q, k) / jnp.sqrt(jnp.float32(D))
            causal = jnp.tril(jnp.ones((T, T), dtype=bool))
            scores = jnp.where(causal, scores, jnp.float32(-1e+30))
            p = jax.nn.softmax(scores, axis=-1)
            y = jnp.einsum('bhqk,bkhd->bqhd', p, v).reshape(B, T, C)
            return y @ proj_w

        def _moe(x, ln_w, ln_b, router_w, expert_wv, expert_proj):
            h = _layernorm(x, ln_w, ln_b)
            logits = h @ router_w
            expert_idx = jnp.argmax(logits, axis=-1)
            E = router_w.shape[-1]
            out = jnp.zeros_like(x)
            for e in range(E):
                gv = h @ expert_wv[e]
                gate_raw, value = jnp.split(gv, 2, axis=-1)
                y = gate_raw * jax.nn.sigmoid(gate_raw) * value @ expert_proj[e]
                out = out + jnp.where((expert_idx == e)[..., None], y, 0.0)
            return out
        C, H, E, B, T = (128, 16, 4, 4, 128)
        Dff = 4 * C
        key = jax.random.key(seed)
        ks = jax.random.split(key, 8)
        s = 0.02
        return {'x': jax.random.normal(ks[0], (B, T, C), dtype=jnp.float32), 'ln1_w': jnp.ones((C,), jnp.float32), 'ln1_b': jnp.zeros((C,), jnp.float32), 'ln2_w': jnp.ones((C,), jnp.float32), 'ln2_b': jnp.zeros((C,), jnp.float32), 'conv_w': jax.random.normal(ks[1], (C, 1, 3), dtype=jnp.float32) * 0.1, 'attn_w': jax.random.normal(ks[2], (C, 3 * C), dtype=jnp.float32) * s, 'proj_w': jax.random.normal(ks[3], (C, C), dtype=jnp.float32) * s, 'router_w': jax.random.normal(ks[4], (C, E), dtype=jnp.float32) * s, 'expert_wv': jax.random.normal(ks[5], (E, C, 2 * Dff), dtype=jnp.float32) * s, 'expert_proj': jax.random.normal(ks[6], (E, Dff, C), dtype=jnp.float32) * s}
    _L0_ffn_in = _L0_ffn_setup()
    _d = {'L0_attn_hidden_tokens': _L0_attn_in['hidden_tokens'], 'L0_attn_W_in': _L0_attn_in['W_in'], 'L0_attn_conv_w': _L0_attn_in['conv_w'], 'L0_attn_conv_b': _L0_attn_in['conv_b'], 'L0_attn_dt_bias': _L0_attn_in['dt_bias'], 'L0_attn_A_log': _L0_attn_in['A_log'], 'L0_attn_D_param': _L0_attn_in['D_param'], 'L0_attn_norm_w': _L0_attn_in['norm_w'], 'L0_attn_W_out': _L0_attn_in['W_out'], 'L0_attn_rms_w': _L0_attn_in['rms_w'], 'L0_attn_mlp_w1': _L0_attn_in['mlp_w1'], 'L0_attn_mlp_b1': _L0_attn_in['mlp_b1'], 'L0_attn_mlp_w2': _L0_attn_in['mlp_w2'], 'L0_attn_mlp_b2': _L0_attn_in['mlp_b2'], 'L0_ffn_ln1_w': _L0_ffn_in['ln1_w'], 'L0_ffn_ln1_b': _L0_ffn_in['ln1_b'], 'L0_ffn_ln2_w': _L0_ffn_in['ln2_w'], 'L0_ffn_ln2_b': _L0_ffn_in['ln2_b'], 'L0_ffn_conv_w': _L0_ffn_in['conv_w'], 'L0_ffn_attn_w': _L0_ffn_in['attn_w'], 'L0_ffn_proj_w': _L0_ffn_in['proj_w'], 'L0_ffn_router_w': _L0_ffn_in['router_w'], 'L0_ffn_expert_wv': _L0_ffn_in['expert_wv'], 'L0_ffn_expert_proj': _L0_ffn_in['expert_proj']}
    _x0 = _d['L0_attn_hidden_tokens']
    _d['L0_attn_hidden_tokens'] = jax.random.normal(jax.random.fold_in(jax.random.key(seed), 1), (8, 512, 128), dtype=_x0.dtype)
    del _x0
    return _d

def reference(L0_attn_hidden_tokens, L0_attn_W_in, L0_attn_conv_w, L0_attn_conv_b, L0_attn_dt_bias, L0_attn_A_log, L0_attn_D_param, L0_attn_norm_w, L0_attn_W_out, L0_attn_rms_w, L0_attn_mlp_w1, L0_attn_mlp_b1, L0_attn_mlp_w2, L0_attn_mlp_b2, L0_ffn_ln1_w, L0_ffn_ln1_b, L0_ffn_ln2_w, L0_ffn_ln2_b, L0_ffn_conv_w, L0_ffn_attn_w, L0_ffn_proj_w, L0_ffn_router_w, L0_ffn_expert_wv, L0_ffn_expert_proj):

    def _L0_attn_ref(hidden_tokens, W_in, conv_w, conv_b, dt_bias, A_log, D_param, norm_w, W_out, rms_w, mlp_w1, mlp_b1, mlp_w2, mlp_b2):
        import jax, jax.numpy as jnp
        import numpy as np
        from jax import lax
        BATCH, SEQ, DMODEL = (2, 256, 128)
        EXPAND, HEADDIM, DSTATE, DCONV, MLP_INNER = (2, 64, 64, 4, 512)
        DIN = EXPAND * DMODEL
        NH = DIN // HEADDIM
        CONV_DIM = DIN + 2 * DSTATE
        DPROJ = 2 * DIN + 2 * DSTATE + NH
        EPS = 1e-05

        def rmsnorm(x, w):
            return x * lax.rsqrt(jnp.mean(x * x, axis=-1, keepdims=True) + EPS) * w

        def _mamba2(x, W_in, conv_w, conv_b, dt_bias, A_log, D_param, norm_w, W_out):
            b, l, _ = x.shape
            zxbcdt = x @ W_in
            z = zxbcdt[..., :DIN]
            xBC = zxbcdt[..., DIN:DIN + CONV_DIM]
            dt = zxbcdt[..., DIN + CONV_DIM:]
            xt = jnp.pad(xBC, ((0, 0), (DCONV - 1, 0), (0, 0))).transpose(0, 2, 1)
            conv = lax.conv_general_dilated(xt, conv_w[:, None, :], (1,), 'VALID', feature_group_count=CONV_DIM, dimension_numbers=('NCH', 'OIH', 'NCH'))
            xBC = jax.nn.silu(conv.transpose(0, 2, 1) + conv_b)
            xs = xBC[..., :DIN].reshape(b, l, NH, HEADDIM)
            Bc = xBC[..., DIN:DIN + DSTATE]
            Cc = xBC[..., DIN + DSTATE:]
            dt = jax.nn.softplus(dt + dt_bias)
            A = -jnp.exp(A_log)
            dA = jnp.exp(dt * A)
            dtx = dt[..., None] * xs

            def step(h, inp):
                dA_t, dtx_t, B_t, C_t = inp
                h = dA_t[..., None, None] * h + dtx_t[..., None] * B_t[:, None, None, :]
                y = jnp.einsum('bhpn,bn->bhp', h, C_t)
                return (h, y)
            h0 = jnp.zeros((b, NH, HEADDIM, DSTATE), x.dtype)
            _, ys = lax.scan(step, h0, (dA.transpose(1, 0, 2), dtx.transpose(1, 0, 2, 3), Bc.transpose(1, 0, 2), Cc.transpose(1, 0, 2)))
            y = ys.transpose(1, 0, 2, 3) + D_param[None, None, :, None] * xs
            y = y.reshape(b, l, DIN)
            y = rmsnorm(y * jax.nn.silu(z), norm_w)
            return y @ W_out
        h = hidden_tokens + _mamba2(hidden_tokens, W_in, conv_w, conv_b, dt_bias, A_log, D_param, norm_w, W_out)
        hn = rmsnorm(h, rms_w)
        mlp = jax.nn.silu(hn @ mlp_w1 + mlp_b1) @ mlp_w2 + mlp_b2
        return h + mlp

    def _L0_ffn_ref(x, ln1_w, ln1_b, ln2_w, ln2_b, conv_w, attn_w, proj_w, router_w, expert_wv, expert_proj):
        import jax, jax.numpy as jnp
        import numpy as np
        EPS = 1e-05

        def _layernorm(x, w, b):
            mu = jnp.mean(x, axis=-1, keepdims=True)
            var = jnp.mean((x - mu) ** 2, axis=-1, keepdims=True)
            return (x - mu) * jax.lax.rsqrt(var + EPS) * w + b

        def _rope_tables(T, D, base=10000.0):
            inv_freq = 1.0 / base ** (jnp.arange(0, D, 2, dtype=jnp.float32) / D)
            t = jnp.arange(T, dtype=jnp.float32)
            freqs = jnp.einsum('i,j->ij', t, inv_freq)
            emb = jnp.concatenate([freqs, freqs], axis=-1)
            return (jnp.cos(emb), jnp.sin(emb))

        def _rotate_half(x):
            x1, x2 = (x[..., :x.shape[-1] // 2], x[..., x.shape[-1] // 2:])
            return jnp.concatenate([-x2, x1], axis=-1)

        def _attn(x, ln_w, ln_b, conv_w, attn_w, proj_w, n_head):
            B, T, C = x.shape
            D = C // n_head
            h = _layernorm(x, ln_w, ln_b)
            hc = jnp.transpose(h, (0, 2, 1))
            hc = jnp.pad(hc, ((0, 0), (0, 0), (2, 0)))
            hc = jax.lax.conv_general_dilated(hc, conv_w, window_strides=(1,), padding='VALID', dimension_numbers=('NCH', 'OIH', 'NCH'), feature_group_count=C)
            h = jnp.transpose(hc, (0, 2, 1))
            qkv = h @ attn_w
            q, k, v = jnp.split(qkv, 3, axis=-1)
            q = q.reshape(B, T, n_head, D)
            k = k.reshape(B, T, n_head, D)
            v = v.reshape(B, T, n_head, D)
            cos, sin = _rope_tables(T, D)
            cos = cos[None, :, None, :]
            sin = sin[None, :, None, :]
            q = q * cos + _rotate_half(q) * sin
            k = k * cos + _rotate_half(k) * sin
            scores = jnp.einsum('bqhd,bkhd->bhqk', q, k) / jnp.sqrt(jnp.float32(D))
            causal = jnp.tril(jnp.ones((T, T), dtype=bool))
            scores = jnp.where(causal, scores, jnp.float32(-1e+30))
            p = jax.nn.softmax(scores, axis=-1)
            y = jnp.einsum('bhqk,bkhd->bqhd', p, v).reshape(B, T, C)
            return y @ proj_w

        def _moe(x, ln_w, ln_b, router_w, expert_wv, expert_proj):
            h = _layernorm(x, ln_w, ln_b)
            logits = h @ router_w
            expert_idx = jnp.argmax(logits, axis=-1)
            E = router_w.shape[-1]
            out = jnp.zeros_like(x)
            for e in range(E):
                gv = h @ expert_wv[e]
                gate_raw, value = jnp.split(gv, 2, axis=-1)
                y = gate_raw * jax.nn.sigmoid(gate_raw) * value @ expert_proj[e]
                out = out + jnp.where((expert_idx == e)[..., None], y, 0.0)
            return out
        n_head = 16
        x = x + _attn(x, ln1_w, ln1_b, conv_w, attn_w, proj_w, n_head)
        x = x + _moe(x, ln2_w, ln2_b, router_w, expert_wv, expert_proj)
        return x
    x = L0_attn_hidden_tokens
    x = x + 0.5 * _L0_ffn_ref(_layernorm(x, axis=-1), L0_ffn_ln1_w, L0_ffn_ln1_b, L0_ffn_ln2_w, L0_ffn_ln2_b, L0_ffn_conv_w, L0_ffn_attn_w, L0_ffn_proj_w, L0_ffn_router_w, L0_ffn_expert_wv, L0_ffn_expert_proj)
    x = x + _L0_attn_ref(_layernorm(x, axis=-1), L0_attn_W_in, L0_attn_conv_w, L0_attn_conv_b, L0_attn_dt_bias, L0_attn_A_log, L0_attn_D_param, L0_attn_norm_w, L0_attn_W_out, L0_attn_rms_w, L0_attn_mlp_w1, L0_attn_mlp_b1, L0_attn_mlp_w2, L0_attn_mlp_b2)
    x = x + 0.5 * _L0_ffn_ref(_layernorm(x, axis=-1), L0_ffn_ln1_w, L0_ffn_ln1_b, L0_ffn_ln2_w, L0_ffn_ln2_b, L0_ffn_conv_w, L0_ffn_attn_w, L0_ffn_proj_w, L0_ffn_router_w, L0_ffn_expert_wv, L0_ffn_expert_proj)
    return x

_drawn_inputs = setup_inputs


def setup_inputs(seed=0):
    import zlib

    import numpy as np

    out = dict(_drawn_inputs(seed))
    spreads = {'L0_attn_conv_b': (0.0, 0.1),
     'L0_attn_norm_w': (1.0, 0.2),
     'L0_attn_rms_w': (1.0, 0.2),
     'L0_attn_mlp_b1': (0.0, 0.349),
     'L0_attn_mlp_b2': (0.0, 0.1),
     'L0_ffn_ln1_w': (1.0, 0.6),
     'L0_ffn_ln1_b': (0.0, 0.8),
     'L0_ffn_ln2_w': (1.0, 0.6),
     'L0_ffn_ln2_b': (0.0, 0.8)}
    factors = {'L0_attn_A_log': 64.0,
     'L0_ffn_conv_w': 8.0,
     'L0_ffn_attn_w': 8.0,
     'L0_ffn_proj_w': 8.0,
     'L0_ffn_router_w': 8.0,
     'L0_ffn_expert_wv': 8.0,
     'L0_ffn_expert_proj': 8.0}
    for name, (base, spread) in spreads.items():
        noise = np.random.default_rng([zlib.crc32(name.encode()), seed]).standard_normal(out[name].shape)
        drawn = base * np.exp(spread * noise) if base else spread * noise
        out[name] = jnp.asarray(drawn.astype(out[name].dtype))
    for name, factor in factors.items():
        out[name] = (out[name] * factor).astype(out[name].dtype)
    return out
```

```python
import concourse.bass as bass
from concourse import mybir
from contextlib import ExitStack

F32 = mybir.dt.float32
BF16 = mybir.dt.bfloat16
ALU = mybir.AluOpType
ACT = mybir.ActivationFunctionType
AX_X = mybir.AxisListType.X

P = 128
EPS = 1e-5
HEADS, HD = 16, 8
GROUP = 4
GROUPS = HEADS // GROUP
STACK = 64
NPROD = 6
MROW = NPROD * HD
NEG = -1e30
EXPERTS, DFF = 4, 512
MH, MP, NS, TAPS = 4, 64, 64, 4
DIN = MH * MP
MLP = 512
ATANH_TERMS = 8

PACK = {}
_at = 0
for _name, _w in (("ln1_w", 1), ("ln1_b", 1), ("ln2_w", 1), ("ln2_b", 1), ("aconv", 3), ("router", EXPERTS),
                  ("mconv", 3 * TAPS), ("mconv_b", 3), ("dt_bias", MH), ("A_log", MH), ("D", 2),
                  ("norm_w", 2), ("rms_w", 1), ("b1", 4), ("b2", 1)):
    PACK[_name] = (_at, _w)
    _at += _w
PACKED = _at


def attention_tasks():
    def maxima(g):
        return [("max", g, 3, 0), ("max", g, 3, 1), ("max", g, 2, 0), ("max", g, 2, 1), ("max", g, 1, 0), ("max", g, 0, 0)]
    tasks = [("hT",), ("qkv", 0), ("qkv", 1), ("qkT", 0), ("qkT", 1), ("qkT", 2), ("qkT", 3)] + maxima(0)
    x = 0
    for g in range(GROUPS):
        nxt = maxima(g + 1) if g + 1 < GROUPS else [None] * 6
        seq = nxt[:2] + [("shift", g), nxt[2], ("exp", g, 0), nxt[3], ("exp", g, 1), nxt[4], ("exp", g, 2)]
        seq += [("back", g - 1) if g else None, nxt[5], ("exp", g, 3), ("exp", g, 4)]
        tasks += [t for t in seq if t]
    return tasks + [("back", GROUPS - 1), ("yT",)]


A_TASKS = attention_tasks()
NA = len(A_TASKS)
E_TASKS = [("hT",), ("logits",)]
for _e in range(EXPERTS):
    E_TASKS += [("mask", _e)] + [(k, _e, c) for c in range(DFF // P) for k in ("gate", "value")]
E_TASKS += [("back",)]
if len(E_TASKS) % 2:
    E_TASKS += [("none",)]
NE = len(E_TASKS)
M_TASKS = ([("uT",), ("xbc", 2), ("xbc", 0), ("xbc", 1), ("dt",), ("z", 0), ("z", 1), ("sums",), ("xsT", 0), ("xsT", 1), ("BT",),
            ("G",)] + [("decay", j) for j in range(4)] + [("state", j) for j in range(3)]
           + [("head_decay", j) for j in range(1, 4)] + [("norm",), ("out",), ("hT",)]
           + [("up", c) for c in range(4)] + [("back",)])
if len(M_TASKS) % 2:
    M_TASKS += [("none",)]
NM = len(M_TASKS)
assert NA % 2 == 0 and NE % 2 == 0 and NM % 2 == 0
A_LINKS, E_LINKS, M_LINKS = 32, 7, 31


def build_program(nc, A):
    NB, T, C = A["x"].shape
    NT = T // P
    assert C == P and NT == 4
    x_v = A["x"].rearrange("b (j p) c -> b p j c", p=P)
    out_v = A["out"].rearrange("b (j p) c -> b p j c", p=P)

    with ExitStack() as ctx:
        def sb(name, shape, dt=F32):
            return ctx.enter_context(nc.sbuf_tensor(name, shape, dt))

        def pb(name, shape, dt=F32):
            return ctx.enter_context(nc.psum_tensor(name, shape, dt))

        aring = [pb(f"aring{i}", [P, 2, 512]) for i in range(2)]
        obank = pb("obank", [P, 512])
        wring = [pb(f"wring{i}", [P, 512]) for i in range(2)]
        acc = pb("acc", [P, 512])

        ident = sb("ident", [P, P])
        identb = sb("identb", [P, P], BF16)
        upto = sb("upto", [P, P])
        after = sb("after", [P, P])
        ones = sb("ones", [P, P])
        neg_keys = sb("neg_keys", [P, P], BF16)
        neg_queries = sb("neg_queries", [P, P], BF16)
        cos = sb("cos", [P, 4, HD])
        sin = sb("sin", [P, 4, HD])
        vec = sb("vec", [P, PACKED])
        attn_w = sb("attn_w", [P, 3 * P])
        proj_w = sb("proj_w", [P, P])
        wv = sb("wv", [P, EXPERTS, 2 * DFF])
        ep = sb("ep", [P, EXPERTS, 4, P])
        W_in = sb("W_in", [P, 2 * DIN + 2 * NS + MH])
        W_out = sb("W_out", [P, 2, P])
        w1 = sb("w1", [P, MLP])
        w2 = sb("w2", [P, 4, P])
        negA = sb("negA", [P, MH])
        tie = sb("tie", [P, EXPERTS])
        pause = sb("pause", [P, 1])
        half = sb("half", [P, 8])

        def v(name, k=0, n=1):
            a = PACK[name][0] + k
            return vec[:, a:a + n]

        x0 = sb("x0", [P, 4, P])
        x1 = sb("x1", [P, 4, P])
        x2 = sb("x2", [P, 4, P])
        x3 = sb("x3", [P, 4, P])
        a_st = sb("a_st", [P, 4, 6])
        a_mv = sb("a_mv", [P, 4, 2])
        a_pw = sb("a_pw", [P, 8])
        a_r = sb("a_r", [P, 8])
        a_rc = sb("a_rc", [P, 4])
        u = sb("u", [P, 4, P])
        hn = sb("hn", [P, 4, P])
        hT = sb("hT", [P, 2 + T])
        cT = sb("cT", [P, T])
        ra = sb("ra", [P, 32, HD])
        rb = sb("rb", [P, 32, HD])
        rqk = [sb("rq", [P, 64, HD]), sb("rk", [P, 64, HD])]
        mid = [sb("mid_q", [P, 64, HD]), sb("mid_k", [P, 64, HD])]
        stk = [sb("stk_q", [P, 64, STACK], BF16), sb("stk_k", [P, 64, STACK], BF16)]
        stT = [sb("stT_q", [P, 8, T], BF16), sb("stT_k", [P, 8, T], BF16)]
        vx = sb("vx", [P, 4, HEADS, 32])
        mx = sb("mx", [P, 4, HEADS])
        mt = sb("mt", [P, 4, HEADS])
        probs = [sb(f"probs{i}", [P, 1024]) for i in range(5)]
        osb = sb("osb", [P, T])
        rden = sb("rden", [P, 4, GROUP])
        y = hn
        yT = cT
        u1 = sb("u1", [P, 4, P])
        e_st = sb("e_st", [P, 4, 6])
        e_mv = sb("e_mv", [P, 4, 2])
        e_pw = sb("e_pw", [P, 4])
        e_r = sb("e_r", [P, 4])
        e_hn = sb("e_hn", [P, 4, P])
        e_hT = sb("e_hT", [P, T])
        lmax = sb("lmax", [P, 4])
        lsel = sb("lsel", [P, 4, EXPERTS])
        pick = sb("pick", [P, 4, EXPERTS], BF16)
        scratch = [sb(f"scratch{i}", [P, 4, T]) for i in range(2)]
        hm = [scratch[0][:, i] for i in range(2)]
        ya = [scratch[0][:, 2 + i] for i in range(2)]
        tg = [scratch[1][:, i] for i in range(2)]
        sg = [scratch[1][:, 2 + i] for i in range(2)]
        moT = sb("moT", [P, T])
        tmp = sb("tmp", [P, 4, P])
        m_st = sb("m_st", [P, 4, 6])
        m_mv = sb("m_mv", [P, 4, 2])
        m_pw = sb("m_pw", [P, 4])
        m_r = sb("m_r", [P, 4])
        mu = sb("mu", [P, 4, P])
        uT = sb("uT", [P, T])
        cpad = [sb(f"cpad{i}", [P, 3 + T]) for i in range(3)]
        conv = sb("conv", [P, 6, T])
        cacc = [conv[:, i] for i in range(3)]
        ct = [conv[:, 3 + i] for i in range(3)]
        xs = [sb(f"xs{i}", [P, T]) for i in range(2)]
        BT = sb("BT", [NS, T])
        CT = sb("CT", [NS, T])
        zt = [sb(f"zt{i}", [P, T]) for i in range(2)]
        zs = [sb(f"zs{i}", [P, T]) for i in range(2)]
        sm = {k: sb("sm_" + k, [P, 4, MH]) for k in ("x", "n", "e", "d", "r", "z", "z2", "p", "q", "w", "dt", "a")}
        edec = sb("edec", [P, 2, 4, MH])
        MV = scratch[0][:].rearrange("p j (h t) -> p j h t", h=MH)
        Ld = conv[:, 0:4].rearrange("p j (h t) -> p j h t", h=MH)
        Ed = sb("Ed", [NS, 4, MH, P])
        Xd = scratch[1][:, 0:2].rearrange("p a (b h d) -> p (a b) h d", b=2, h=MH)
        Xw = scratch[1][:, 2:4].rearrange("p a (b h d) -> p (a b) h d", b=2, h=MH)
        Bt = sb("Bt", [P, 4, NS])
        Gm = sb("Gm", [P, 4, P])
        St = sb("St", [NS, 4, MH, MP])
        yd = e_hT[:]
        gT = ct[1:3]
        gq = zt
        mh = moT[:].rearrange("p (j c) -> p j c", j=4)
        sq = sb("sq", [P, P])
        ssq = sb("ssq", [P, 4])
        m_hn = e_hn
        mhT = e_hT
        gb = tg
        gt = sg
        ga = ya
        mlT = moT

        names = """
            setup_chain const_loaded weights_loaded ones_set setup_pool setup_dve setup_act setup_dve2
            x_loaded x_free out_stored out_ready
            a_link a_link_dve a_link2 a_var a_rstd a_hn a_hT a_cT a_rope a_high a_mid a_low a_stT a_max a_shift a_exp a_pv a_osb a_y a_yT a_proj a_u1
            a_filled a_freed0 a_freed1 a_pad
            e_link e_sg e_var e_rstd e_hn e_hT e_pick e_hm e_tanh e_ya e_down e_moT e_x
            w_filled w_freed0 w_freed1 e_down1
            m_link m_var m_rstd m_u m_uT m_pad m_conv m_ctanh m_xs m_BC m_ztanh m_zs m_dtexpin m_dtexp m_a m_MV m_esum m_Xd m_Xw m_Bt m_G
            m_L m_Lg m_E m_Ce m_St m_Y m_yd m_gT m_gq m_var2 m_rstd2 m_mh m_ssq m_var3 m_rstd3 m_hn m_hT m_gb m_gtanh m_ga m_mlp m_mlT m_x
        """.split()
        s = {n: ctx.enter_context(nc.semaphore(n)) for n in names}
        a_freed = [s["a_freed0"], s["a_freed1"]]
        w_freed = [s["w_freed0"], s["w_freed1"]]
        WB = 2 * NE + NM
        block = ctx.enter_context(nc.Block())

        loads = [(ident, A["consts"][:, 0:P]), (upto, A["consts"][:, P:2 * P]), (after, A["consts"][:, 2 * P:3 * P]),
                 (cos, A["consts"][:, 3 * P:3 * P + 4 * HD].rearrange("p (j d) -> p j d", d=HD)),
                 (sin, A["consts"][:, 3 * P + 4 * HD:3 * P + 8 * HD].rearrange("p (j d) -> p j d", d=HD)),
                 (vec, A["packed"])]
        wloads = [(attn_w, A["attn_w"]), (proj_w, A["proj_w"]), (wv, A["wv"].rearrange("e c n -> c e n")),
                  (ep, A["ep"].rearrange("e (k f) c -> f e k c", f=P)), (W_in, A["W_in"]),
                  (W_out, A["W_out"].rearrange("(k f) c -> f k c", f=P)), (w1, A["w1"]),
                  (w2, A["w2"].rearrange("(k f) c -> f k c", f=P))]

        @block.sync
        def _(sp):
            for dst, src in loads:
                sp.dma_start(dst[:], src).then_inc(s["const_loaded"], 16)
            sp.sem_inc(s["x_free"], 1)
            sp.sem_inc(s["out_stored"], 16)
            for dst, src in wloads:
                sp.dma_start(dst[:], src).then_inc(s["weights_loaded"], 16)
            with sp.Fori(0, NB) as i:
                sp.wait_ge(s["x_free"], i + 1)
                sp.dma_start(x0[:], x_v[bass.ds(i, 1)].rearrange("b p j c -> p (b j) c")).then_inc(s["x_loaded"], 16)
                sp.wait_ge(s["e_x"], 2 * i + 2)
                sp.dma_start(out_v[bass.ds(i, 1)].rearrange("b p j c -> p (b j) c"), x3[:]).then_inc(s["out_stored"], 16)
            sp.wait_ge(s["out_stored"], 16 * (NB + 1))

        @block.tensor
        def _(pe):
            def transpose4(dst, src, ind):
                for j in range(4):
                    last = pe.transpose(dst(j), src(j), ind)
                return last

            def attention(n):
                base, half_base = n * NA, n * (NA // 2)

                def pv(x):
                    g, k = divmod(x, 5)
                    pr = probs[k]
                    pe.wait_ge(s["a_exp"], n * 20 + x + 1)
                    if k == 0 and g > 0:
                        pe.wait_ge(s["a_osb"], n * GROUPS + g)
                    if k < 4:
                        pair, blocks = k % 2, [[(0, 0, 512)], [(1, 0, 384), (3, 384, 128)]][k // 2]
                        parts = [(2 * pair + a, kb, 512 * a + c, w) for a in range(2) for kb, c, w in blocks]
                    else:
                        parts = [(2 * pair + a, 2, 512 * a + 256 * pair, 256) for pair in range(2) for a in range(2)]
                    for hl, kb, c, w in parts:
                        last = pe.matmul(obank[32 * hl:32 * hl + 32, 512 - w:512], vx[:, kb, GROUP * g + hl, :],
                                         pr[:, c:c + w], start=(k < 2), stop=(k == 4), skip_group_check=True)
                    last.then_inc(s["a_pv"], 1)

                x = 0
                for t, task in enumerate(A_TASKS):
                    kind, ring = task[0], aring[t % 2]
                    pe.wait_ge(a_freed[t % 2], half_base + t // 2 + 1)
                    if kind == "hT":
                        pe.wait_ge(s["a_hn"], n + 1)
                        last = transpose4(lambda j: ring[:, 0, j * P:(j + 1) * P], lambda j: hn[:, j, :], ident[:])
                    elif kind == "qkv":
                        pe.wait_ge(s["a_cT"], n + 1)
                        for b in range(2):
                            j = 2 * task[1] + b
                            last = pe.matmul(ring[:, b, 0:3 * P], cT[:, j * P:(j + 1) * P], attn_w[:], start=True, stop=True)
                    elif kind == "qkT":
                        side, hf = divmod(task[1], 2)
                        pe.wait_ge(s["a_low"], 2 * n + side + 1)
                        rb16 = ring[:].bitcast(BF16)
                        for b in range(4):
                            hp = 4 * hf + b
                            last = transpose4(lambda j: rb16[:, b // 2, (b % 2) * 512 + j * P:(b % 2) * 512 + (j + 1) * P],
                                              lambda j: stk[side][:, 16 * j + 2 * hp:16 * j + 2 * hp + 2, :].rearrange("p h k -> p (h k)"),
                                              identb[:])
                    elif kind == "max":
                        _, g, j, pair = task
                        if g == 0 and j == 3 and pair == 0:
                            pe.wait_ge(s["a_stT"], n * 8 + 4)
                        w = P * (j + 1)
                        heads = [(pair, a) for a in range(2)] if j >= 2 else [(q, a) for q in range(2) for a in range(2)]
                        for q, a in heads:
                            hp = 2 * g + q
                            bank, col = (a, 0) if j >= 2 else (a, q * w)
                            rows = slice(STACK * a, STACK * a + STACK)
                            pe.matmul(ring[:, bank, col:col + w], stT[0][rows, hp, j * P:(j + 1) * P], stT[1][rows, hp, 0:w],
                                      start=True, stop=False)
                            last = pe.matmul(ring[:, bank, col + w - P:col + w], identb[:], neg_keys[:], start=False, stop=True)
                    elif kind == "shift":
                        g = task[1]
                        pe.wait_ge(s["a_shift"], n * GROUPS + g + 1)
                        rb16 = ring[:].bitcast(BF16)
                        for b in range(2):
                            hp = 2 * g + b
                            last = transpose4(lambda j: rb16[:, 0, b * 512 + j * P:b * 512 + (j + 1) * P],
                                              lambda j: stk[0][:, 16 * j + 2 * hp:16 * j + 2 * hp + 2, :].rearrange("p h k -> p (h k)"),
                                              identb[:])
                    elif kind == "exp":
                        _, g, k = task
                        if k == 0:
                            pe.wait_ge(s["a_stT"], n * 8 + 5 + g)
                        if k < 4:
                            pair, blocks = k % 2, [[(0, 0, 512)], [(1, 0, 384), (3, 384, 128)]][k // 2]
                            parts = [(pair, a, kb, a, c, w) for a in range(2) for kb, c, w in blocks]
                        else:
                            parts = [(q, a, 2, a, 256 * q, 256) for q in range(2) for a in range(2)]
                        for q, a, kb, bank, c, w in parts:
                            hp = 2 * g + q
                            rows = slice(STACK * a, STACK * a + STACK)
                            pe.matmul(ring[:, bank, c:c + w], stT[1][rows, hp, kb * P:(kb + 1) * P], stT[0][rows, hp, T - w:T],
                                      start=True, stop=False)
                            last = pe.matmul(ring[:, bank, c:c + P], identb[:], neg_queries[:], start=False, stop=True)
                    elif kind == "back":
                        g = task[1]
                        if g == GROUPS - 1:
                            pv(18)
                            pv(19)
                        pe.wait_ge(s["a_osb"], n * GROUPS + g + 1)
                        last = transpose4(lambda j: ring[:, 0, j * P:(j + 1) * P], lambda j: osb[:, j * P:(j + 1) * P], ident[:])
                    elif kind == "yT":
                        pe.wait_ge(s["a_y"], n * GROUPS + GROUPS)
                        last = transpose4(lambda j: ring[:, 0, j * P:(j + 1) * P], lambda j: y[:, j, :], ident[:])
                    last.then_inc(s["a_filled"], 1)
                    if kind == "exp":
                        if x >= 2:
                            pv(x - 2)
                        x += 1
                pe.wait_ge(s["a_yT"], n + 1)
                for j in range(4):
                    last = pe.matmul(obank[:, j * P:(j + 1) * P], yT[:, j * P:(j + 1) * P], proj_w[:], start=True, stop=True)
                last.then_inc(s["a_proj"], 1)

            def fill(k, base, half_base, t):
                pe.wait_ge(w_freed[t % 2], half_base + t // 2 + 1)
                return wring[t % 2]

            def experts(n, base, half_base):
                def down(e, c):
                    k = 4 * e + c
                    pe.wait_ge(s["e_ya"], n * 16 + k + 1)
                    pe.matmul(acc[:], ep[:, e, c, :], ya[k % 2][:], start=(k == 0), stop=(k == 15)).then_inc(s["e_down"], 1)

                for t, task in enumerate(E_TASKS):
                    kind = task[0]
                    if kind == "none":
                        pe.wait_ge(s["w_filled"], base + t)
                        pe.wait_ge(w_freed[t % 2], half_base + t // 2 + 1)
                        pe.sem_inc(s["w_filled"], 1)
                        continue
                    ring = fill("e", base, half_base, t)
                    if kind == "hT":
                        pe.wait_ge(s["e_hn"], n + 1)
                        last = transpose4(lambda j: ring[:, j * P:(j + 1) * P], lambda j: e_hn[:, j, :], ident[:])
                    elif kind == "logits":
                        pe.wait_ge(s["e_hT"], n + 1)
                        for j in range(4):
                            last = pe.matmul(ring[:, EXPERTS * j:EXPERTS * (j + 1)], e_hT[:, j * P:(j + 1) * P], v("router", 0, EXPERTS),
                                             start=True, stop=True)
                    elif kind == "mask":
                        e = task[1]
                        if e == 0:
                            pe.wait_ge(s["e_pick"], n + 1)
                        for j in range(4):
                            last = pe.matmul(ring[:, j * P:(j + 1) * P], pick[:, j, e:e + 1].to_broadcast([P, P]), identb[:],
                                             start=True, stop=True)
                    elif kind in ("gate", "value"):
                        _, e, c = task
                        if kind == "gate" and c == 0:
                            pe.wait_ge(s["e_hm"], n * EXPERTS + e + 1)
                        o = (DFF if kind == "value" else 0) + c * P
                        last = pe.matmul(ring[:], wv[:, e, o:o + P], hm[e % 2][:], start=True, stop=True)
                    elif kind == "back":
                        down(3, 3)
                        pe.wait_ge(s["e_moT"], n + 1)
                        last = transpose4(lambda j: ring[:, j * P:(j + 1) * P], lambda j: moT[:, j * P:(j + 1) * P], ident[:])
                    last.then_inc(s["w_filled"], 1)
                    if kind == "value" and 4 * e + c >= 1:
                        down(*divmod(4 * e + c - 1, 4))

            def mamba(i, base, half_base):
                def chunk(ring, w, src, n0, m=P):
                    return pe.matmul(ring, w[:, n0:n0 + m], src[:], start=True, stop=True)

                for t, task in enumerate(M_TASKS):
                    kind = task[0]
                    if kind == "none":
                        pe.wait_ge(s["w_filled"], base + t)
                        pe.wait_ge(w_freed[t % 2], half_base + t // 2 + 1)
                        pe.sem_inc(s["w_filled"], 1)
                        continue
                    if kind == "norm":
                        for c in range(2):
                            if c == 1:
                                pe.wait_ge(s["m_yd"], 2 * i + 1)
                            for j in range(4):
                                if c == 0:
                                    pe.wait_ge(s["m_Lg"], 4 * i + j + 1)
                                    if j == 0:
                                        pe.wait_ge(s["m_Xd"], 2 * i + 2)
                                    if j > 0:
                                        pe.wait_ge(s["m_Ce"], 3 * i + j)
                                        pe.wait_ge(s["m_St"], 3 * i + j)
                                for a in range(2):
                                    h = 2 * c + a
                                    dst = acc[MP * a:MP * a + MP, j * P:(j + 1) * P]
                                    last = pe.matmul(dst, Xd[:, j, h, :], Ld[:, j, h, :], start=True, stop=(j == 0), skip_group_check=True)
                                    if j > 0:
                                        last = pe.matmul(dst, St[:, j, h, :], Ed[:, j, h, :], start=False, stop=True, skip_group_check=True)
                            last.then_inc(s["m_Y"], 1)
                    ring = fill("m", base, half_base, t)
                    if kind == "uT":
                        pe.wait_ge(s["m_u"], i + 1)
                        last = transpose4(lambda j: ring[:, j * P:(j + 1) * P], lambda j: mu[:, j, :], ident[:])
                    elif kind == "xbc":
                        pe.wait_ge(s["m_uT"], i + 1)
                        last = chunk(ring[:], W_in, uT, DIN + task[1] * P)
                    elif kind == "z":
                        last = chunk(ring[:], W_in, uT, task[1] * P)
                    elif kind == "dt":
                        for j in range(4):
                            last = pe.matmul(ring[:, MH * j:MH * (j + 1)], uT[:, j * P:(j + 1) * P], W_in[:, 2 * DIN + 2 * NS:],
                                             start=True, stop=True)
                    elif kind == "sums":
                        pe.wait_ge(s["m_a"], i + 1)
                        av = sm["a"][:].rearrange("p j h -> p (j h)")
                        pe.matmul(ring[:, 0:16], after[:], av, start=True, stop=True)
                        last = pe.matmul(ring[:, 16:32], ones[:], av, start=True, stop=True)
                    elif kind == "xsT":
                        c = task[1]
                        pe.wait_ge(s["m_xs"], 2 * i + c + 1)
                        last = transpose4(lambda j: ring[:, j * P:(j + 1) * P], lambda j: xs[c][:, j * P:(j + 1) * P], ident[:])
                    elif kind == "BT":
                        pe.wait_ge(s["m_BC"], 2 * i + 1)
                        for j in range(4):
                            last = pe.matmul(ring[:, j * NS:(j + 1) * NS], BT[:, j * P:(j + 1) * P], ident[0:NS, 0:NS], start=True, stop=True)
                    elif kind == "G":
                        pe.wait_ge(s["m_BC"], 2 * i + 2)
                        for j in range(4):
                            last = pe.matmul(ring[:, j * P:(j + 1) * P], BT[:, j * P:(j + 1) * P], CT[:, j * P:(j + 1) * P], start=True, stop=True)
                    elif kind == "decay":
                        j = task[1]
                        pe.wait_ge(s["m_MV"], 4 * i + j + 1)
                        last = pe.matmul(ring[:], after[:], MV[:, j].rearrange("p h t -> p (h t)"), start=True, stop=True)
                    elif kind == "head_decay":
                        j = task[1]
                        last = pe.matmul(ring[0:NS, :], ones[:, 0:NS], MV[:, j].rearrange("p h t -> p (h t)"), start=True, stop=True)
                    elif kind == "state":
                        j = task[1]
                        if j == 0:
                            pe.wait_ge(s["m_Xw"], i + 1)
                            pe.wait_ge(s["m_Bt"], i + 1)
                        last = pe.matmul(ring[0:NS, 0:MH * MP], Bt[:, j, :], Xw[:, j].rearrange("p h d -> p (h d)"), start=True, stop=True)
                    elif kind == "norm":
                        pe.wait_ge(s["m_gq"], 2 * i + 2)
                        for j in range(4):
                            for c in range(2):
                                last = pe.matmul(ring[:, j:j + 1], gq[c][:, j * P:(j + 1) * P], ones[:, 0:1], start=(c == 0), stop=(c == 1))
                    elif kind == "out":
                        for j in range(4):
                            for c in range(2):
                                last = pe.matmul(ring[:, j * P:(j + 1) * P], gT[c][:, j * P:(j + 1) * P], W_out[:, c, :], start=(c == 0), stop=(c == 1))
                    elif kind == "hT":
                        pe.wait_ge(s["m_hn"], i + 1)
                        last = transpose4(lambda j: ring[:, j * P:(j + 1) * P], lambda j: m_hn[:, j, :], ident[:])
                    elif kind == "up":
                        pe.wait_ge(s["m_hT"], i + 1)
                        last = chunk(ring[:], w1, mhT, task[1] * P)
                    elif kind == "back":
                        for c in range(4):
                            pe.wait_ge(s["m_ga"], 4 * i + c + 1)
                            pe.matmul(acc[:], w2[:, c, :], ga[c % 2][:], start=(c == 0), stop=(c == 3)).then_inc(s["m_mlp"], 1)
                        pe.wait_ge(s["m_mlT"], i + 1)
                        last = transpose4(lambda j: ring[:, j * P:(j + 1) * P], lambda j: mlT[:, j * P:(j + 1) * P], ident[:])
                    last.then_inc(s["w_filled"], 1)

            pe.wait_ge(s["const_loaded"], 16 * len(loads))
            pe.wait_ge(s["weights_loaded"], 16 * len(wloads))
            pe.wait_ge(s["setup_dve"], 1)
            pe.wait_ge(s["setup_dve2"], 1)
            with pe.Fori(0, NB) as i:
                attention(2 * i)
                experts(2 * i, i * WB, i * (WB // 2))
                mamba(i, i * WB + NE, i * (WB // 2) + NE // 2)
                attention(2 * i + 1)
                experts(2 * i + 1, i * WB + NE + NM, i * (WB // 2) + (NE + NM) // 2)

        @block.scalar
        def _(act):
            def copy(dst, src):
                return act.activation(dst, src, ACT.Copy)

            def attention(n):
                def copy_out(g):
                    act.wait_ge(s["a_pv"], n * 20 + 5 * g + 5)
                    if g > 0:
                        act.wait_ge(s["a_y"], n * GROUPS + g)
                    copy(osb[:], obank[:]).then_inc(s["a_osb"], 1)

                for side in range(2):
                    st = stk[side][:, :, 0:MROW].rearrange("p h (k d) -> p h k d", d=HD)
                    hi = st[:, :, 0:3, :] if side == 0 else st[:, :, 2:5, :]
                    act.wait_ge(s["a_rope"], 4 * n + 4)
                    if side == 0:
                        act.wait_ge(s["a_pad"], n + 1)
                    copy(hi, rqk[side][:].unsqueeze(2).to_broadcast([P, 64, 3, HD])).then_inc(s["a_high"], 1)
                for side in range(2):
                    st = stk[side][:, :, 0:MROW].rearrange("p h (k d) -> p h k d", d=HD)
                    md = st[:, :, 3:6:2, :] if side == 0 else st[:, :, 1:6:4, :]
                    act.wait_ge(s["a_mid"], 2 * n + side + 1)
                    copy(md, mid[side][:].unsqueeze(2).to_broadcast([P, 64, 2, HD])).then_inc(s["a_link"], 1)
                x = 0
                for t, task in enumerate(A_TASKS):
                    kind, ring = task[0], aring[t % 2]
                    if kind == "qkT":
                        side, hf = divmod(task[1], 2)
                        act.wait_ge(s["a_filled"], n * NA + t + 1)
                        copy(stT[side][:, 4 * hf:4 * hf + 4, :], ring[:].bitcast(BF16).rearrange("p b (h t) -> p (b h) t", h=2)).then_inc(s["a_stT"], 1)
                        act.wait_ge(s["a_stT"], n * 8 + task[1] + 1)
                        act.sem_inc(a_freed[t % 2], 1)
                    elif kind == "shift":
                        g = task[1]
                        act.wait_ge(s["a_filled"], n * NA + t + 1)
                        copy(stT[0][:, 2 * g:2 * g + 2, :], ring[:, 0, :].bitcast(BF16).rearrange("p (h t) -> p h t", h=2)).then_inc(s["a_stT"], 1)
                        act.wait_ge(s["a_stT"], n * 8 + 5 + g)
                        act.sem_inc(a_freed[t % 2], 1)
                    elif kind == "exp":
                        act.wait_ge(s["a_filled"], n * NA + t + 1)
                        if x >= 5:
                            act.wait_ge(s["a_pv"], n * 20 + x - 4)
                        act.activation(probs[x % 5][:], ring[:].rearrange("p b t -> p (b t)"), ACT.Exp, scale=float(HD) ** -0.5).then_inc(s["a_exp"], 1)
                        act.wait_ge(s["a_exp"], n * 20 + x + 1)
                        act.sem_inc(a_freed[t % 2], 1)
                        if x % 5 == 1 and x > 1:
                            copy_out(x // 5 - 1)
                        x += 1
                copy_out(GROUPS - 1)
                act.wait_ge(s["a_filled"], n * NA + NA)
                copy(yT[:], aring[(NA - 1) % 2][:, 0, :]).then_inc(s["a_yT"], 1)
                act.wait_ge(s["a_yT"], n + 1)
                act.sem_inc(a_freed[(NA - 1) % 2], 1)

            def experts(n, base):
                for t, task in enumerate(E_TASKS):
                    kind, ring = task[0], wring[t % 2]
                    if kind == "gate":
                        _, e, c = task
                        k = 4 * e + c
                        act.wait_ge(s["w_filled"], base + t + 1)
                        if k >= 2:
                            act.wait_ge(s["e_ya"], n * 16 + k - 1)
                        act.activation(tg[k % 2][:], ring[:], ACT.Tanh).then_inc(s["e_tanh"], 1)
                    elif kind == "back":
                        act.wait_ge(s["e_down"], n * 16 + 16)
                        copy(moT[:], acc[:]).then_inc(s["e_moT"], 1)
                    elif kind == "none":
                        act.wait_ge(s["w_filled"], base + t + 1)
                        act.sem_inc(w_freed[t % 2], 1)

            def mamba(i, base):
                def freed(t, sem, value):
                    act.wait_ge(sem, value)
                    act.sem_inc(w_freed[t % 2], 1)

                for t, task in enumerate(M_TASKS):
                    kind, ring = task[0], wring[t % 2]
                    if kind in ("uT", "xbc", "z", "sums", "BT", "decay", "head_decay", "hT", "up", "none"):
                        act.wait_ge(s["w_filled"], base + t + 1)
                    if kind == "uT":
                        copy(uT[:], ring[:]).then_inc(s["m_uT"], 1)
                        freed(t, s["m_uT"], i + 1)
                    elif kind == "xbc":
                        copy(cpad[task[1]][:, 3:], ring[:]).then_inc(s["m_pad"], 1)
                        freed(t, s["m_pad"], 3 * i + [2, 3, 1][task[1]])
                    elif kind == "z":
                        act.activation(zt[task[1]][:], ring[:], ACT.Tanh).then_inc(s["m_ztanh"], 1)
                        if task[1] == 1:
                            act.wait_ge(s["m_dtexpin"], i + 1)
                            act.activation(sm["e"][:], sm["n"][:], ACT.Exp).then_inc(s["m_dtexp"], 1)
                            for k, c in enumerate((2, 0, 1)):
                                act.wait_ge(s["m_conv"], 3 * i + k + 1)
                                act.activation(ct[c][:], cacc[c][:], ACT.Tanh).then_inc(s["m_ctanh"], 1)
                    elif kind == "sums":
                        act.activation(edec[:].rearrange("p a j h -> p (a j h)"), ring[:, 0:32], ACT.Exp).then_inc(s["m_esum"], 1)
                        freed(t, s["m_esum"], i + 1)
                    elif kind == "BT":
                        copy(Bt[:].rearrange("p j n -> p (j n)"), ring[:, 0:4 * NS]).then_inc(s["m_Bt"], 1)
                        freed(t, s["m_Bt"], i + 1)
                    elif kind == "decay":
                        j = task[1]
                        act.activation(Ld[:, j].rearrange("p h t -> p (h t)"), ring[:], ACT.Exp).then_inc(s["m_L"], 1)
                        freed(t, s["m_L"], 4 * i + j + 1)
                    elif kind == "head_decay":
                        j = task[1]
                        act.activation(Ed[:, j].rearrange("p h t -> p (h t)"), ring[0:NS, :], ACT.Exp).then_inc(s["m_E"], 1)
                        freed(t, s["m_E"], 3 * i + j)
                        if j == 3:
                            for c in range(2):
                                act.wait_ge(s["m_gT"], 2 * i + c + 1)
                                act.activation(gq[c][:], gT[c][:], ACT.Square).then_inc(s["m_gq"], 1)
                            for j in range(4):
                                act.wait_ge(s["m_mh"], 4 * i + j + 1)
                                if j > 0:
                                    act.wait_ge(s["m_ssq"], 4 * i + j)
                                act.activation(sq[:], mh[:, j, :], ACT.Square, accum_out=ssq[:, j:j + 1]).then_inc(s["m_ssq"], 1)
                    elif kind == "hT":
                        copy(mhT[:], ring[:]).then_inc(s["m_hT"], 1)
                        freed(t, s["m_hT"], i + 1)
                    elif kind == "up":
                        c = task[1]
                        if c >= 2:
                            act.wait_ge(s["m_ga"], 4 * i + c - 1)
                        act.activation(gb[c % 2][:], ring[:], ACT.Identity, bias=v("b1", c)).then_inc(s["m_gb"], 1)
                        freed(t, s["m_gb"], 4 * i + c + 1)
                        act.activation(gt[c % 2][:], gb[c % 2][:], ACT.Tanh).then_inc(s["m_gtanh"], 1)
                    elif kind == "back":
                        act.wait_ge(s["m_mlp"], 4 * i + 4)
                        act.activation(mlT[:], acc[:], ACT.Identity, bias=v("b2")).then_inc(s["m_mlT"], 1)
                    elif kind == "none":
                        act.sem_inc(w_freed[t % 2], 1)

            act.wait_ge(s["const_loaded"], 16 * len(loads))
            act.wait_ge(s["setup_dve"], 1)
            act.activation(negA[:], negA[:], ACT.Exp).then_inc(s["setup_act"], 1)
            act.wait_ge(s["setup_dve2"], 1)
            for k in range(2):
                act.sem_inc(a_freed[k], 1)
                act.sem_inc(w_freed[k], 1)
            with act.Fori(0, NB) as i:
                attention(2 * i)
                experts(2 * i, i * WB)
                mamba(i, i * WB + NE)
                attention(2 * i + 1)
                experts(2 * i + 1, i * WB + NE + NM)

        @block.gpsimd
        def _(pool):
            def rsqrt(dst, src, ready, count, done):
                pool.wait_ge(ready, count)
                w = dst.shape[1]
                pool.tensor_tensor(dst[:], src[:], half[:, 0:w], ALU.pow).then_inc(done, 1)

            def attention(n):
                rsqrt(a_r, a_pw, s["a_var"], n + 1, s["a_rstd"])
                pool.memset(stk[0][:, :, MROW:MROW + 3], 0.0).then_inc(s["a_pad"], 1)

            def experts(n):
                rsqrt(e_r, e_pw, s["e_var"], n + 1, s["e_rstd"])

            def mamba(i):
                rsqrt(m_r, m_pw, s["m_var"], i + 1, s["m_rstd"])
                pool.wait_ge(s["m_a"], i + 1)
                for j in range(4):
                    pool.tensor_tensor(MV[:, j], upto[:].unsqueeze(1).to_broadcast([P, MH, P]),
                                       sm["a"][:, j, :].unsqueeze(2).to_broadcast([P, MH, P]), ALU.mult).then_inc(s["m_MV"], 1)
                pool.wait_ge(s["m_esum"], i + 1)
                pool.wait_ge(s["m_Xd"], 2 * i + 2)
                pool.tensor_tensor(Xw[:].rearrange("p j h d -> p (j h) d"), Xd[:].rearrange("p j h d -> p (j h) d"),
                                   edec[:, 0].rearrange("p j h -> p (j h)").unsqueeze(2).to_broadcast([P, 16, MP]), ALU.mult).then_inc(s["m_Xw"], 1)
                pool.wait_ge(s["m_G"], i + 1)
                for j in range(4):
                    pool.wait_ge(s["m_L"], 4 * i + j + 1)
                    pool.tensor_tensor(Ld[:, j], Ld[:, j], Gm[:, j].unsqueeze(1).to_broadcast([P, MH, P]), ALU.mult).then_inc(s["m_Lg"], 1)
                for j in range(1, 4):
                    pool.wait_ge(s["m_E"], 3 * i + j)
                    pool.tensor_tensor(Ed[:, j], Ed[:, j], CT[:, j * P:(j + 1) * P].unsqueeze(1).to_broadcast([NS, MH, P]), ALU.mult).then_inc(s["m_Ce"], 1)
                rsqrt(m_r, m_pw, s["m_var2"], i + 1, s["m_rstd2"])
                rsqrt(m_r, m_pw, s["m_var3"], i + 1, s["m_rstd3"])

            pool.memset(half[:], -0.5).then_inc(s["setup_pool"], 1)
            pool.memset(ones[:], 1.0).then_inc(s["setup_pool"], 1)
            for e in range(EXPERTS):
                pool.memset(tie[:, e:e + 1], float(EXPERTS - e)).then_inc(s["setup_pool"], 1)
            pool.memset(hT[:, 0:2], 0.0).then_inc(s["setup_pool"], 1)
            for c in range(3):
                pool.memset(cpad[c][:, 0:3], 0.0).then_inc(s["setup_pool"], 1)
            pool.memset(vx[:, :, :, HD:HD + 1], 1.0).then_inc(s["setup_pool"], 1)
            pool.memset(vx[:, :, :, HD + 1:], 0.0).then_inc(s["setup_pool"], 1)
            pool.memset(stk[0][:, :, MROW:], 0.0).then_inc(s["setup_pool"], 1)
            pool.memset(stk[1][:, :, MROW:MROW + 3], 1.0).then_inc(s["setup_pool"], 1)
            pool.memset(stk[1][:, :, MROW + 3:], 0.0).then_inc(s["setup_pool"], 1)
            pool.wait_ge(s["setup_pool"], 15)
            with pool.Fori(0, NB) as i:
                attention(2 * i)
                experts(2 * i)
                mamba(i)
                attention(2 * i + 1)
                experts(2 * i + 1)

        @block.vector
        def _(dve):
            links = [0, 0, 0]
            seen = {}

            def linker(sem, per, n):
                count = [0]

                def link(ins):
                    count[0] += 1
                    ins.then_inc(sem, 1)
                    dve.wait_ge(sem, n * per + count[0])
                return link, count

            def statistics(link, src, st, mv):
                for j in range(4):
                    last = dve.bn_stats(st[:, j, :], src[:, j, :])
                link(last)
                dve.memset(pause[:], 0.0)
                for j in range(4):
                    last = dve.bn_aggr(mv[:, j, :], st[:, j, :])
                link(last)

            def attention(n, src, src_ready, src_count):
                link, count = linker(s["a_link_dve"], A_LINKS, n)

                def freed(t, sem, value):
                    dve.wait_ge(sem, value)
                    dve.sem_inc(a_freed[t % 2], 1)

                dve.wait_ge(src_ready, src_count)
                statistics(link, src, a_st, a_mv)
                var, mean = a_mv[:, :, 1], a_mv[:, :, 0]
                link(dve.tensor_scalar(a_pw[:, 0:4], var, EPS, None, ALU.add))
                link(dve.reciprocal(a_rc[:], a_pw[:, 0:4]))
                link(dve.tensor_tensor(a_pw[:, 4:8], var, a_rc[:], ALU.mult))
                dve.tensor_scalar(a_pw[:, 4:8], a_pw[:, 4:8], EPS, None, ALU.add).then_inc(s["a_var"], 1)
                dve.wait_ge(s["a_rstd"], n + 1)
                link(dve.tensor_tensor(a_rc[:], a_r[:, 0:4], a_r[:, 4:8], ALU.mult))
                for j in range(4):
                    last = dve.tensor_scalar(hn[:, j, :], src[:, j, :], a_mv[:, j, 0:1], a_rc[:, j:j + 1], ALU.subtract, ALU.mult)
                last.then_inc(s["a_hn"], 1)
                for j in range(4):
                    last = dve.tensor_scalar(u[:, j, :], src[:, j, :], a_mv[:, j, 0:1], a_r[:, j:j + 1], ALU.subtract, ALU.mult)
                last.then_inc(s["a_link2"], 1)
                for t, task in enumerate(A_TASKS):
                    kind, ring = task[0], aring[t % 2]
                    filled = n * NA + t + 1
                    if kind == "hT":
                        dve.wait_ge(s["a_filled"], filled)
                        dve.tensor_scalar(hT[:, 2:], ring[:, 0, :], v("ln1_w"), v("ln1_b"), ALU.mult, ALU.add).then_inc(s["a_hT"], 1)
                        freed(t, s["a_hT"], n + 1)
                        link(dve.tensor_scalar(cT[:], hT[:, 0:T], v("aconv", 0), None, ALU.mult))
                        link(dve.scalar_tensor_tensor(out=cT[:], in0=hT[:, 1:T + 1], scalar=v("aconv", 1), in1=cT[:], op0=ALU.mult, op1=ALU.add))
                        dve.scalar_tensor_tensor(out=cT[:], in0=hT[:, 2:T + 2], scalar=v("aconv", 2), in1=cT[:], op0=ALU.mult, op1=ALU.add).then_inc(s["a_cT"], 1)
                    elif kind == "qkv":
                        dve.wait_ge(s["a_filled"], filled)
                        for b in range(2):
                            j = 2 * task[1] + b
                            qk = ring[:, b, 0:2 * P].rearrange("p (h d) -> p h d", d=HD)
                            hf = HD // 2
                            if j > 0:
                                dve.wait_ge(s["a_rope"], 4 * n + j)
                            dve.tensor_tensor(ra[:], qk, cos[:, j, :].unsqueeze(1).to_broadcast([P, 32, HD]), ALU.mult)
                            dve.tensor_tensor(rb[:, :, 0:hf], qk[:, :, hf:], sin[:, j, 0:hf].unsqueeze(1).to_broadcast([P, 32, hf]), ALU.mult)
                            dve.tensor_tensor(rb[:, :, hf:], qk[:, :, 0:hf], sin[:, j, hf:].unsqueeze(1).to_broadcast([P, 32, hf]), ALU.mult)
                            link(dve.tensor_copy(vx[:, j, :, 0:HD], ring[:, b, 2 * P:3 * P].rearrange("p (h d) -> p h d", d=HD)))
                            if b == 1:
                                dve.sem_inc(a_freed[t % 2], 1)
                            dve.tensor_tensor(rqk[0][:, 16 * j:16 * j + 16, :], ra[:, 0:16, :], rb[:, 0:16, :], ALU.add)
                            dve.tensor_tensor(rqk[1][:, 16 * j:16 * j + 16, :], ra[:, 16:32, :], rb[:, 16:32, :], ALU.add).then_inc(s["a_rope"], 1)
                        if task[1] == 1:
                            dve.wait_ge(s["a_rope"], 4 * n + 4)
                            for side in range(2):
                                dve.wait_ge(s["a_high"], 2 * n + side + 1)
                                hi = stk[side][:, :, 2 * HD:3 * HD]
                                dve.tensor_tensor(mid[side][:], rqk[side][:], hi, ALU.subtract).then_inc(s["a_mid"], 1)
                            for side in range(2):
                                dve.wait_ge(s["a_link"], 2 * n + side + 1)
                                dve.wait_ge(s["a_mid"], 2 * n + side + 1)
                                lo, md = (stk[0][:, :, 4 * HD:5 * HD], stk[0][:, :, 3 * HD:4 * HD]) if side == 0 else \
                                    (stk[1][:, :, 0:HD], stk[1][:, :, HD:2 * HD])
                                dve.tensor_tensor(lo, mid[side][:], md, ALU.subtract).then_inc(s["a_low"], 1)
                    elif kind == "max":
                        _, g, j, pair = task
                        w = P * (j + 1)
                        dve.wait_ge(s["a_filled"], filled)
                        h0 = GROUP * g
                        if j >= 2:
                            src_ap, dst = ring[:, :, 0:w], mx[:, j, h0 + 2 * pair:h0 + 2 * pair + 2]
                        else:
                            src_ap = ring[:, :, 0:2 * w].rearrange("p a (q w) -> p a q w", w=w)
                            dst = mx[:, j, h0:h0 + 4].rearrange("p (q a) -> p a q", a=2)
                        dve.tensor_reduce(dst, src_ap, AX_X, ALU.max).then_inc(s["a_max"], 1)
                        m = 6 * g + {3: 0, 2: 2, 1: 4, 0: 5}[j] + pair
                        freed(t, s["a_max"], n * 24 + m + 1)
                        if j == 0:
                            rows = stk[0][:].rearrange("p (j h) k -> p j h k", j=4)[:, :, h0:h0 + GROUP, :]
                            hi, md, lo = (rows[:, :, :, MROW + k] for k in range(3))
                            m_g, t_g = mx[:, :, h0:h0 + GROUP], mt[:, :, h0:h0 + GROUP]
                            link(dve.tensor_scalar(hi, m_g, -1.0, None, ALU.mult))
                            link(dve.tensor_scalar(t_g, m_g, -1.0, None, ALU.mult))
                            link(dve.tensor_tensor(t_g, t_g, hi, ALU.subtract))
                            link(dve.tensor_copy(md, t_g))
                            dve.tensor_tensor(lo, t_g, md, ALU.subtract).then_inc(s["a_shift"], 1)
                    elif kind == "back":
                        g = task[1]
                        dve.wait_ge(s["a_filled"], filled)
                        o = ring[:, 0, :].rearrange("p (j h k) -> p j h k", j=4, k=32)
                        link(dve.reciprocal(rden[:], o[:, :, :, HD]))
                        for j in range(4):
                            last = dve.tensor_tensor(y[:, j, 32 * g:32 * g + 32].rearrange("p (h d) -> p h d", d=HD), o[:, j, :, 0:HD],
                                                     rden[:, j, :].unsqueeze(2).to_broadcast([P, GROUP, HD]), ALU.mult)
                        last.then_inc(s["a_y"], 1)
                        freed(t, s["a_y"], n * GROUPS + g + 1)
                dve.wait_ge(s["a_proj"], n + 1)
                dve.wait_ge(s["a_link2"], n + 1)
                dve.tensor_tensor(u1[:], u[:], obank[:].rearrange("p (j c) -> p j c", j=4), ALU.add).then_inc(s["a_u1"], 1)
                assert count[0] == A_LINKS, count

            def experts(n, base, src, dst):
                link, count = linker(s["e_link"], E_LINKS, n)

                def freed(t, sem, value):
                    dve.wait_ge(sem, value)
                    dve.sem_inc(w_freed[t % 2], 1)

                dve.wait_ge(s["a_u1"], n + 1)
                statistics(link, u1, e_st, e_mv)
                dve.tensor_scalar(e_pw[:], e_mv[:, :, 1], EPS, None, ALU.add).then_inc(s["e_var"], 1)
                dve.wait_ge(s["e_rstd"], n + 1)
                for j in range(4):
                    last = dve.tensor_scalar(e_hn[:, j, :], u1[:, j, :], e_mv[:, j, 0:1], e_r[:, j:j + 1], ALU.subtract, ALU.mult)
                last.then_inc(s["e_hn"], 1)
                for t, task in enumerate(E_TASKS):
                    kind, ring = task[0], wring[t % 2]
                    if kind != "none":
                        dve.wait_ge(s["w_filled"], base + t + 1)
                    if kind == "hT":
                        dve.tensor_scalar(e_hT[:], ring[:], v("ln2_w"), v("ln2_b"), ALU.mult, ALU.add).then_inc(s["e_hT"], 1)
                        freed(t, s["e_hT"], n + 1)
                    elif kind == "logits":
                        lg = ring[:, 0:4 * EXPERTS].rearrange("p (j e) -> p j e", e=EXPERTS)
                        link(dve.tensor_reduce(lmax[:], lg, AX_X, ALU.max))
                        link(dve.tensor_tensor(lsel[:], lg, lmax[:].unsqueeze(2).to_broadcast([P, 4, EXPERTS]), ALU.is_equal))
                        dve.sem_inc(w_freed[t % 2], 1)
                        link(dve.tensor_tensor(lsel[:], lsel[:], tie[:].unsqueeze(1).to_broadcast([P, 4, EXPERTS]), ALU.mult))
                        link(dve.tensor_reduce(lmax[:], lsel[:], AX_X, ALU.max))
                        dve.tensor_tensor(pick[:], lsel[:], lmax[:].unsqueeze(2).to_broadcast([P, 4, EXPERTS]), ALU.is_equal).then_inc(s["e_pick"], 1)
                    elif kind == "mask":
                        e = task[1]
                        if e >= 2:
                            dve.wait_ge(s["e_down"], n * 16 + 4 * (e - 1) - 1)
                        dve.tensor_tensor(hm[e % 2][:], e_hT[:], ring[:], ALU.mult).then_inc(s["e_hm"], 1)
                        freed(t, s["e_hm"], n * EXPERTS + e + 1)
                    elif kind == "gate":
                        _, e, c = task
                        k = 4 * e + c
                        dve.wait_ge(s["e_tanh"], n * 16 + k + 1)
                        ins = dve.scalar_tensor_tensor(out=sg[k % 2][:], in0=tg[k % 2][:], scalar=1.0, in1=ring[:], op0=ALU.add, op1=ALU.mult)
                        ins.then_inc(s["e_sg"], 1)
                        freed(t, s["e_sg"], n * 16 + k + 1)
                    elif kind == "value":
                        _, e, c = task
                        k = 4 * e + c
                        if k >= 2:
                            dve.wait_ge(s["e_down"], n * 16 + k - 1)
                        dve.tensor_tensor(ya[k % 2][:], sg[k % 2][:], ring[:], ALU.mult).then_inc(s["e_ya"], 1)
                        freed(t, s["e_ya"], n * 16 + k + 1)
                    elif kind == "back":
                        link(dve.tensor_tensor(tmp[:], u1[:], ring[:].rearrange("p (j c) -> p j c", j=4), ALU.add))
                        dve.sem_inc(w_freed[t % 2], 1)
                        if dst is x3:
                            dve.wait_ge(s["out_stored"], 8 * n + 8)
                        dve.scalar_tensor_tensor(out=dst[:].rearrange("p j c -> p (j c)"), in0=tmp[:].rearrange("p j c -> p (j c)"), scalar=0.5,
                                                 in1=src[:].rearrange("p j c -> p (j c)"), op0=ALU.mult, op1=ALU.add).then_inc(s["e_x"], 1)
                        dve.wait_ge(s["e_x"], n + 1)
                        if dst is x1:
                            dve.sem_inc(s["x_free"], 1)
                assert count[0] == E_LINKS, count

            def mamba(i, base):
                link, count = linker(s["m_link"], M_LINKS, i)

                def freed(t, sem, value):
                    dve.wait_ge(sem, value)
                    dve.sem_inc(w_freed[t % 2], 1)

                statistics(link, x1, m_st, m_mv)
                dve.tensor_scalar(m_pw[:], m_mv[:, :, 1], EPS, None, ALU.add).then_inc(s["m_var"], 1)
                dve.wait_ge(s["m_rstd"], i + 1)
                for j in range(4):
                    last = dve.tensor_scalar(mu[:, j, :], x1[:, j, :], m_mv[:, j, 0:1], m_r[:, j:j + 1], ALU.subtract, ALU.mult)
                last.then_inc(s["m_u"], 1)

                def convolve(k, c):
                    dve.wait_ge(s["m_pad"], 3 * i + k + 1)
                    link(dve.tensor_scalar(cacc[c][:], cpad[c][:, 0:T], v("mconv", TAPS * c), v("mconv_b", c), ALU.mult, ALU.add))
                    for q in range(1, TAPS):
                        ins = dve.scalar_tensor_tensor(out=cacc[c][:], in0=cpad[c][:, q:q + T], scalar=v("mconv", TAPS * c + q), in1=cacc[c][:],
                                                       op0=ALU.mult, op1=ALU.add)
                        if q < TAPS - 1:
                            link(ins)
                    ins.then_inc(s["m_conv"], 1)

                def silu(dst, th, h):
                    return dve.scalar_tensor_tensor(out=dst, in0=th, scalar=1.0, in1=h, op0=ALU.add, op1=ALU.mult)

                def step_size():
                    S = {k: sm[k][:] for k in sm}
                    flat = {k: sm[k][:].rearrange("p j h -> p (j h)") for k in sm}
                    dve.wait_ge(s["m_dtexp"], i + 1)
                    link(dve.tensor_scalar(S["d"], S["e"], 2.0, None, ALU.add))
                    link(dve.reciprocal(S["r"], S["d"]))
                    link(dve.tensor_tensor(S["z"], S["e"], S["r"], ALU.mult))
                    link(dve.tensor_tensor(S["z2"], S["z"], S["z"], ALU.mult))
                    link(dve.tensor_scalar(S["p"], S["z2"], 1.0 / (2 * ATANH_TERMS - 1), None, ALU.mult))
                    for k in range(ATANH_TERMS - 2, 0, -1):
                        link(dve.scalar_tensor_tensor(out=flat["p"], in0=flat["p"], scalar=1.0 / (2 * k + 1), in1=flat["z2"], op0=ALU.add, op1=ALU.mult))
                    link(dve.scalar_tensor_tensor(out=flat["q"], in0=flat["p"], scalar=1.0, in1=flat["z"], op0=ALU.add, op1=ALU.mult))
                    link(dve.tensor_scalar(S["w"], S["x"], 0.0, None, ALU.max))
                    link(dve.scalar_tensor_tensor(out=flat["dt"], in0=flat["q"], scalar=2.0, in1=flat["w"], op0=ALU.mult, op1=ALU.add))
                    link(dve.tensor_tensor(S["w"], S["dt"], negA[:].unsqueeze(1).to_broadcast([P, 4, MH]), ALU.mult))
                    dve.tensor_scalar(S["a"], S["w"], -1000.0, None, ALU.max).then_inc(s["m_a"], 1)

                for t, task in enumerate(M_TASKS):
                    kind, ring = task[0], wring[t % 2]
                    if kind in ("dt", "z", "xsT", "G", "state", "norm", "out", "back"):
                        dve.wait_ge(s["w_filled"], base + t + 1)
                    if kind == "dt":
                        link(dve.tensor_tensor(sm["x"][:], ring[:, 0:4 * MH].rearrange("p (j h) -> p j h", h=MH),
                                               v("dt_bias", 0, MH).unsqueeze(1).to_broadcast([P, 4, MH]), ALU.add))
                        dve.sem_inc(w_freed[t % 2], 1)
                        fx = sm["x"][:].rearrange("p j h -> p (j h)")
                        dve.scalar_tensor_tensor(out=sm["n"][:].rearrange("p j h -> p (j h)"), in0=fx, scalar=-1.0, in1=fx,
                                                 op0=ALU.mult, op1=ALU.min).then_inc(s["m_dtexpin"], 1)
                    elif kind == "z":
                        c = task[1]
                        dve.wait_ge(s["m_ztanh"], 2 * i + c + 1)
                        silu(zs[c][:], zt[c][:], ring[:]).then_inc(s["m_zs"], 1)
                        freed(t, s["m_zs"], 2 * i + c + 1)
                        if c == 1:
                            step_size()
                            for k, cc in enumerate((2, 0, 1)):
                                convolve(k, cc)
                            dve.wait_ge(s["m_ctanh"], 3 * i + 1)
                            silu(BT[:], ct[2][0:NS, :], cacc[2][0:NS, :]).then_inc(s["m_BC"], 1)
                            silu(CT[:], ct[2][NS:P, :], cacc[2][NS:P, :]).then_inc(s["m_BC"], 1)
                            for c2 in range(2):
                                dve.wait_ge(s["m_ctanh"], 3 * i + c2 + 2)
                                silu(xs[c2][:], ct[c2][:], cacc[c2][:]).then_inc(s["m_xs"], 1)
                    elif kind == "xsT":
                        c = task[1]
                        r4 = ring[:].rearrange("p (j a d) -> p j a d", j=4, a=2)
                        for j in range(4):
                            last = dve.tensor_tensor(Xd[:, j, 2 * c:2 * c + 2, :], r4[:, j], sm["dt"][:, j, 2 * c:2 * c + 2].unsqueeze(2).to_broadcast([P, 2, MP]), ALU.mult)
                        last.then_inc(s["m_Xd"], 1)
                        freed(t, s["m_Xd"], 2 * i + c + 1)
                    elif kind == "G":
                        dve.tensor_tensor(Gm[:], ring[:].rearrange("p (j t) -> p j t", j=4), upto[:].unsqueeze(1).to_broadcast([P, 4, P]), ALU.mult).then_inc(s["m_G"], 1)
                        freed(t, s["m_G"], i + 1)
                    elif kind == "state":
                        j = task[1]
                        new = ring[0:NS, 0:MH * MP].rearrange("p (h d) -> p h d", d=MP)
                        if j == 0:
                            dve.tensor_copy(St[:, 1], new).then_inc(s["m_St"], 1)
                        else:
                            dve.wait_ge(s["m_esum"], i + 1)
                            dve.wait_ge(s["m_St"], 3 * i + j)
                            link(dve.tensor_tensor(St[:, 0], St[:, j], edec[0:NS, 1, j, :].unsqueeze(2).to_broadcast([NS, MH, MP]), ALU.mult))
                            dve.tensor_tensor(St[:, j + 1], St[:, 0], new, ALU.add).then_inc(s["m_St"], 1)
                        freed(t, s["m_St"], 3 * i + j + 1)
                    elif kind == "norm":
                        link(dve.tensor_scalar(m_pw[:], ring[:, 0:4], 1.0 / DIN, EPS, ALU.mult, ALU.add))
                        dve.sem_inc(w_freed[t % 2], 1)
                        dve.sem_inc(s["m_var2"], 1)
                    elif kind == "out":
                        dve.wait_ge(s["m_rstd2"], i + 1)
                        for j in range(4):
                            dve.scalar_tensor_tensor(out=mh[:, j, :], in0=ring[:, j * P:(j + 1) * P], scalar=m_r[:, j:j + 1], in1=mu[:, j, :],
                                                     op0=ALU.mult, op1=ALU.add).then_inc(s["m_mh"], 1)
                        freed(t, s["m_mh"], 4 * i + 4)
                        dve.wait_ge(s["m_ssq"], 4 * i + 4)
                        dve.tensor_scalar(m_pw[:], ssq[:], 1.0 / P, EPS, ALU.mult, ALU.add).then_inc(s["m_var3"], 1)
                        dve.wait_ge(s["m_rstd3"], i + 1)
                        for j in range(4):
                            last = dve.tensor_scalar(m_hn[:, j, :], mh[:, j, :], m_r[:, j:j + 1], None, ALU.mult)
                        last.then_inc(s["m_hn"], 1)
                        link(dve.tensor_tensor(tmp[:], mh[:], x1[:], ALU.add))
                    elif kind == "up":
                        c = task[1]
                        dve.wait_ge(s["m_gtanh"], 4 * i + c + 1)
                        if c >= 2:
                            dve.wait_ge(s["m_mlp"], 4 * i + c - 1)
                        silu(ga[c % 2][:], gt[c % 2][:], gb[c % 2][:]).then_inc(s["m_ga"], 1)
                    elif kind == "back":
                        dve.tensor_tensor(x2[:], tmp[:], ring[:].rearrange("p (j c) -> p j c", j=4), ALU.add).then_inc(s["m_x"], 1)
                        freed(t, s["m_x"], i + 1)
                    elif kind == "head_decay" and task[1] == 3:
                        for c in range(2):
                            dve.wait_ge(s["m_Y"], 2 * i + c + 1)
                            dve.scalar_tensor_tensor(out=yd[:], in0=xs[c][:], scalar=v("D", c), in1=acc[:], op0=ALU.mult, op1=ALU.add).then_inc(s["m_yd"], 1)
                            dve.wait_ge(s["m_yd"], 2 * i + c + 1)
                            dve.tensor_tensor(gT[c][:], yd[:], zs[c][:], ALU.mult).then_inc(s["m_gT"], 1)
                            dve.wait_ge(s["m_gT"], 2 * i + c + 1)
                assert count[0] == M_LINKS, count

            sc = 0

            def step(ins):
                nonlocal sc
                sc += 1
                ins.then_inc(s["setup_chain"], 1)

            dve.wait_ge(s["const_loaded"], 16 * len(loads))
            dve.tensor_scalar(negA[:], v("A_log", 0, MH), 88.0, None, ALU.min).then_inc(s["setup_dve"], 1)
            step(dve.tensor_copy(identb[:], ident[:]))
            step(dve.tensor_scalar(neg_keys[:], after[:], 0.0, None, ALU.mult))
            step(dve.tensor_scalar(neg_queries[:], after[:], NEG, None, ALU.mult))
            step(dve.tensor_scalar(v("mconv", 0, 12), v("mconv", 0, 12), 0.5, None, ALU.mult))
            step(dve.tensor_scalar(v("mconv_b", 0, 3), v("mconv_b", 0, 3), 0.5, None, ALU.mult))
            step(dve.tensor_scalar(v("b1", 0, 4), v("b1", 0, 4), 0.5, None, ALU.mult))
            dve.wait_ge(s["setup_chain"], 6)
            step(dve.tensor_tensor(tmp[:, 0, :], upto[:], ident[:], ALU.subtract))
            dve.wait_ge(s["setup_chain"], 7)
            step(dve.tensor_scalar(neg_keys[:], tmp[:, 0, :], NEG, None, ALU.mult))
            dve.wait_ge(s["weights_loaded"], 16 * len(wloads))
            for e in range(EXPERTS):
                step(dve.tensor_scalar(wv[:, e, 0:DFF], wv[:, e, 0:DFF], 0.5, None, ALU.mult))
            step(dve.tensor_scalar(W_in[:, 0:DIN], W_in[:, 0:DIN], 0.5, None, ALU.mult))
            step(dve.tensor_scalar(w1[:], w1[:], v("rms_w"), 0.5, ALU.mult, ALU.mult))
            for c in range(2):
                step(dve.tensor_scalar(W_out[:, c, :], W_out[:, c, :], v("norm_w", c), None, ALU.mult))
            dve.wait_ge(s["setup_act"], 1)
            step(dve.tensor_scalar(negA[:], negA[:], -1.0, None, ALU.mult))
            dve.wait_ge(s["setup_chain"], sc)
            dve.wait_ge(s["setup_pool"], 15)
            dve.sem_inc(s["setup_dve2"], 1)
            with dve.Fori(0, NB) as i:
                attention(2 * i, x0, s["x_loaded"], 16 * i + 16)
                experts(2 * i, i * WB, x0, x1)
                mamba(i, i * WB + NE)
                attention(2 * i + 1, x2, s["m_x"], i + 1)
                experts(2 * i + 1, i * WB + NE + NM, x2, x3)


_WEIGHTS = {"attn_w": "L0_ffn_attn_w", "proj_w": "L0_ffn_proj_w", "wv": "L0_ffn_expert_wv", "ep": "L0_ffn_expert_proj",
            "W_in": "L0_attn_W_in", "W_out": "L0_attn_W_out", "w1": "L0_attn_mlp_w1", "w2": "L0_attn_mlp_w2"}


def packed_vectors(inputs):
    import numpy as np

    def get(name):
        return np.asarray(inputs[name])

    def rows(a):
        return np.broadcast_to(a[None, :], (P, a.shape[0]))

    cols = {
        "ln1_w": get("L0_ffn_ln1_w")[:, None], "ln1_b": get("L0_ffn_ln1_b")[:, None],
        "ln2_w": get("L0_ffn_ln2_w")[:, None], "ln2_b": get("L0_ffn_ln2_b")[:, None],
        "aconv": get("L0_ffn_conv_w")[:, 0, :], "router": get("L0_ffn_router_w"),
        "mconv": get("L0_attn_conv_w").reshape(3, P, TAPS).transpose(1, 0, 2).reshape(P, 3 * TAPS),
        "mconv_b": get("L0_attn_conv_b").reshape(3, P).T,
        "dt_bias": rows(get("L0_attn_dt_bias")), "A_log": rows(get("L0_attn_A_log")),
        "D": np.repeat(get("L0_attn_D_param"), MP).reshape(2, P).T,
        "norm_w": get("L0_attn_norm_w").reshape(2, P).T, "rms_w": get("L0_attn_rms_w")[:, None],
        "b1": get("L0_attn_mlp_b1").reshape(4, P).T, "b2": get("L0_attn_mlp_b2")[:, None],
    }
    return np.ascontiguousarray(np.concatenate([cols[name] for name in PACK], axis=1))


def shape_constants(T):
    import numpy as np
    r = np.arange(P)
    upto = (r[:, None] <= r[None, :]).astype(np.float32)
    after = (r[:, None] > r[None, :]).astype(np.float32)
    inv = (np.float32(1.0) / np.float32(10000.0) ** (np.arange(0, HD, 2, dtype=np.float32) / np.float32(HD))).astype(np.float32)
    ang = np.arange(T, dtype=np.float32)[:, None] * inv[None, :]
    ang = np.concatenate([ang, ang], axis=1)
    sign = np.where(np.arange(HD) < HD // 2, np.float32(-1), np.float32(1))
    cos = np.cos(ang).astype(np.float32).reshape(T // P, P, HD).transpose(1, 0, 2).reshape(P, -1)
    sin = (np.sin(ang) * sign).astype(np.float32).reshape(T // P, P, HD).transpose(1, 0, 2).reshape(P, -1)
    return np.ascontiguousarray(np.concatenate([np.eye(P, dtype=np.float32), upto, after, cos, sin], axis=1))


def kernel(**inputs):
    import numpy as np
    import concourse.bacc as bacc
    from concourse.bass_utils import run_bass_kernel_spmd

    x = np.ascontiguousarray(inputs["L0_attn_hidden_tokens"])
    host = {"x": x, "packed": packed_vectors(inputs), "consts": shape_constants(x.shape[1])}
    host.update({k: np.ascontiguousarray(inputs[n]) for k, n in _WEIGHTS.items()})
    nc = bacc.Bacc("TRN2", target_bir_lowering=False, num_devices=1)
    A = {k: nc.dram_tensor(f"in_{k}", a.shape, F32, kind="ExternalInput").ap() for k, a in host.items()}
    A["out"] = nc.dram_tensor("out_x", x.shape, F32, kind="ExternalOutput").ap()
    build_program(nc, A)
    r = run_bass_kernel_spmd(nc, [{f"in_{k}": a for k, a in host.items()}], core_ids=[0])
    return r.results[0]["out_x"]
```

```python
import concourse.bass as bass
from concourse import mybir
from contextlib import ExitStack

F32 = mybir.dt.float32
BF16 = mybir.dt.bfloat16
ALU = mybir.AluOpType
ACT = mybir.ActivationFunctionType
AX_X = mybir.AxisListType.X

P = 128
EPS = 1e-5
HEADS, HD = 16, 8
GROUP = 4
GROUPS = HEADS // GROUP
STACK = 64
NPROD = 6
EXPS = 10
PV_LAG = 3
MROW = NPROD * HD
NEG = -1e30
EXPERTS, DFF = 4, 512
MH, MP, NS, TAPS = 4, 64, 64, 4
DIN = MH * MP
MLP = 512
ATANH_TERMS = 8

PACK = {}
_at = 0
for _name, _w in (("ln1_w", 1), ("ln1_b", 1), ("ln2_w", 1), ("ln2_b", 1), ("aconv", 3), ("router", EXPERTS),
                  ("mconv", 3 * TAPS), ("mconv_b", 3), ("dt_bias", MH), ("A_log", MH), ("D", 2),
                  ("norm_w", 2), ("rms_w", 1), ("b1", 4), ("b2", 1)):
    PACK[_name] = (_at, _w)
    _at += _w
PACKED = _at


NO_FILL = ("stats", "norm", "high", "mid", "low", "proj", "e_stats", "e_norm", "last_down", "pv_last", "conv", "step_size", "BC", "xs", "Y", "mh_var", "mh_norm")


def attention_steps():
    def maxima(g):
        return ([("max", g, j, h) for j in (3, 2) for h in range(GROUP)] + [("max", g, 1, a) for a in range(2)]
                + [("max", g, 0, 0)])
    steps = [("stats",), ("norm",), ("hT",)] + [("qkv", j) for j in range(4)] + [("high",), ("mid",), ("low",)]
    steps += [("qkT", i) for i in range(8)] + maxima(0)
    for g in range(GROUPS):
        nxt = maxima(g + 1) if g + 1 < GROUPS else [None] * 11
        seq = nxt[:3] + [("shift", g), nxt[3]]
        for x in range(EXPS):
            seq += [("exp", g, x), ("back", g - 1) if g and x == EXPS - 5 else None] + nxt[4 + x:5 + x]
        steps += [t for t in seq if t]
    return steps + [("pv_last",), ("back", GROUPS - 1), ("yT",), ("proj",), ("e_stats",), ("e_norm",)]


def expert_steps():
    steps = [("hT",), ("logits",), ("mask", 0)]
    for e in range(EXPERTS):
        for c in range(DFF // P):
            steps += [("gate", e, c), ("value", e, c)]
            if c == 1 and e + 1 < EXPERTS:
                steps.append(("mask", e + 1))
    return steps + [("last_down",), ("back",)]


def mamba_steps():
    return ([("stats",), ("norm",), ("uT",), ("xbc", 2), ("xbc", 0), ("dt",), ("conv", 2), ("xbc", 1), ("z", 0), ("conv", 0),
             ("z", 1), ("conv", 1), ("step_size",), ("BC",), ("sums",), ("xs", 0), ("xs", 1), ("xsT", 0), ("xsT", 1), ("BT",), ("G",)]
            + [("decay", j) for j in range(4)] + [("state", j) for j in range(3)] + [("head_decay", j) for j in range(1, 4)]
            + [("Y", c, j) for c in range(2) for j in range(4)]
            + [("sumsq",), ("out",), ("mh_var",), ("mh_norm",), ("hT",)] + [("up", c) for c in range(4)] + [("last_down",), ("back",)])


SLOTS = 3


def numbered(steps):
    fills, out = 0, []
    for step in steps:
        out.append((None if step[0] in NO_FILL else fills, step))
        fills += step[0] not in NO_FILL
    while fills % SLOTS:
        out.append((fills, ("none", fills)))
        fills += 1
    return out, fills, {step: t for t, step in out if t is not None}


A_TASKS, NA, A_STEP = numbered(attention_steps())
E_TASKS, NE, E_STEP = numbered(expert_steps())
M_TASKS, NM, M_STEP = numbered(mamba_steps())
A_LAP, W_LAP = NA // SLOTS, (4 * NE + 2 * NM) // SLOTS

A_TIMES = {"stats": (1, 0, 0, 2.5, 3.5), "norm": (1, 0, 0, 2, 0), "hT": (1, 1.7, 0.6, 2, 1),
           "qkv": (3, 0.7, 0, 1.6, 0), "high": (1, 0, 2.7, 0, 2), "mid": (1, 0, 2, 1.2, 0),
           "low": (1, 0, 0, 1.3, 0), "qkT": (2, 0.5, 0.8, 0.8, 0), "max": (3, 0.25, 0, 0.65, 0),
           "shift": (3, 0.5, 2.1, 0, 0), "exp": (3, 0.75, 0.63, 0, 0), "back": (1, 1.7, 0, 1, 0),
           "pv_last": (1, 1.3, 0.6, 0, 0), "yT": (1, 1.7, 0.6, 0, 0), "proj": (1, 1.7, 0, 0.7, 0),
           "e_stats": (1, 0, 0, 2.5, 3.5), "e_norm": (1, 0, 0, 1.2, 0), "none": (1, 0, 0, 0, 0)}
E_TIMES = {"hT": (1, 1.7, 0.6, 0, 0), "logits": (1, 1.7, 0, 1.5, 0), "mask": (3, 0.35, 0, 0.96, 0),
           "gate": (3, 0.9, 0.65, 0, 0), "value": (3, 1.8, 0, 1.3, 0), "last_down": (1, 0.9, 0.65, 0, 0),
           "back": (1, 1.7, 0, 1.5, 0), "none": (1, 0, 0, 0, 0)}
M_TIMES = {"stats": (1, 0, 0, 2.5, 2.5), "norm": (1, 0, 0, 1, 0), "uT": (1, 1.7, 0.6, 0, 0),
           "xbc": (3, 0.9, 1.3, 0, 0), "dt": (3, 1.7, 0, 0.5, 0), "conv": (2, 0, 0.6, 2.5, 0),
           "z": (3, 0.9, 0.6, 0.8, 0), "step_size": (1, 0, 0.6, 4.5, 0), "BC": (1, 0, 0, 1.5, 0.5),
           "sums": (1, 0.9, 0.3, 0, 0), "xs": (3, 0, 0, 0.7, 0), "xsT": (2, 1.7, 0, 1, 0),
           "BT": (3, 0.8, 0.4, 0, 0), "G": (3, 1.7, 0, 0.6, 0), "decay": (3, 0.9, 0.6, 0, 0),
           "state": (3, 0.4, 0, 0.6, 0), "head_decay": (3, 0.9, 0.6, 0, 0), "Y": (2, 1.88, 0, 0.3, 0),
           "sumsq": (1, 3.4, 0, 0.3, 3), "out": (2, 3.4, 0.8, 1, 0), "mh_var": (1, 0, 0, 0.2, 3),
           "mh_norm": (1, 0, 0, 1.3, 0), "hT": (1, 1.7, 0.6, 0, 0), "up": (3, 1.7, 1.3, 0.7, 0),
           "last_down": (1, 0.9, 0.6, 0, 0), "back": (1, 1.7, 0, 0.7, 0), "none": (1, 0, 0, 0, 0)}
FIRST = (("qkv", 0), ("qkT", 0), ("max", 0, 3, 0), ("exp", 0, 0), ("mask", 0), ("gate", 0, 0), ("xbc", 2), ("up", 0))


def times(steps, table):
    return [((1,) + table[s[0]][1:]) if s in FIRST else table[s[0]] for _, s in steps]


A_COST, E_COST, M_COST = times(A_TASKS, A_TIMES), times(E_TASKS, E_TIMES), times(M_TASKS, M_TIMES)

A_LINKS, H_LINKS, E_LINKS, M_LINKS = 28, 2, 5, 28


E1_AT = [0, NE + NM]
M_AT = [NE, 2 * NE + NM]
E2_AT = [2 * NE + 2 * NM, 3 * NE + 2 * NM]


PA = [0.98, 1.0]
SL = 1.0
def merge(first, second, ahead):
    lanes, through, order = (first, second), ([], []), []
    engines = [0.0, 0.0, 0.0]
    total = [sum(max(c[1:4]) for c in lane) for lane in lanes]
    behind = [0.0, 0.0]
    while len(through[0]) < len(first) or len(through[1]) < len(second):
        start = {}
        for k in range(2):
            if len(through[k]) < len(lanes[k]):
                cost, done = lanes[k][len(through[k])], through[k]
                before = done[len(done) - int(cost[0])] if len(done) >= cost[0] else 0.0
                first_engine = min([e for e in range(3) if cost[1 + e] > 0] or [0])
                start[k] = max(engines[first_engine], before)
        soonest = min(start.values())
        k = min(start, key=lambda k: (max(start[k], soonest + SL), behind[k] / total[k] * (1 / ahead if k == 0 else 1)))
        cost, at = lanes[k][len(through[k])], start[k]
        for e in range(3):
            if cost[1 + e]:
                at = engines[e] = max(at, engines[e]) + cost[1 + e] + (0.15 if e else 0)
        behind[k] += max(cost[1:4])
        through[k].append(at + cost[4])
        order.append(k)
    return order


def together(first, second, order):
    for k in order:
        next((first, second)[k])


def alone(stage):
    for _ in stage:
        pass


def schedule(pairs, loop, A1, A2, E1, E2, M, weights=lambda: None):
    def expert_then_mamba(i, k):
        yield from E1(i, k)
        yield from M(i, k)

    long, short = merge(A_COST, E_COST + M_COST, PA[0]), merge(A_COST, E_COST, PA[1])

    def rest(i):
        together(A1(i, 1), expert_then_mamba(i, 0), long)
        together(A2(i, 0), expert_then_mamba(i, 1), long)
        together(A2(i, 1), E2(i, 0), short)

    alone(A1(0, 0))
    weights()
    with loop(0, pairs - 1) as i:
        rest(i)
        together(A1(i + 1, 0), E2(i, 1), short)
    rest(pairs - 1)
    alone(E2(pairs - 1, 1))


def build_program(nc, A):
    NB, T, C = A["x"].shape
    NT = T // P
    assert C == P and NT == 4
    x_v = A["x"].rearrange("b (j p) c -> b p j c", p=P)
    out_v = A["out"].rearrange("b (j p) c -> b p j c", p=P)

    with ExitStack() as ctx:
        def sb(name, shape, dt=F32):
            return ctx.enter_context(nc.sbuf_tensor(name, shape, dt))

        def pb(name, shape, dt=F32):
            return ctx.enter_context(nc.psum_tensor(name, shape, dt))

        aring = [pb(f"aring{i}", [P, 512]) for i in range(SLOTS)]
        obank = pb("obank", [P, 512])
        wring = [pb(f"wring{i}", [P, 512]) for i in range(SLOTS)]
        acc = pb("acc", [P, 512])

        ident = sb("ident", [P, P])
        identb = sb("identb", [P, P], BF16)
        upto = sb("upto", [P, P])
        after = sb("after", [P, P])
        ones = sb("ones", [P, P])
        neg_keys = sb("neg_keys", [P, P], BF16)
        neg_queries = sb("neg_queries", [P, P], BF16)
        cos = sb("cos", [P, 4, HD])
        sin = sb("sin", [P, 4, HD])
        vec = sb("vec", [P, PACKED])
        attn_w = sb("attn_w", [P, 3 * P])
        proj_w = sb("proj_w", [P, P])
        wv = sb("wv", [P, EXPERTS, 2 * DFF])
        ep = sb("ep", [P, EXPERTS, 4, P])
        W_in = sb("W_in", [P, 2 * DIN + 2 * NS + MH])
        W_out = sb("W_out", [P, 2, P])
        w1 = sb("w1", [P, MLP])
        w2 = sb("w2", [P, 4, P])
        negA = sb("negA", [P, MH])
        tie = sb("tie", [P, EXPERTS])
        pause = sb("pause", [P, 1])
        half = sb("half", [P, 8])

        def v(name, k=0, n=1):
            a = PACK[name][0] + k
            return vec[:, a:a + n]

        x0 = [sb(f"x0_{k}", [P, 4, P]) for k in range(2)]
        x1 = [sb(f"x1_{k}", [P, 4, P]) for k in range(2)]
        x2 = [sb(f"x2_{k}", [P, 4, P]) for k in range(2)]
        x3 = sb("x3", [P, 4, P])
        a_st = sb("a_st", [P, 4, 6])
        a_mv = sb("a_mv", [P, 4, 2])
        a_pw = sb("a_pw", [P, 8])
        a_r = sb("a_r", [P, 8])
        a_rc = sb("a_rc", [P, 4])
        u = sb("u", [P, 4, P])
        hn = sb("hn", [P, 4, P])
        hT = sb("hT", [P, 2 + T])
        cT = sb("cT", [P, T])
        ra = sb("ra", [P, 32, HD])
        rb = sb("rb", [P, 32, HD])
        prob_mem = sb("prob_mem", [P, 5, 1024])
        probs = [prob_mem[:, i // 2, (i % 2) * 512:(i % 2 + 1) * 512] for i in range(EXPS)]
        stk = [sb("stk_q", [P, 64, STACK], BF16)[:],
               prob_mem[:, 0:2].bitcast(BF16).rearrange("p a (h k) -> p (a h) k", k=STACK)]
        stq = [sb(f"stq{a}", [P, 8, T], BF16) for a in range(2)]
        stkT = sb("stkT", [P, 8, T], BF16)
        rqk = [probs[6 + k].rearrange("p (h d) -> p h d", d=HD) for k in range(2)]
        mid = [probs[8 + k].rearrange("p (h d) -> p h d", d=HD) for k in range(2)]
        vx = sb("vx", [P, 4, HEADS, 32])
        mx = sb("mx", [P, 4, HEADS])
        mt = sb("mt", [P, 4, HEADS])
        osb = sb("osb", [P, T])
        rden = sb("rden", [P, 4, GROUP])
        y = hn
        yT = cT
        u1 = [sb(f"u1_{k}", [P, 4, P]) for k in range(2)]
        e_st = sb("e_st", [P, 4, 6])
        e_mv = sb("e_mv", [P, 4, 2])
        e_pw = sb("e_pw", [P, 4])
        e_r = sb("e_r", [P, 4])
        e_hn = sb("e_hn", [P, 4, P])
        e_hT = sb("e_hT", [P, T])
        lmax = sb("lmax", [P, 4])
        lsel = sb("lsel", [P, 4, EXPERTS])
        pick = sb("pick", [P, 4, EXPERTS], BF16)
        scratch = [sb(f"scratch{i}", [P, 4, T]) for i in range(2)]
        hm = [scratch[0][:, i] for i in range(2)]
        ya = [scratch[0][:, 2 + i] for i in range(2)]
        tg = [scratch[1][:, i] for i in range(2)]
        sg = [scratch[1][:, 2 + i] for i in range(2)]
        moT = sb("moT", [P, T])
        tmp = sb("tmp", [P, 4, P])
        m_st = sb("m_st", [P, 4, 6])
        m_mv = sb("m_mv", [P, 4, 2])
        m_pw = sb("m_pw", [P, 4])
        m_r = sb("m_r", [P, 4])
        mu = sb("mu", [P, 4, P])
        uT = sb("uT", [P, T])
        cpad = [sb(f"cpad{i}", [P, 3 + T]) for i in range(3)]
        conv = sb("conv", [P, 6, T])
        cacc = [conv[:, i] for i in range(3)]
        ct = [conv[:, 3 + i] for i in range(3)]
        xs = [sb(f"xs{i}", [P, T]) for i in range(2)]
        BT = sb("BT", [NS, T])
        CT = sb("CT", [NS, T])
        zt = [sb(f"zt{i}", [P, T]) for i in range(2)]
        zs = [sb(f"zs{i}", [P, T]) for i in range(2)]
        sm = {k: sb("sm_" + k, [P, 4, MH]) for k in ("x", "n", "e", "d", "r", "z", "z2", "p", "q", "w", "dt", "a")}
        edec = sb("edec", [P, 2, 4, MH])
        MV = scratch[0][:].rearrange("p j (h t) -> p j h t", h=MH)
        Ld = conv[:, 0:4].rearrange("p j (h t) -> p j h t", h=MH)
        Ed = sb("Ed", [NS, 4, MH, P])
        Xd = scratch[1][:, 0:2].rearrange("p a (b h d) -> p (a b) h d", b=2, h=MH)
        Xw = scratch[1][:, 2:4].rearrange("p a (b h d) -> p (a b) h d", b=2, h=MH)
        Bt = sb("Bt", [P, 4, NS])
        Gm = sb("Gm", [P, 4, P])
        St = sb("St", [NS, 4, MH, MP])
        yd = e_hT[:]
        gT = ct[1:3]
        gq = zt
        mh = moT[:].rearrange("p (j c) -> p j c", j=4)
        sq = sb("sq", [P, P])
        ssq = sb("ssq", [P, 4])
        m_hn = zt[0][:].rearrange("p (j c) -> p j c", j=4)
        mhT = e_hT
        gb = tg
        gt = sg
        ga = ya
        mlT = moT

        names = """
            setup_chain const_loaded attn_w_loaded weights_loaded setup_weights setup_pool setup_dve setup_act setup_dve2 x_loaded0
            x_loaded1 x_free0 x_free1 out_stored a_link a_link_dve a_u a_var a_rstd a_hn a_cT a_rope
            a_high a_mid a_low a_shift a_pv a_osb a_proj a_u1 a_filled a_freed0 a_freed1 a_freed2 a_pad e_link e_head_link e_var
            e_rstd e_hn e_pick e_tanh e_down e_moT e_x w_filled w_freed0 w_freed1 w_freed2 m_link m_var m_rstd m_u
            m_conv m_ctanh m_xs m_BC m_ztanh m_dtexpin m_dtexp m_a m_MV m_Xw m_Lg m_Ce m_Y m_yd m_gT m_gq
            m_var2 m_rstd2 m_mh m_ssq m_var3 m_rstd3 m_hn m_gtanh m_ga m_mlp m_mlT m_x
        """.split()
        s = {n: ctx.enter_context(nc.semaphore(n)) for n in names}
        a_freed = [s[f"a_freed{k}"] for k in range(SLOTS)]
        w_freed = [s[f"w_freed{k}"] for k in range(SLOTS)]
        x_loaded, x_free = [s["x_loaded0"], s["x_loaded1"]], [s["x_free0"], s["x_free1"]]
        WB = 4 * NE + 2 * NM
        PAIRS = NB // 2
        block = ctx.enter_context(nc.Block())

        def used(eng, freed, lap, steps, fill=None):
            for slot in range(SLOTS):
                counts = [t // SLOTS + 2 for t in steps if t % SLOTS == slot]
                if fill is not None and fill % SLOTS == slot:
                    counts.append(fill // SLOTS + 1)
                if counts:
                    eng.wait_ge(freed[slot], lap + max(counts))

        def a_used(eng, n, *tasks, fill=None):
            used(eng, a_freed, n * A_LAP, [A_STEP[task] for task in tasks], fill)

        def w_used(eng, lap, *steps, fill=None):
            used(eng, w_freed, lap, steps, fill)

        def copy_stacks(copy, task, ring):
            src = ring[:].bitcast(BF16).rearrange("p (h t) -> p h t", h=2)
            side, quarter = divmod(task[1], 4) if task[0] == "qkT" else (0, task[1])
            heads = slice(2 * quarter, 2 * quarter + 2)
            if side == 0:
                copy(stq[0][0:STACK, heads, :], src[0:STACK])
                return copy(stq[1][STACK:P, heads, :], src[STACK:P])
            return copy(stkT[:, heads, :], src)

        loads = [(ident, A["consts"][:, 0:P]), (upto, A["consts"][:, P:2 * P]), (after, A["consts"][:, 2 * P:3 * P]),
                 (cos, A["consts"][:, 3 * P:3 * P + 4 * HD].rearrange("p (j d) -> p j d", d=HD)),
                 (sin, A["consts"][:, 3 * P + 4 * HD:3 * P + 8 * HD].rearrange("p (j d) -> p j d", d=HD)),
                 (vec, A["packed"])]
        wloads = [(wv, A["wv"].rearrange("e c n -> c e n")),
                  (ep, A["ep"].rearrange("e (k f) c -> f e k c", f=P)), (W_in, A["W_in"]),
                  (W_out, A["W_out"].rearrange("(k f) c -> f k c", f=P)), (w1, A["w1"]),
                  (w2, A["w2"].rearrange("(k f) c -> f k c", f=P))]

        @block.sync
        def _(sp):
            for dst, src in loads:
                sp.dma_start(dst[:], src).then_inc(s["const_loaded"], 16)
            def load(i, k):
                sp.dma_start(x0[k][:], x_v[bass.ds(2 * i + k, 1)].rearrange("b p j c -> p (b j) c")).then_inc(x_loaded[k], 16)

            def store(i, k):
                sp.wait_ge(s["e_x"], 4 * i + 3 + k)
                sp.dma_start(out_v[bass.ds(2 * i + k, 1)].rearrange("b p j c -> p (b j) c"), x3[:]).then_inc(s["out_stored"], 16)

            sp.sem_inc(s["out_stored"], 16)
            load(0, 0)
            sp.dma_start(attn_w[:], A["attn_w"]).then_inc(s["attn_w_loaded"], 16)
            sp.dma_start(proj_w[:], A["proj_w"]).then_inc(s["attn_w_loaded"], 16)
            for dst, src in wloads:
                sp.dma_start(dst[:], src).then_inc(s["weights_loaded"], 16)
            load(0, 1)
            with sp.Fori(0, PAIRS - 1) as i:
                for k in range(2):
                    sp.wait_ge(x_free[k], i + 1)
                    load(i + 1, k)
                for k in range(2):
                    store(i, k)
            for k in range(2):
                store(PAIRS - 1, k)
            sp.wait_ge(s["out_stored"], 16 * (NB + 1))

        @block.tensor
        def _(pe):
            def transpose4(dst, src, ind):
                for j in range(4):
                    last = pe.transpose(dst(j), src(j), ind)
                return last

            def attention(n):
                def blocks(k, a):
                    if k < 2:
                        return [(k, a, 0, 0, 512)]
                    if k < 4:
                        return [(k - 2, a, 1, 0, 384), (k - 2, a, 3, 384, 128)]
                    return [(q, a, 2, 256 * q, 256) for q in range(2)]

                def pv(x):
                    g, k = divmod(x, EXPS)
                    a_used(pe, n, ("exp", g, k))
                    if k == 0 and g > 0:
                        pe.wait_ge(s["a_osb"], n * GROUPS + g)
                    for q, a, kb, c, w in blocks(k // 2, k % 2):
                        hl = 2 * q + a
                        last = pe.matmul(obank[32 * hl:32 * hl + 32, 512 - w:512], vx[:, kb, GROUP * g + hl, :],
                                         probs[k][:, c:c + w], start=(k < 4), stop=(k >= 8), skip_group_check=True)
                    last.then_inc(s["a_pv"], 1)

                def both_heads(j, hp, side):
                    return stk[side][:, 16 * j + 2 * hp:16 * j + 2 * hp + 2, :].rearrange("p h k -> p (h k)")

                x = 0
                for t, task in A_TASKS:
                    kind = task[0]
                    if kind == "none":
                        pe.wait_ge(s["a_filled"], n * NA + t)
                        a_used(pe, n, fill=t)
                        pe.sem_inc(s["a_filled"], 1)
                        yield
                        continue
                    if t is None:
                        if kind == "proj":
                            a_used(pe, n, ("yT",))
                            for j in range(4):
                                last = pe.matmul(obank[:, j * P:(j + 1) * P], yT[:, j * P:(j + 1) * P], proj_w[:], start=True, stop=True)
                            last.then_inc(s["a_proj"], 1)
                        elif kind == "pv_last":
                            for k in range(GROUPS * EXPS - PV_LAG, GROUPS * EXPS):
                                pv(k)
                        yield
                        continue
                    ring = aring[t % SLOTS]
                    rb16 = ring[:].bitcast(BF16)
                    reads = {("max", 0, 3, 0): [("qkT", i) for i in range(8)], ("yT",): [("back", GROUPS - 1)]}.get(task, [])
                    if kind == "exp" and task[2] == 0:
                        reads = [("shift", task[1])]
                    a_used(pe, n, *reads, fill=t)
                    if kind == "hT":
                        pe.wait_ge(s["a_hn"], n + 1)
                        last = transpose4(lambda j: ring[:, j * P:(j + 1) * P], lambda j: hn[:, j, :], ident[:])
                    elif kind == "qkv":
                        j = task[1]
                        if j == 0:
                            pe.wait_ge(s["a_cT"], n + 1)
                            pe.wait_ge(s["attn_w_loaded"], 32)
                        last = pe.matmul(ring[:, 0:3 * P], cT[:, j * P:(j + 1) * P], attn_w[:], start=True, stop=True)
                    elif kind == "qkT":
                        side, quarter = divmod(task[1], 4)
                        pe.wait_ge(s["a_low"], 2 * n + side + 1)
                        for b in range(2):
                            last = transpose4(lambda j: rb16[:, b * 512 + j * P:b * 512 + (j + 1) * P],
                                              lambda j: both_heads(j, 2 * quarter + b, side), identb[:])
                    elif kind == "max":
                        _, g, j, k = task
                        w = P * (j + 1)
                        heads = [divmod(k, 2)] if j >= 2 else [(q, k) for q in range(2)] if j == 1 else [divmod(h, 2) for h in range(4)]
                        for c, (q, a) in enumerate(heads):
                            hp = 2 * g + q
                            pe.matmul(ring[:, c * w:(c + 1) * w], stq[a][:, hp, j * P:(j + 1) * P], stkT[:, hp, 0:w],
                                      start=True, stop=False)
                            last = pe.matmul(ring[:, (c + 1) * w - P:(c + 1) * w], identb[:], neg_keys[:], start=False, stop=True)
                    elif kind == "shift":
                        g = task[1]
                        pe.wait_ge(s["a_shift"], n * GROUPS + g + 1)
                        for b in range(2):
                            last = transpose4(lambda j: rb16[:, b * 512 + j * P:b * 512 + (j + 1) * P],
                                              lambda j: both_heads(j, 2 * g + b, 0), identb[:])
                    elif kind == "exp":
                        _, g, k = task
                        for q, a, kb, c, w in blocks(k // 2, k % 2):
                            hp = 2 * g + q
                            pe.matmul(ring[:, c:c + w], stkT[:, hp, kb * P:(kb + 1) * P], stq[a][:, hp, T - w:T],
                                      start=True, stop=False)
                            last = pe.matmul(ring[:, c:c + P], identb[:], neg_queries[:], start=False, stop=True)
                    elif kind == "back":
                        g = task[1]
                        pe.wait_ge(s["a_osb"], n * GROUPS + g + 1)
                        last = transpose4(lambda j: ring[:, j * P:(j + 1) * P], lambda j: osb[:, j * P:(j + 1) * P], ident[:])
                    elif kind == "yT":
                        last = transpose4(lambda j: ring[:, j * P:(j + 1) * P], lambda j: y[:, j, :], ident[:])
                    last.then_inc(s["a_filled"], 1)
                    if kind == "exp":
                        if x >= PV_LAG:
                            pv(x - PV_LAG)
                        x += 1
                    yield

            def experts(n, base, lap):
                def down(e, c):
                    k = 4 * e + c
                    w_used(pe, lap, E_STEP["value", e, c])
                    pe.matmul(acc[:], ep[:, e, c, :], ya[k % 2][:], start=(k == 0), stop=(k == 15)).then_inc(s["e_down"], 1)

                for t, task in E_TASKS:
                    kind = task[0]
                    if kind == "last_down":
                        down(3, 3)
                        yield
                        continue
                    if kind == "none":
                        pe.wait_ge(s["w_filled"], base + t)
                        pe.wait_ge(w_freed[t % SLOTS], lap + t // SLOTS + 1)
                        pe.sem_inc(s["w_filled"], 1)
                        yield
                        continue
                    ring = wring[t % SLOTS]
                    reads = []
                    if kind == "logits":
                        reads = [E_STEP["hT",]]
                    elif kind == "gate" and task[2] == 0:
                        reads = [E_STEP["mask", task[1]]]
                    w_used(pe, lap, *reads, fill=t)
                    if kind == "hT":
                        pe.wait_ge(s["e_hn"], n + 1)
                        last = transpose4(lambda j: ring[:, j * P:(j + 1) * P], lambda j: e_hn[:, j, :], ident[:])
                    elif kind == "logits":
                        for j in range(4):
                            last = pe.matmul(ring[:, EXPERTS * j:EXPERTS * (j + 1)], e_hT[:, j * P:(j + 1) * P], v("router", 0, EXPERTS),
                                             start=True, stop=True)
                    elif kind == "mask":
                        e = task[1]
                        if e == 0:
                            pe.wait_ge(s["e_pick"], n + 1)
                        for j in range(4):
                            last = pe.matmul(ring[:, j * P:(j + 1) * P], pick[:, j, e:e + 1].to_broadcast([P, P]), identb[:],
                                             start=True, stop=True)
                    elif kind in ("gate", "value"):
                        _, e, c = task
                        o = (DFF if kind == "value" else 0) + c * P
                        last = pe.matmul(ring[:], wv[:, e, o:o + P], hm[e % 2][:], start=True, stop=True)
                    elif kind == "back":
                        pe.wait_ge(s["e_moT"], n + 1)
                        last = transpose4(lambda j: ring[:, j * P:(j + 1) * P], lambda j: moT[:, j * P:(j + 1) * P], ident[:])
                    last.then_inc(s["w_filled"], 1)
                    if kind == "value" and 4 * e + c >= 1:
                        down(*divmod(4 * e + c - 1, 4))
                    yield

            def mamba(i, base, lap):
                def chunk(ring, w, src, n0, m=P):
                    return pe.matmul(ring, w[:, n0:n0 + m], src[:], start=True, stop=True)

                def mlp_down(c):
                    pe.wait_ge(s["m_ga"], 4 * i + c + 1)
                    pe.matmul(acc[:], w2[:, c, :], ga[c % 2][:], start=(c == 0), stop=(c == 3)).then_inc(s["m_mlp"], 1)

                for t, task in M_TASKS:
                    kind = task[0]
                    if kind == "none":
                        pe.wait_ge(s["w_filled"], base + t)
                        pe.wait_ge(w_freed[t % SLOTS], lap + t // SLOTS + 1)
                        pe.sem_inc(s["w_filled"], 1)
                        yield
                        continue
                    if t is None:
                        if kind == "Y":
                            _, c, j = task
                            if c == 0:
                                pe.wait_ge(s["m_Lg"], 4 * i + j + 1)
                                if j == 0:
                                    w_used(pe, lap, M_STEP["xsT", 1])
                                else:
                                    pe.wait_ge(s["m_Ce"], 3 * i + j)
                                    w_used(pe, lap, M_STEP["state", j - 1])
                            elif j == 0:
                                pe.wait_ge(s["m_yd"], 2 * i + 1)
                            for a in range(2):
                                h = 2 * c + a
                                dst = acc[MP * a:MP * a + MP, j * P:(j + 1) * P]
                                last = pe.matmul(dst, Xd[:, j, h, :], Ld[:, j, h, :], start=True, stop=(j == 0), skip_group_check=True)
                                if j > 0:
                                    last = pe.matmul(dst, St[:, j, h, :], Ed[:, j, h, :], start=False, stop=True, skip_group_check=True)
                            if j == 3:
                                last.then_inc(s["m_Y"], 1)
                        elif kind == "last_down":
                            mlp_down(3)
                        yield
                        continue
                    ring = wring[t % SLOTS]
                    reads = {"xbc": [M_STEP["uT",]], "up": [M_STEP["hT",]]}.get(kind, [])
                    if task == ("state", 0):
                        reads = [M_STEP["BT",]]
                    w_used(pe, lap, *reads, fill=t)
                    if kind == "uT":
                        pe.wait_ge(s["m_u"], i + 1)
                        last = transpose4(lambda j: ring[:, j * P:(j + 1) * P], lambda j: mu[:, j, :], ident[:])
                    elif kind == "xbc":
                        last = chunk(ring[:], W_in, uT, DIN + task[1] * P)
                    elif kind == "z":
                        last = chunk(ring[:], W_in, uT, task[1] * P)
                    elif kind == "dt":
                        for j in range(4):
                            last = pe.matmul(ring[:, MH * j:MH * (j + 1)], uT[:, j * P:(j + 1) * P], W_in[:, 2 * DIN + 2 * NS:],
                                             start=True, stop=True)
                    elif kind == "sums":
                        pe.wait_ge(s["m_a"], i + 1)
                        av = sm["a"][:].rearrange("p j h -> p (j h)")
                        pe.matmul(ring[:, 0:16], after[:], av, start=True, stop=True)
                        last = pe.matmul(ring[:, 16:32], ones[:], av, start=True, stop=True)
                    elif kind == "xsT":
                        c = task[1]
                        pe.wait_ge(s["m_xs"], 2 * i + c + 1)
                        last = transpose4(lambda j: ring[:, j * P:(j + 1) * P], lambda j: xs[c][:, j * P:(j + 1) * P], ident[:])
                    elif kind == "BT":
                        pe.wait_ge(s["m_BC"], 2 * i + 1)
                        for j in range(4):
                            last = pe.matmul(ring[:, j * NS:(j + 1) * NS], BT[:, j * P:(j + 1) * P], ident[0:NS, 0:NS], start=True, stop=True)
                    elif kind == "G":
                        pe.wait_ge(s["m_BC"], 2 * i + 2)
                        for j in range(4):
                            last = pe.matmul(ring[:, j * P:(j + 1) * P], BT[:, j * P:(j + 1) * P], CT[:, j * P:(j + 1) * P], start=True, stop=True)
                    elif kind == "decay":
                        j = task[1]
                        pe.wait_ge(s["m_MV"], 4 * i + j + 1)
                        last = pe.matmul(ring[:], after[:], MV[:, j].rearrange("p h t -> p (h t)"), start=True, stop=True)
                    elif kind == "head_decay":
                        j = task[1]
                        last = pe.matmul(ring[0:NS, :], ones[:, 0:NS], MV[:, j].rearrange("p h t -> p (h t)"), start=True, stop=True)
                    elif kind == "state":
                        j = task[1]
                        if j == 0:
                            pe.wait_ge(s["m_Xw"], i + 1)
                        last = pe.matmul(ring[0:NS, 0:MH * MP], Bt[:, j, :], Xw[:, j].rearrange("p h d -> p (h d)"), start=True, stop=True)
                    elif kind == "sumsq":
                        pe.wait_ge(s["m_gq"], 2 * i + 2)
                        for j in range(4):
                            for c in range(2):
                                last = pe.matmul(ring[:, j:j + 1], gq[c][:, j * P:(j + 1) * P], ones[:, 0:1], start=(c == 0), stop=(c == 1))
                    elif kind == "out":
                        for j in range(4):
                            for c in range(2):
                                last = pe.matmul(ring[:, j * P:(j + 1) * P], gT[c][:, j * P:(j + 1) * P], W_out[:, c, :], start=(c == 0), stop=(c == 1))
                    elif kind == "hT":
                        pe.wait_ge(s["m_hn"], i + 1)
                        last = transpose4(lambda j: ring[:, j * P:(j + 1) * P], lambda j: m_hn[:, j, :], ident[:])
                    elif kind == "up":
                        last = chunk(ring[:], w1, mhT, task[1] * P)
                    elif kind == "back":
                        pe.wait_ge(s["m_mlT"], i + 1)
                        last = transpose4(lambda j: ring[:, j * P:(j + 1) * P], lambda j: mlT[:, j * P:(j + 1) * P], ident[:])
                    last.then_inc(s["w_filled"], 1)
                    if kind == "up" and task[1] > 0:
                        mlp_down(task[1] - 1)
                    yield

            pe.wait_ge(s["const_loaded"], 16 * len(loads))
            pe.wait_ge(s["setup_dve2"], 1)
            schedule(PAIRS, pe.Fori,
                     lambda i, k: attention(4 * i + k), lambda i, k: attention(4 * i + 2 + k),
                     lambda i, k: experts(4 * i + k, i * WB + E1_AT[k], i * W_LAP + E1_AT[k] // SLOTS),
                     lambda i, k: experts(4 * i + 2 + k, i * WB + E2_AT[k], i * W_LAP + E2_AT[k] // SLOTS),
                     lambda i, k: mamba(2 * i + k, i * WB + M_AT[k], i * W_LAP + M_AT[k] // SLOTS),
                     lambda: pe.wait_ge(s["setup_weights"], 1))

        @block.scalar
        def _(act):
            def copy(dst, src):
                return act.activation(dst, src, ACT.Copy)

            def attention(n):
                def copy_out(g):
                    act.wait_ge(s["a_pv"], (n * GROUPS + g + 1) * EXPS)
                    if g > 0:
                        a_used(act, n, ("back", g - 1))
                    copy(osb[:], obank[:]).then_inc(s["a_osb"], 1)

                def high():
                    for side in range(2):
                        st = stk[side][:, :, 0:MROW].rearrange("p h (k d) -> p h k d", d=HD)
                        hi = st[:, :, 0:3, :] if side == 0 else st[:, :, 2:5, :]
                        if side == 0:
                            act.wait_ge(s["a_rope"], 4 * n + 4)
                            act.wait_ge(s["a_pad"], n + 1)
                        copy(hi, rqk[side].unsqueeze(2).to_broadcast([P, 64, 3, HD])).then_inc(s["a_high"], 1)

                def middle():
                    for side in range(2):
                        st = stk[side][:, :, 0:MROW].rearrange("p h (k d) -> p h k d", d=HD)
                        md = st[:, :, 3:6:2, :] if side == 0 else st[:, :, 1:6:4, :]
                        act.wait_ge(s["a_mid"], 2 * n + side + 1)
                        copy(md, mid[side].unsqueeze(2).to_broadcast([P, 64, 2, HD])).then_inc(s["a_link"], 1)

                x = 0
                for t, task in A_TASKS:
                    kind = task[0]
                    if t is not None:
                        ring = aring[t % SLOTS]
                    if kind == "hT":
                        act.wait_ge(s["a_filled"], n * NA + t + 1)
                        act.activation(hT[:, 2:], ring[:], ACT.Identity, scale=v("ln1_w"), bias=v("ln1_b")).then_inc(a_freed[t % SLOTS], 1)
                    elif kind == "high":
                        high()
                    elif kind == "mid":
                        middle()
                    elif kind == "shift" or (kind == "qkT" and task[1] % 2 == 0):
                        act.wait_ge(s["a_filled"], n * NA + t + 1)
                        copy_stacks(copy, task, ring).then_inc(a_freed[t % SLOTS], 1)
                    elif kind == "exp":
                        act.wait_ge(s["a_filled"], n * NA + t + 1)
                        if x >= EXPS:
                            act.wait_ge(s["a_pv"], n * GROUPS * EXPS + x - EXPS + 1)
                        act.activation(probs[x % EXPS], ring[:], ACT.Exp, scale=float(HD) ** -0.5).then_inc(a_freed[t % SLOTS], 1)
                        if x % EXPS == PV_LAG - 1 and x > EXPS:
                            copy_out(x // EXPS - 1)
                        x += 1
                    elif kind == "pv_last":
                        copy_out(GROUPS - 1)
                    elif kind == "yT":
                        act.wait_ge(s["a_filled"], n * NA + t + 1)
                        copy(yT[:], ring[:]).then_inc(a_freed[t % SLOTS], 1)
                    elif kind == "none":
                        act.wait_ge(s["a_filled"], n * NA + t + 1)
                        act.sem_inc(a_freed[t % SLOTS], 1)
                    yield

            def experts(n, base, lap):
                for t, task in E_TASKS:
                    kind = task[0]
                    if t is not None:
                        ring = wring[t % SLOTS]
                    if kind == "hT":
                        act.wait_ge(s["w_filled"], base + t + 1)
                        act.activation(e_hT[:], ring[:], ACT.Identity, scale=v("ln2_w"), bias=v("ln2_b")).then_inc(w_freed[t % SLOTS], 1)
                    elif kind == "gate":
                        _, e, c = task
                        k = 4 * e + c
                        act.wait_ge(s["w_filled"], base + t + 1)
                        if k >= 2:
                            w_used(act, lap, E_STEP[("gate",) + divmod(k - 2, 4)])
                        act.activation(tg[k % 2][:], ring[:], ACT.Tanh).then_inc(s["e_tanh"], 1)
                    elif kind == "last_down":
                        act.wait_ge(s["e_down"], n * 16 + 16)
                        copy(moT[:], acc[:]).then_inc(s["e_moT"], 1)
                    elif kind == "none":
                        act.wait_ge(s["w_filled"], base + t + 1)
                        act.sem_inc(w_freed[t % SLOTS], 1)
                    yield

            def mamba(i, base, lap):
                for t, task in M_TASKS:
                    kind = task[0]
                    if t is not None:
                        ring = wring[t % SLOTS]
                    if kind in ("uT", "xbc", "z", "sums", "BT", "decay", "head_decay", "hT", "up", "none"):
                        act.wait_ge(s["w_filled"], base + t + 1)
                    if kind == "uT":
                        copy(uT[:], ring[:]).then_inc(w_freed[t % SLOTS], 1)
                    elif kind == "xbc":
                        c = task[1]
                        copy(cpad[c][:, 3:], ring[:])
                        act.activation(cacc[c], ring[:], ACT.Identity, scale=v("mconv", TAPS * c + TAPS - 1), bias=v("mconv_b", c)).then_inc(w_freed[t % SLOTS], 1)
                    elif kind == "z":
                        act.activation(zt[task[1]][:], ring[:], ACT.Tanh).then_inc(s["m_ztanh"], 1)
                        if task[1] == 0:
                            act.wait_ge(s["m_dtexpin"], i + 1)
                            act.activation(sm["e"][:], sm["n"][:], ACT.Exp).then_inc(s["m_dtexp"], 1)
                    elif kind in ("conv", "step_size") and task != ("conv", 2):
                        k, c = {("conv", 0): (0, 2), ("conv", 1): (1, 0), ("step_size",): (2, 1)}[task]
                        act.wait_ge(s["m_conv"], 3 * i + k + 1)
                        act.activation(ct[c][:], cacc[c][:], ACT.Tanh).then_inc(s["m_ctanh"], 1)
                    elif kind == "sums":
                        act.activation(edec[:].rearrange("p a j h -> p (a j h)"), ring[:, 0:32], ACT.Exp).then_inc(w_freed[t % SLOTS], 1)
                    elif kind == "BT":
                        copy(Bt[:].rearrange("p j n -> p (j n)"), ring[:, 0:4 * NS]).then_inc(w_freed[t % SLOTS], 1)
                    elif kind == "decay":
                        j = task[1]
                        act.activation(Ld[:, j].rearrange("p h t -> p (h t)"), ring[:], ACT.Exp).then_inc(w_freed[t % SLOTS], 1)
                    elif kind == "head_decay":
                        j = task[1]
                        act.activation(Ed[:, j].rearrange("p h t -> p (h t)"), ring[0:NS, :], ACT.Exp).then_inc(w_freed[t % SLOTS], 1)
                    elif kind == "Y" and task[2] == 3:
                        c = task[1]
                        act.wait_ge(s["m_gT"], 2 * i + c + 1)
                        act.activation(gq[c][:], gT[c][:], ACT.Square).then_inc(s["m_gq"], 1)
                    elif kind == "out":
                        for j in range(4):
                            act.wait_ge(s["m_mh"], 4 * i + j + 1)
                            if j > 0:
                                act.wait_ge(s["m_ssq"], 4 * i + j)
                            act.activation(sq[:], mh[:, j, :], ACT.Square, accum_out=ssq[:, j:j + 1]).then_inc(s["m_ssq"], 1)
                    elif kind == "hT":
                        copy(mhT[:], ring[:]).then_inc(w_freed[t % SLOTS], 1)
                    elif kind == "up":
                        c = task[1]
                        if c >= 2:
                            act.wait_ge(s["m_ga"], 4 * i + c - 1)
                        act.activation(gb[c % 2][:], ring[:], ACT.Identity, bias=v("b1", c)).then_inc(w_freed[t % SLOTS], 1)
                        w_used(act, lap, t)
                        act.activation(gt[c % 2][:], gb[c % 2][:], ACT.Tanh).then_inc(s["m_gtanh"], 1)
                    elif kind == "last_down":
                        act.wait_ge(s["m_mlp"], 4 * i + 4)
                        act.activation(mlT[:], acc[:], ACT.Identity, bias=v("b2")).then_inc(s["m_mlT"], 1)
                    elif kind == "none":
                        act.sem_inc(w_freed[t % SLOTS], 1)
                    yield

            act.wait_ge(s["const_loaded"], 16 * len(loads))
            act.wait_ge(s["setup_dve"], 1)
            act.activation(negA[:], negA[:], ACT.Exp).then_inc(s["setup_act"], 1)
            act.wait_ge(s["setup_dve2"], 1)
            for k in range(SLOTS):
                act.sem_inc(a_freed[k], 1)
                act.sem_inc(w_freed[k], 1)
            schedule(PAIRS, act.Fori,
                     lambda i, k: attention(4 * i + k), lambda i, k: attention(4 * i + 2 + k),
                     lambda i, k: experts(4 * i + k, i * WB + E1_AT[k], i * W_LAP + E1_AT[k] // SLOTS),
                     lambda i, k: experts(4 * i + 2 + k, i * WB + E2_AT[k], i * W_LAP + E2_AT[k] // SLOTS),
                     lambda i, k: mamba(2 * i + k, i * WB + M_AT[k], i * W_LAP + M_AT[k] // SLOTS))

        @block.gpsimd
        def _(pool):
            def rsqrt(dst, src, ready, count, done):
                pool.wait_ge(ready, count)
                w = dst.shape[1]
                pool.tensor_tensor(dst[:], src[:], half[:, 0:w], ALU.pow).then_inc(done, 1)

            def attention(n):
                for _, task in A_TASKS:
                    kind = task[0]
                    if kind == "stats":
                        rsqrt(a_r, a_pw, s["a_var"], n + 1, s["a_rstd"])
                        pool.memset(stk[1][:, :, MROW:MROW + 3], 1.0)
                        pool.memset(stk[1][:, :, MROW + 3:], 0.0)
                        pool.memset(stk[0][:, :, MROW:MROW + 3], 0.0).then_inc(s["a_pad"], 1)
                    elif kind == "e_stats":
                        rsqrt(e_r, e_pw, s["e_var"], n + 1, s["e_rstd"])
                    yield

            def experts(n):
                for _ in E_TASKS:
                    yield

            def mamba(i, lap):
                for t, task in M_TASKS:
                    kind = task[0]
                    if kind == "stats":
                        rsqrt(m_r, m_pw, s["m_var"], i + 1, s["m_rstd"])
                    elif kind == "sums":
                        pool.wait_ge(s["m_a"], i + 1)
                        for j in range(4):
                            pool.tensor_tensor(MV[:, j], upto[:].unsqueeze(1).to_broadcast([P, MH, P]),
                                               sm["a"][:, j, :].unsqueeze(2).to_broadcast([P, MH, P]), ALU.mult).then_inc(s["m_MV"], 1)
                    elif kind == "xsT" and task[1] == 1:
                        w_used(pool, lap, M_STEP["sums",], M_STEP["xsT", 0], M_STEP["xsT", 1])
                        pool.tensor_tensor(Xw.rearrange("p j h d -> p (j h) d"), Xd.rearrange("p j h d -> p (j h) d"),
                                           edec[:, 0].rearrange("p j h -> p (j h)").unsqueeze(2).to_broadcast([P, 16, MP]), ALU.mult).then_inc(s["m_Xw"], 1)
                    elif kind == "decay":
                        j = task[1]
                        w_used(pool, lap, M_STEP["G",], t)
                        pool.tensor_tensor(Ld[:, j], Ld[:, j], Gm[:, j].unsqueeze(1).to_broadcast([P, MH, P]), ALU.mult).then_inc(s["m_Lg"], 1)
                    elif kind == "head_decay":
                        j = task[1]
                        w_used(pool, lap, t)
                        pool.tensor_tensor(Ed[:, j], Ed[:, j], CT[:, j * P:(j + 1) * P].unsqueeze(1).to_broadcast([NS, MH, P]), ALU.mult).then_inc(s["m_Ce"], 1)
                    elif kind == "sumsq":
                        rsqrt(m_r, m_pw, s["m_var2"], i + 1, s["m_rstd2"])
                    elif kind == "mh_var":
                        rsqrt(m_r, m_pw, s["m_var3"], i + 1, s["m_rstd3"])
                    yield

            pool.memset(half[:], -0.5).then_inc(s["setup_pool"], 1)
            pool.memset(ones[:], 1.0).then_inc(s["setup_pool"], 1)
            for e in range(EXPERTS):
                pool.memset(tie[:, e:e + 1], float(EXPERTS - e)).then_inc(s["setup_pool"], 1)
            pool.memset(hT[:, 0:2], 0.0).then_inc(s["setup_pool"], 1)
            for c in range(3):
                pool.memset(cpad[c][:, 0:3], 0.0).then_inc(s["setup_pool"], 1)
            pool.memset(vx[:, :, :, HD:HD + 1], 1.0).then_inc(s["setup_pool"], 1)
            pool.memset(vx[:, :, :, HD + 1:], 0.0).then_inc(s["setup_pool"], 1)
            pool.memset(stk[0][:, :, MROW:], 0.0).then_inc(s["setup_pool"], 1)
            pool.wait_ge(s["setup_pool"], 13)
            schedule(PAIRS, pool.Fori,
                     lambda i, k: attention(4 * i + k), lambda i, k: attention(4 * i + 2 + k),
                     lambda i, k: experts(4 * i + k), lambda i, k: experts(4 * i + 2 + k), lambda i, k: mamba(2 * i + k, i * W_LAP + M_AT[k] // SLOTS))

        @block.vector
        def _(dve):
            links = [0, 0, 0]
            seen = {}

            def linker(sem, per, n):
                count = [0]

                def link(ins):
                    count[0] += 1
                    ins.then_inc(sem, 1)
                    dve.wait_ge(sem, n * per + count[0])
                return link, count

            def statistics(link, src, st, mv):
                for j in range(4):
                    last = dve.bn_stats(st[:, j, :], src[:, j, :])
                link(last)
                dve.memset(pause[:], 0.0)
                for j in range(4):
                    last = dve.bn_aggr(mv[:, j, :], st[:, j, :])
                link(last)

            def attention(n, src, src_ready, src_count, u1):
                link, count = linker(s["a_link_dve"], A_LINKS, n)
                head_link, head_count = linker(s["e_head_link"], H_LINKS, n)
                dve.wait_ge(src_ready, src_count)
                statistics(link, src, a_st, a_mv)
                var, mean = a_mv[:, :, 1], a_mv[:, :, 0]
                link(dve.tensor_scalar(a_pw[:, 0:4], var, EPS, None, ALU.add))
                link(dve.reciprocal(a_rc[:], a_pw[:, 0:4]))
                link(dve.tensor_tensor(a_pw[:, 4:8], var, a_rc[:], ALU.mult))
                dve.tensor_scalar(a_pw[:, 4:8], a_pw[:, 4:8], EPS, None, ALU.add).then_inc(s["a_var"], 1)
                yield
                dve.wait_ge(s["a_rstd"], n + 1)
                link(dve.tensor_tensor(a_rc[:], a_r[:, 0:4], a_r[:, 4:8], ALU.mult))
                for j in range(4):
                    last = dve.tensor_scalar(hn[:, j, :], src[:, j, :], a_mv[:, j, 0:1], a_rc[:, j:j + 1], ALU.subtract, ALU.mult)
                last.then_inc(s["a_hn"], 1)
                yield
                for t, task in A_TASKS[2:]:
                    kind = task[0]
                    if t is not None:
                        ring, filled = aring[t % SLOTS], n * NA + t + 1
                    if kind == "hT":
                        a_used(dve, n, task)
                        link(dve.tensor_scalar(cT[:], hT[:, 0:T], v("aconv", 0), None, ALU.mult))
                        link(dve.scalar_tensor_tensor(out=cT[:], in0=hT[:, 1:T + 1], scalar=v("aconv", 1), in1=cT[:], op0=ALU.mult, op1=ALU.add))
                        dve.scalar_tensor_tensor(out=cT[:], in0=hT[:, 2:T + 2], scalar=v("aconv", 2), in1=cT[:], op0=ALU.mult, op1=ALU.add).then_inc(s["a_cT"], 1)
                    elif kind == "qkv":
                        dve.wait_ge(s["a_filled"], filled)
                        j = task[1]
                        qk = ring[:, 0:2 * P].rearrange("p (h d) -> p h d", d=HD)
                        hf = HD // 2
                        if j > 0:
                            dve.wait_ge(s["a_rope"], 4 * n + j)
                        dve.tensor_tensor(ra[:], qk, cos[:, j, :].unsqueeze(1).to_broadcast([P, 32, HD]), ALU.mult)
                        dve.tensor_tensor(rb[:, :, 0:hf], qk[:, :, hf:], sin[:, j, 0:hf].unsqueeze(1).to_broadcast([P, 32, hf]), ALU.mult)
                        dve.tensor_tensor(rb[:, :, hf:], qk[:, :, 0:hf], sin[:, j, hf:].unsqueeze(1).to_broadcast([P, 32, hf]), ALU.mult)
                        dve.tensor_copy(vx[:, j, :, 0:HD], ring[:, 2 * P:3 * P].rearrange("p (h d) -> p h d", d=HD)).then_inc(a_freed[t % SLOTS], 1)
                        a_used(dve, n, task)
                        dve.tensor_tensor(rqk[0][:, 16 * j:16 * j + 16, :], ra[:, 0:16, :], rb[:, 0:16, :], ALU.add)
                        dve.tensor_tensor(rqk[1][:, 16 * j:16 * j + 16, :], ra[:, 16:32, :], rb[:, 16:32, :], ALU.add).then_inc(s["a_rope"], 1)
                    elif kind == "qkT" and task[1] % 2:
                        dve.wait_ge(s["a_filled"], filled)
                        copy_stacks(dve.tensor_copy, task, ring).then_inc(a_freed[t % SLOTS], 1)
                    elif kind == "high":
                        for j in range(4):
                            last = dve.tensor_scalar(u[:, j, :], src[:, j, :], a_mv[:, j, 0:1], a_r[:, j:j + 1], ALU.subtract, ALU.mult)
                        last.then_inc(s["a_u"], 1)
                    elif kind == "mid":
                        dve.wait_ge(s["a_rope"], 4 * n + 4)
                        for side in range(2):
                            dve.wait_ge(s["a_high"], 2 * n + side + 1)
                            hi = stk[side][:, :, 2 * HD:3 * HD]
                            dve.tensor_tensor(mid[side], rqk[side], hi, ALU.subtract).then_inc(s["a_mid"], 1)
                    elif kind == "low":
                        for side in range(2):
                            dve.wait_ge(s["a_link"], 2 * n + side + 1)
                            dve.wait_ge(s["a_mid"], 2 * n + side + 1)
                            lo, md = (stk[0][:, :, 4 * HD:5 * HD], stk[0][:, :, 3 * HD:4 * HD]) if side == 0 else \
                                (stk[1][:, :, 0:HD], stk[1][:, :, HD:2 * HD])
                            dve.tensor_tensor(lo, mid[side], md, ALU.subtract).then_inc(s["a_low"], 1)
                    elif kind == "max":
                        _, g, j, k = task
                        w = P * (j + 1)
                        dve.wait_ge(s["a_filled"], filled)
                        h0 = GROUP * g
                        if j >= 2:
                            src_ap, dst = ring[:, 0:w], mx[:, j, h0 + k:h0 + k + 1]
                        elif j == 1:
                            src_ap, dst = ring[:, 0:2 * w].rearrange("p (q w) -> p q w", w=w), mx[:, j, h0 + k:h0 + k + 3:2]
                        else:
                            src_ap, dst = ring[:].rearrange("p (h w) -> p h w", w=w), mx[:, j, h0:h0 + 4]
                        dve.tensor_reduce(dst, src_ap, AX_X, ALU.max).then_inc(a_freed[t % SLOTS], 1)
                        if j == 0:
                            a_used(dve, n, task, ("max", g, 1, 0), ("max", g, 1, 1))
                            rows = stk[0][:].rearrange("p (j h) k -> p j h k", j=4)[:, :, h0:h0 + GROUP, :]
                            hi, md, lo = (rows[:, :, :, MROW + k] for k in range(3))
                            m_g, t_g = mx[:, :, h0:h0 + GROUP], mt[:, :, h0:h0 + GROUP]
                            link(dve.tensor_scalar(hi, m_g, -1.0, None, ALU.mult))
                            link(dve.tensor_scalar(t_g, m_g, -1.0, None, ALU.mult))
                            link(dve.tensor_tensor(t_g, t_g, hi, ALU.subtract))
                            link(dve.tensor_copy(md, t_g))
                            dve.tensor_tensor(lo, t_g, md, ALU.subtract).then_inc(s["a_shift"], 1)
                    elif kind == "back":
                        g = task[1]
                        dve.wait_ge(s["a_filled"], filled)
                        o = ring[:].rearrange("p (j h k) -> p j h k", j=4, k=32)
                        link(dve.reciprocal(rden[:], o[:, :, :, HD]))
                        for j in range(4):
                            last = dve.tensor_tensor(y[:, j, 32 * g:32 * g + 32].rearrange("p (h d) -> p h d", d=HD), o[:, j, :, 0:HD],
                                                     rden[:, j, :].unsqueeze(2).to_broadcast([P, GROUP, HD]), ALU.mult)
                        last.then_inc(a_freed[t % SLOTS], 1)
                    elif kind == "proj":
                        dve.wait_ge(s["a_proj"], n + 1)
                        dve.wait_ge(s["a_u"], n + 1)
                        dve.tensor_tensor(u1[:], u[:], obank[:].rearrange("p (j c) -> p j c", j=4), ALU.add).then_inc(s["a_u1"], 1)
                        assert count[0] == A_LINKS, count
                    elif kind == "e_stats":
                        dve.wait_ge(s["a_u1"], n + 1)
                        statistics(head_link, u1, e_st, e_mv)
                        assert head_count[0] == H_LINKS, head_count
                        dve.tensor_scalar(e_pw[:], e_mv[:, :, 1], EPS, None, ALU.add).then_inc(s["e_var"], 1)
                    elif kind == "e_norm":
                        dve.wait_ge(s["e_rstd"], n + 1)
                        for j in range(4):
                            last = dve.tensor_scalar(e_hn[:, j, :], u1[:, j, :], e_mv[:, j, 0:1], e_r[:, j:j + 1], ALU.subtract, ALU.mult)
                        last.then_inc(s["e_hn"], 1)
                    yield

            def experts(n, base, lap, u1, src, dst, result):
                link, count = linker(s["e_link"], E_LINKS, n)

                for t, task in E_TASKS:
                    kind = task[0]
                    if t is not None:
                        ring = wring[t % SLOTS]
                    if kind in ("logits", "mask", "back"):
                        dve.wait_ge(s["w_filled"], base + t + 1)
                    if kind == "logits":
                        lg = ring[:, 0:4 * EXPERTS].rearrange("p (j e) -> p j e", e=EXPERTS)
                        link(dve.tensor_reduce(lmax[:], lg, AX_X, ALU.max))
                        link(dve.tensor_tensor(lsel[:], lg, lmax[:].unsqueeze(2).to_broadcast([P, 4, EXPERTS]), ALU.is_equal))
                        dve.sem_inc(w_freed[t % SLOTS], 1)
                        link(dve.tensor_tensor(lsel[:], lsel[:], tie[:].unsqueeze(1).to_broadcast([P, 4, EXPERTS]), ALU.mult))
                        link(dve.tensor_reduce(lmax[:], lsel[:], AX_X, ALU.max))
                        dve.tensor_tensor(pick[:], lsel[:], lmax[:].unsqueeze(2).to_broadcast([P, 4, EXPERTS]), ALU.is_equal).then_inc(s["e_pick"], 1)
                    elif kind == "mask":
                        e = task[1]
                        w_used(dve, lap, E_STEP["hT",])
                        dve.tensor_tensor(hm[e % 2][:], e_hT[:], ring[:], ALU.mult).then_inc(w_freed[t % SLOTS], 1)
                    elif kind == "value":
                        _, e, c = task
                        k = 4 * e + c
                        gate = E_STEP["gate", e, c]
                        dve.wait_ge(s["e_tanh"], n * 16 + k + 1)
                        dve.scalar_tensor_tensor(out=sg[k % 2][:], in0=tg[k % 2][:], scalar=1.0, in1=wring[gate % SLOTS][:], op0=ALU.add,
                                                 op1=ALU.mult).then_inc(w_freed[gate % SLOTS], 1)
                        if k >= 2:
                            dve.wait_ge(s["e_down"], n * 16 + k - 1)
                        w_used(dve, lap, gate)
                        dve.wait_ge(s["w_filled"], base + t + 1)
                        dve.tensor_tensor(ya[k % 2][:], sg[k % 2][:], ring[:], ALU.mult).then_inc(w_freed[t % SLOTS], 1)
                    elif kind == "back":
                        link(dve.tensor_tensor(tmp[:], u1[:], ring[:].rearrange("p (j c) -> p j c", j=4), ALU.add))
                        dve.sem_inc(w_freed[t % SLOTS], 1)
                        if result is not None:
                            dve.wait_ge(s["out_stored"], 16 * result + 16)
                        dve.scalar_tensor_tensor(out=dst[:].rearrange("p j c -> p (j c)"), in0=tmp[:].rearrange("p j c -> p (j c)"), scalar=0.5,
                                                 in1=src[:].rearrange("p j c -> p (j c)"), op0=ALU.mult, op1=ALU.add).then_inc(s["e_x"], 1)
                        dve.wait_ge(s["e_x"], n + 1)
                        if result is None:
                            dve.sem_inc(x_free[x0.index(src)], 1)
                        assert count[0] == E_LINKS, count
                    yield

            def mamba(i, base, lap, x1, x2):
                link, count = linker(s["m_link"], M_LINKS, i)

                statistics(link, x1, m_st, m_mv)
                dve.tensor_scalar(m_pw[:], m_mv[:, :, 1], EPS, None, ALU.add).then_inc(s["m_var"], 1)
                yield
                dve.wait_ge(s["m_rstd"], i + 1)
                for j in range(4):
                    last = dve.tensor_scalar(mu[:, j, :], x1[:, j, :], m_mv[:, j, 0:1], m_r[:, j:j + 1], ALU.subtract, ALU.mult)
                last.then_inc(s["m_u"], 1)
                yield

                def convolve(c):
                    w_used(dve, lap, M_STEP["xbc", c])
                    for q in range(TAPS - 1):
                        ins = dve.scalar_tensor_tensor(out=cacc[c][:], in0=cpad[c][:, q:q + T], scalar=v("mconv", TAPS * c + q), in1=cacc[c][:],
                                                       op0=ALU.mult, op1=ALU.add)
                        if q < TAPS - 2:
                            link(ins)
                    ins.then_inc(s["m_conv"], 1)

                def silu(dst, th, h):
                    return dve.scalar_tensor_tensor(out=dst, in0=th, scalar=1.0, in1=h, op0=ALU.add, op1=ALU.mult)

                def step_size():
                    S = {k: sm[k][:] for k in sm}
                    flat = {k: sm[k][:].rearrange("p j h -> p (j h)") for k in sm}
                    dve.wait_ge(s["m_dtexp"], i + 1)
                    link(dve.tensor_scalar(S["d"], S["e"], 2.0, None, ALU.add))
                    link(dve.reciprocal(S["r"], S["d"]))
                    link(dve.tensor_tensor(S["z"], S["e"], S["r"], ALU.mult))
                    link(dve.tensor_tensor(S["z2"], S["z"], S["z"], ALU.mult))
                    link(dve.tensor_scalar(S["p"], S["z2"], 1.0 / (2 * ATANH_TERMS - 1), None, ALU.mult))
                    for k in range(ATANH_TERMS - 2, 0, -1):
                        link(dve.scalar_tensor_tensor(out=flat["p"], in0=flat["p"], scalar=1.0 / (2 * k + 1), in1=flat["z2"], op0=ALU.add, op1=ALU.mult))
                    link(dve.scalar_tensor_tensor(out=flat["q"], in0=flat["p"], scalar=1.0, in1=flat["z"], op0=ALU.add, op1=ALU.mult))
                    link(dve.tensor_scalar(S["w"], S["x"], 0.0, None, ALU.max))
                    link(dve.scalar_tensor_tensor(out=flat["dt"], in0=flat["q"], scalar=2.0, in1=flat["w"], op0=ALU.mult, op1=ALU.add))
                    link(dve.tensor_tensor(S["w"], S["dt"], negA[:].unsqueeze(1).to_broadcast([P, 4, MH]), ALU.mult))
                    dve.tensor_scalar(S["a"], S["w"], -1000.0, None, ALU.max).then_inc(s["m_a"], 1)

                for t, task in M_TASKS[2:]:
                    kind = task[0]
                    if t is not None:
                        ring = wring[t % SLOTS]
                    if kind == "Y" and task[2] == 3:
                        c = task[1]
                        if c == 1:
                            dve.wait_ge(s["m_gT"], 2 * i + 1)
                        dve.wait_ge(s["m_Y"], 2 * i + c + 1)
                        dve.scalar_tensor_tensor(out=yd[:], in0=xs[c][:], scalar=v("D", c), in1=acc[:], op0=ALU.mult, op1=ALU.add).then_inc(s["m_yd"], 1)
                        dve.wait_ge(s["m_yd"], 2 * i + c + 1)
                        dve.tensor_tensor(gT[c][:], yd[:], zs[c][:], ALU.mult).then_inc(s["m_gT"], 1)
                    if kind in ("dt", "z", "xsT", "G", "state", "sumsq", "out", "back"):
                        dve.wait_ge(s["w_filled"], base + t + 1)
                    if kind == "dt":
                        link(dve.tensor_tensor(sm["x"][:], ring[:, 0:4 * MH].rearrange("p (j h) -> p j h", h=MH),
                                               v("dt_bias", 0, MH).unsqueeze(1).to_broadcast([P, 4, MH]), ALU.add))
                        dve.sem_inc(w_freed[t % SLOTS], 1)
                        fx = sm["x"][:].rearrange("p j h -> p (j h)")
                        dve.scalar_tensor_tensor(out=sm["n"][:].rearrange("p j h -> p (j h)"), in0=fx, scalar=-1.0, in1=fx,
                                                 op0=ALU.mult, op1=ALU.min).then_inc(s["m_dtexpin"], 1)
                    elif kind == "z":
                        c = task[1]
                        dve.wait_ge(s["m_ztanh"], 2 * i + c + 1)
                        silu(zs[c][:], zt[c][:], ring[:]).then_inc(w_freed[t % SLOTS], 1)
                    elif kind == "conv":
                        convolve(task[1])
                    elif kind == "step_size":
                        step_size()
                    elif kind == "BC":
                        dve.wait_ge(s["m_ctanh"], 3 * i + 1)
                        silu(BT[:], ct[2][0:NS, :], cacc[2][0:NS, :]).then_inc(s["m_BC"], 1)
                        silu(CT[:], ct[2][NS:P, :], cacc[2][NS:P, :]).then_inc(s["m_BC"], 1)
                    elif kind == "xs":
                        c = task[1]
                        dve.wait_ge(s["m_ctanh"], 3 * i + c + 2)
                        silu(xs[c][:], ct[c][:], cacc[c][:]).then_inc(s["m_xs"], 1)
                    elif kind == "xsT":
                        c = task[1]
                        r4 = ring[:].rearrange("p (j a d) -> p j a d", j=4, a=2)
                        for j in range(4):
                            last = dve.tensor_tensor(Xd[:, j, 2 * c:2 * c + 2, :], r4[:, j], sm["dt"][:, j, 2 * c:2 * c + 2].unsqueeze(2).to_broadcast([P, 2, MP]), ALU.mult)
                        last.then_inc(w_freed[t % SLOTS], 1)
                    elif kind == "G":
                        dve.tensor_tensor(Gm[:], ring[:].rearrange("p (j t) -> p j t", j=4), upto[:].unsqueeze(1).to_broadcast([P, 4, P]), ALU.mult).then_inc(w_freed[t % SLOTS], 1)
                    elif kind == "state":
                        j = task[1]
                        new = ring[0:NS, 0:MH * MP].rearrange("p (h d) -> p h d", d=MP)
                        if j == 0:
                            dve.tensor_copy(St[:, 1], new).then_inc(w_freed[t % SLOTS], 1)
                        else:
                            w_used(dve, lap, M_STEP["sums",], t - 1)
                            link(dve.tensor_tensor(St[:, 0], St[:, j], edec[0:NS, 1, j, :].unsqueeze(2).to_broadcast([NS, MH, MP]), ALU.mult))
                            dve.tensor_tensor(St[:, j + 1], St[:, 0], new, ALU.add).then_inc(w_freed[t % SLOTS], 1)
                    elif kind == "sumsq":
                        link(dve.tensor_scalar(m_pw[:], ring[:, 0:4], 1.0 / DIN, EPS, ALU.mult, ALU.add))
                        dve.sem_inc(w_freed[t % SLOTS], 1)
                        dve.sem_inc(s["m_var2"], 1)
                    elif kind == "out":
                        dve.wait_ge(s["m_rstd2"], i + 1)
                        for j in range(4):
                            dve.scalar_tensor_tensor(out=mh[:, j, :], in0=ring[:, j * P:(j + 1) * P], scalar=m_r[:, j:j + 1], in1=mu[:, j, :],
                                                     op0=ALU.mult, op1=ALU.add).then_inc(s["m_mh"], 1)
                        dve.wait_ge(s["m_mh"], 4 * i + 4)
                        dve.sem_inc(w_freed[t % SLOTS], 1)
                    elif kind == "mh_var":
                        dve.wait_ge(s["m_ssq"], 4 * i + 4)
                        dve.tensor_scalar(m_pw[:], ssq[:], 1.0 / P, EPS, ALU.mult, ALU.add).then_inc(s["m_var3"], 1)
                    elif kind == "mh_norm":
                        dve.wait_ge(s["m_rstd3"], i + 1)
                        for j in range(4):
                            last = dve.tensor_scalar(m_hn[:, j, :], mh[:, j, :], m_r[:, j:j + 1], None, ALU.mult)
                        last.then_inc(s["m_hn"], 1)
                        link(dve.tensor_tensor(tmp[:], mh[:], x1[:], ALU.add))
                    elif kind == "up":
                        c = task[1]
                        dve.wait_ge(s["m_gtanh"], 4 * i + c + 1)
                        if c >= 2:
                            dve.wait_ge(s["m_mlp"], 4 * i + c - 1)
                        silu(ga[c % 2][:], gt[c % 2][:], gb[c % 2][:]).then_inc(s["m_ga"], 1)
                    elif kind == "back":
                        dve.tensor_tensor(x2[:], tmp[:], ring[:].rearrange("p (j c) -> p j c", j=4), ALU.add).then_inc(s["m_x"], 1)
                        dve.wait_ge(s["m_x"], i + 1)
                        dve.sem_inc(w_freed[t % SLOTS], 1)
                        assert count[0] == M_LINKS, count
                    yield

            sc = 0

            def step(ins):
                nonlocal sc
                sc += 1
                ins.then_inc(s["setup_chain"], 1)

            dve.wait_ge(s["const_loaded"], 16 * len(loads))
            dve.tensor_scalar(negA[:], v("A_log", 0, MH), 88.0, None, ALU.min).then_inc(s["setup_dve"], 1)
            step(dve.tensor_copy(identb[:], ident[:]))
            step(dve.tensor_scalar(neg_keys[:], after[:], 0.0, None, ALU.mult))
            step(dve.tensor_scalar(neg_queries[:], after[:], NEG, None, ALU.mult))
            step(dve.tensor_scalar(v("mconv", 0, 12), v("mconv", 0, 12), 0.5, None, ALU.mult))
            step(dve.tensor_scalar(v("mconv_b", 0, 3), v("mconv_b", 0, 3), 0.5, None, ALU.mult))
            step(dve.tensor_scalar(v("b1", 0, 4), v("b1", 0, 4), 0.5, None, ALU.mult))
            dve.wait_ge(s["setup_chain"], 6)
            step(dve.memset(stq[0][STACK:P], 0.0))
            step(dve.memset(stq[1][0:STACK], 0.0))
            step(dve.tensor_tensor(tmp[:, 0, :], upto[:], ident[:], ALU.subtract))
            dve.wait_ge(s["setup_chain"], 9)
            step(dve.tensor_scalar(neg_keys[:], tmp[:, 0, :], NEG, None, ALU.mult))
            dve.wait_ge(s["setup_act"], 1)
            step(dve.tensor_scalar(negA[:], negA[:], -1.0, None, ALU.mult))
            dve.wait_ge(s["setup_chain"], sc)
            dve.wait_ge(s["setup_pool"], 13)
            dve.sem_inc(s["setup_dve2"], 1)

            def weights():
                dve.wait_ge(s["weights_loaded"], 16 * len(wloads))
                for e in range(EXPERTS):
                    step(dve.tensor_scalar(wv[:, e, 0:DFF], wv[:, e, 0:DFF], 0.5, None, ALU.mult))
                step(dve.tensor_scalar(W_in[:, 0:DIN], W_in[:, 0:DIN], 0.5, None, ALU.mult))
                step(dve.tensor_scalar(w1[:], w1[:], v("rms_w"), 0.5, ALU.mult, ALU.mult))
                for c in range(2):
                    step(dve.tensor_scalar(W_out[:, c, :], W_out[:, c, :], v("norm_w", c), None, ALU.mult))
                dve.wait_ge(s["setup_chain"], sc)
                dve.sem_inc(s["setup_weights"], 1)

            schedule(PAIRS, dve.Fori,
                     lambda i, k: attention(4 * i + k, x0[k], x_loaded[k], 16 * i + 16, u1[k]),
                     lambda i, k: attention(4 * i + 2 + k, x2[k], s["m_x"], 2 * i + k + 1, u1[k]),
                     lambda i, k: experts(4 * i + k, i * WB + E1_AT[k], i * W_LAP + E1_AT[k] // SLOTS, u1[k], x0[k], x1[k], None),
                     lambda i, k: experts(4 * i + 2 + k, i * WB + E2_AT[k], i * W_LAP + E2_AT[k] // SLOTS, u1[k], x2[k], x3, 2 * i + k),
                     lambda i, k: mamba(2 * i + k, i * WB + M_AT[k], i * W_LAP + M_AT[k] // SLOTS, x1[k], x2[k]), weights)


_WEIGHTS = {"attn_w": "L0_ffn_attn_w", "proj_w": "L0_ffn_proj_w", "wv": "L0_ffn_expert_wv", "ep": "L0_ffn_expert_proj",
            "W_in": "L0_attn_W_in", "W_out": "L0_attn_W_out", "w1": "L0_attn_mlp_w1", "w2": "L0_attn_mlp_w2"}


def packed_vectors(inputs):
    import numpy as np

    def get(name):
        return np.asarray(inputs[name])

    def rows(a):
        return np.broadcast_to(a[None, :], (P, a.shape[0]))

    cols = {
        "ln1_w": get("L0_ffn_ln1_w")[:, None], "ln1_b": get("L0_ffn_ln1_b")[:, None],
        "ln2_w": get("L0_ffn_ln2_w")[:, None], "ln2_b": get("L0_ffn_ln2_b")[:, None],
        "aconv": get("L0_ffn_conv_w")[:, 0, :], "router": get("L0_ffn_router_w"),
        "mconv": get("L0_attn_conv_w").reshape(3, P, TAPS).transpose(1, 0, 2).reshape(P, 3 * TAPS),
        "mconv_b": get("L0_attn_conv_b").reshape(3, P).T,
        "dt_bias": rows(get("L0_attn_dt_bias")), "A_log": rows(get("L0_attn_A_log")),
        "D": np.repeat(get("L0_attn_D_param"), MP).reshape(2, P).T,
        "norm_w": get("L0_attn_norm_w").reshape(2, P).T, "rms_w": get("L0_attn_rms_w")[:, None],
        "b1": get("L0_attn_mlp_b1").reshape(4, P).T, "b2": get("L0_attn_mlp_b2")[:, None],
    }
    return np.ascontiguousarray(np.concatenate([cols[name] for name in PACK], axis=1))


def shape_constants(T):
    import numpy as np
    r = np.arange(P)
    upto = (r[:, None] <= r[None, :]).astype(np.float32)
    after = (r[:, None] > r[None, :]).astype(np.float32)
    inv = (np.float32(1.0) / np.float32(10000.0) ** (np.arange(0, HD, 2, dtype=np.float32) / np.float32(HD))).astype(np.float32)
    ang = np.arange(T, dtype=np.float32)[:, None] * inv[None, :]
    ang = np.concatenate([ang, ang], axis=1)
    sign = np.where(np.arange(HD) < HD // 2, np.float32(-1), np.float32(1))
    cos = np.cos(ang).astype(np.float32).reshape(T // P, P, HD).transpose(1, 0, 2).reshape(P, -1)
    sin = (np.sin(ang) * sign).astype(np.float32).reshape(T // P, P, HD).transpose(1, 0, 2).reshape(P, -1)
    return np.ascontiguousarray(np.concatenate([np.eye(P, dtype=np.float32), upto, after, cos, sin], axis=1))


def kernel(**inputs):
    import numpy as np
    import concourse.bacc as bacc
    from concourse.bass_utils import run_bass_kernel_spmd

    x = np.ascontiguousarray(inputs["L0_attn_hidden_tokens"])
    host = {"x": x, "packed": packed_vectors(inputs), "consts": shape_constants(x.shape[1])}
    host.update({k: np.ascontiguousarray(inputs[n]) for k, n in _WEIGHTS.items()})
    nc = bacc.Bacc("TRN2", target_bir_lowering=False, num_devices=1)
    A = {k: nc.dram_tensor(f"in_{k}", a.shape, F32, kind="ExternalInput").ap() for k, a in host.items()}
    A["out"] = nc.dram_tensor("out_x", x.shape, F32, kind="ExternalOutput").ap()
    build_program(nc, A)
    r = run_bass_kernel_spmd(nc, [{f"in_{k}": a for k, a in host.items()}], core_ids=[0])
    return r.results[0]["out_x"]
```

```python
import concourse.bass as bass
from concourse import mybir
from contextlib import ExitStack

F32 = mybir.dt.float32
BF16 = mybir.dt.bfloat16
ALU = mybir.AluOpType
ACT = mybir.ActivationFunctionType
AX_X = mybir.AxisListType.X

P = 128
EPS = 1e-5
HEADS, HD = 16, 8
GROUP = 4
GROUPS = HEADS // GROUP
STACK = 64
NPROD = 6
EXPS = 10
PRODUCTS = (((0, 1, 2, 3), 6), ((4, 5, 6, 7), EXPS), ((8, 9), EXPS + 2))
MROW = NPROD * HD
NEG = -1e30
EXPERTS, DFF = 4, 512
MH, MP, NS, TAPS = 4, 64, 64, 4
DIN = MH * MP
MLP = 512
ATANH_TERMS = 8

PACK = {}
_at = 0
for _name, _w in (("ln1_w", 1), ("ln1_b", 1), ("ln2_w", 1), ("ln2_b", 1), ("aconv", 3), ("router", EXPERTS),
                  ("mconv", 3 * TAPS), ("mconv_b", 3), ("dt_bias", MH), ("A_log", MH), ("D", 2),
                  ("norm_w", 2), ("rms_w", 1), ("b1", 4), ("b2", 1)):
    PACK[_name] = (_at, _w)
    _at += _w
PACKED = _at


NO_FILL = ("stats", "norm", "high", "mid", "low", "pv_last", "proj", "e_stats", "e_norm", "last_down",
           "conv", "step_size", "BC", "xs", "Y0", "mh_var", "mh_norm")



def attention_steps():
    def maxima(g):
        return ([("max", g, j, h) for j in (3, 2) for h in range(GROUP)] + [("max", g, 1, a) for a in range(2)]
                + [("max", g, 0, 0)])
    steps = [("stats",), ("norm",), ("hT",)] + [("qkv", j) for j in range(4)] + [("high",), ("mid",), ("low",)]
    steps += [("qkT", i) for i in range(8)] + maxima(0)
    for g in range(GROUPS):
        nxt = maxima(g + 1) if g + 1 < GROUPS else [None] * 11
        seq = nxt[:3] + [("shift", g), nxt[3]]
        for x in range(EXPS):
            seq += [("exp", g, x), ("back", g - 1) if g and x == EXPS - 5 else None] + nxt[4 + x:5 + x]
        steps += [t for t in seq if t]
    return steps + [("pv_last",), ("back", GROUPS - 1), ("yT",), ("proj",), ("e_stats",), ("e_norm",), ("e_hT",), ("logits",)]


def expert_steps():
    steps = [("mask", 0)]
    for e in range(EXPERTS):
        for c in range(DFF // P):
            steps += [("gate", e, c), ("value", e, c)]
            if c == 1 and e + 1 < EXPERTS:
                steps.append(("mask", e + 1))
    return steps + [("last_down",), ("back",)]


def mamba_steps():
    return ([("stats",), ("norm",), ("uT",), ("xbc", 2), ("xbc", 0), ("dt",), ("conv", 2), ("xbc", 1), ("z", 0), ("conv", 0),
             ("z", 1), ("conv", 1), ("step_size",), ("BC",), ("sums",), ("xs", 0), ("xs", 1), ("xsT", 0), ("xsT", 1), ("BT",), ("G",)]
            + [("decay", j) for j in range(4)] + [("state", j) for j in range(3)] + [("head_decay", j) for j in range(1, 4)]
            + [("Y0", j) for j in range(4)] + [("Y1",)]
            + [("sumsq",), ("out",), ("mh_var",), ("mh_norm",), ("hT",)] + [("up", c) for c in range(4)]
            + [("last_down",), ("back",)])


SLOTS = 3


def numbered(steps):
    fills, out = 0, []
    for step in steps:
        out.append((None if step[0] in NO_FILL else fills, step))
        fills += step[0] not in NO_FILL
    return out, fills, {step: t for t, step in out if t is not None}


A_TASKS, NA, A_STEP = numbered(attention_steps())
E_TASKS, NE, E_STEP = numbered(expert_steps())
M_TASKS, NM, M_STEP = numbered(mamba_steps())
PAIR_FILLS = 4 * NE + 2 * NM
assert NA % SLOTS == 0 and PAIR_FILLS % SLOTS == 0
A_LAP, W_LAP = NA // SLOTS, PAIR_FILLS // SLOTS

A_LINKS, H_LINKS, P_LINKS, E_LINKS, M_LINKS = 28, 2, 4, 1, 27


E1_AT = [0, NE + NM]
M_AT = [NE, 2 * NE + NM]
E2_AT = [2 * NE + 2 * NM, 3 * NE + 2 * NM]


TURNS = (
    "0010010010011002001010120123301203011104431000022b4600030030320140133330203310511211100100"
    "100100110011010101201232112111111044301000220a50212203133102031325120332311121110010010010"
    "111010101100311333342113e3ogm100010010111010101012120330322303i3ni"
)


def alone(stage):
    for _ in stage:
        pass


def schedule(pairs, loop, A1, A2, E1, E2, M, weights=lambda: None):
    a, e, m = len(A_TASKS), len(E_TASKS), len(M_TASKS)

    def pair(i, last):
        attentions = [A1(i, 1), A2(i, 0), A2(i, 1)] + ([] if last else [A1(i + 1, 0)])
        others = [E1(i, 0), M(i, 0), E1(i, 1), M(i, 1), E2(i, 0), E2(i, 1)]
        lanes = [(step for stage in stages for step in stage) for stages in (attentions, others)]
        after = {(0, a): e + m - 1, (1, e + m): a - 1,
                 (0, 2 * a): 2 * (e + m) - 1,
                 (1, 2 * (e + m)): 2 * a - 1, (1, 2 * (e + m) + e): 3 * a - 1,
                 (0, 4 * a - 5): 2 * (e + m) + e - 1}
        order = [k for turn in TURNS for k in [0] * int(turn, 36) + [1]] + [0] * (4 * a)
        at, steps = [0, 0], (len(attentions) * a, 4 * e + 2 * m)
        for k in order:
            if at[k] < steps[k]:
                assert at[1 - k] > after.get((k, at[k]), -1)
                next(lanes[k])
                at[k] += 1
        assert all(next(lane, None) is None for lane in lanes)

    alone(A1(0, 0))
    weights()
    with loop(0, pairs - 1) as i:
        pair(i, False)
    pair(pairs - 1, True)


def build_program(nc, A):
    NB, T, C = A["x"].shape
    NT = T // P
    assert C == P and NT == 4
    x_v = A["x"].rearrange("b (j p) c -> b p j c", p=P)
    out_v = A["out"].rearrange("b (j p) c -> b p j c", p=P)

    with ExitStack() as ctx:
        def sb(name, shape, dt=F32):
            return ctx.enter_context(nc.sbuf_tensor(name, shape, dt))

        def pb(name, shape, dt=F32):
            return ctx.enter_context(nc.psum_tensor(name, shape, dt))

        aring = [pb(f"aring{i}", [P, 512]) for i in range(SLOTS)]
        obank = pb("obank", [P, 512])
        wring = [pb(f"wring{i}", [P, 512]) for i in range(SLOTS)]
        acc = pb("acc", [P, 512])

        ident = sb("ident", [P, P])
        identb = sb("identb", [P, P], BF16)
        upto = sb("upto", [P, P])
        after = sb("after", [P, P])
        ones = sb("ones", [P, P])
        neg_keys = sb("neg_keys", [P, P], BF16)
        neg_queries = sb("neg_queries", [P, P], BF16)
        cos = sb("cos", [P, 4, HD])
        sin = sb("sin", [P, 4, HD])
        vec = sb("vec", [P, PACKED])
        attn_w = sb("attn_w", [P, 3 * P])
        proj_w = sb("proj_w", [P, P])
        wv = sb("wv", [P, EXPERTS, 2 * DFF])
        ep = sb("ep", [P, EXPERTS, 4, P])
        W_in = sb("W_in", [P, 2 * DIN + 2 * NS + MH])
        W_out = sb("W_out", [P, 2, P])
        w1 = sb("w1", [P, MLP])
        w2 = sb("w2", [P, 4, P])
        negA = sb("negA", [P, MH])
        tie = sb("tie", [P, EXPERTS])
        pause = sb("pause", [P, 1])
        pool_pause = sb("pool_pause", [P, 1])
        half = sb("half", [P, 8])

        def v(name, k=0, n=1):
            a = PACK[name][0] + k
            return vec[:, a:a + n]

        x0 = [sb(f"x0_{k}", [P, 4, P]) for k in range(2)]
        x1 = [sb(f"x1_{k}", [P, 4, P]) for k in range(2)]
        x2 = [sb(f"x2_{k}", [P, 4, P]) for k in range(2)]
        x3 = sb("x3", [P, 4, P])
        a_st = sb("a_st", [P, 4, 6])
        a_mv = sb("a_mv", [P, 4, 2])
        a_pw = sb("a_pw", [P, 8])
        a_r = sb("a_r", [P, 8])
        a_rc = sb("a_rc", [P, 4])
        u = sb("u", [P, 4, P])
        hn = sb("hn", [P, 4, P])
        hT = sb("hT", [P, 2 + T])
        cT = sb("cT", [P, T])
        ra = sb("ra", [P, 32, HD])
        rb = sb("rb", [P, 32, HD])
        prob_mem = sb("prob_mem", [P, 5, 1024])
        probs = [prob_mem[:, i // 2, (i % 2) * 512:(i % 2 + 1) * 512] for i in range(EXPS)]
        stk = [sb("stk_q", [P, 64, STACK], BF16)[:],
               prob_mem[:, 0:2].bitcast(BF16).rearrange("p a (h k) -> p (a h) k", k=STACK)]
        stq = [sb(f"stq{a}", [P, 8, T], BF16) for a in range(2)]
        stkT = sb("stkT", [P, 8, T], BF16)
        rqk = [probs[6 + k].rearrange("p (h d) -> p h d", d=HD) for k in range(2)]
        mid = [probs[8 + k].rearrange("p (h d) -> p h d", d=HD) for k in range(2)]
        vx = sb("vx", [P, 4, HEADS, 32])
        mx = sb("mx", [P, 4, HEADS])
        mt = sb("mt", [P, 4, HEADS])
        osb = sb("osb", [P, T])
        rden = sb("rden", [P, 4, GROUP])
        y = hn
        yT = cT
        u1 = [sb(f"u1_{k}", [P, 4, P]) for k in range(2)]
        e_st = sb("e_st", [P, 4, 6])
        e_mv = sb("e_mv", [P, 4, 2])
        e_pw = sb("e_pw", [P, 4])
        e_r = sb("e_r", [P, 4])
        e_hn = u
        e_hT = [sb(f"e_hT{k}", [P, T]) for k in range(2)]
        lmax = sb("lmax", [P, 4])
        lsel = sb("lsel", [P, 4, EXPERTS])
        pick = [sb(f"pick{k}", [P, 4, EXPERTS], BF16) for k in range(2)]
        scratch = [sb(f"scratch{i}", [P, 4, T]) for i in range(2)]
        hm = [scratch[0][:, i] for i in range(2)]
        ya = [scratch[0][:, 2 + i] for i in range(2)]
        tg = [scratch[1][:, i] for i in range(2)]
        sg = [scratch[1][:, 2 + i] for i in range(2)]
        moT = sb("moT", [P, T])
        tmp = sb("tmp", [P, 4, P])
        m_st = sb("m_st", [P, 4, 6])
        m_mv = sb("m_mv", [P, 4, 2])
        m_pw = sb("m_pw", [P, 4])
        m_r = sb("m_r", [P, 4])
        mu = sb("mu", [P, 4, P])
        uT = sb("uT", [P, T])
        cpad = [sb(f"cpad{i}", [P, 3 + T]) for i in range(3)]
        conv = sb("conv", [P, 6, T])
        cacc = [conv[:, i] for i in range(3)]
        ct = [conv[:, 3 + i] for i in range(3)]
        xs = [sb(f"xs{i}", [P, T]) for i in range(2)]
        BT = sb("BT", [NS, T])
        CT = sb("CT", [NS, T])
        zt = [sb(f"zt{i}", [P, T]) for i in range(2)]
        zs = [sb(f"zs{i}", [P, T]) for i in range(2)]
        sm = {k: sb("sm_" + k, [P, 4, MH]) for k in ("x", "n", "e", "d", "r", "z", "z2", "p", "q", "w", "dt", "a")}
        edec = sb("edec", [P, 2, 4, MH])
        MV = scratch[0][:].rearrange("p j (h t) -> p j h t", h=MH)
        Ld = conv[:, 0:4].rearrange("p j (h t) -> p j h t", h=MH)
        Ed = sb("Ed", [NS, 4, MH, P])
        Xd = scratch[1][:, 0:2].rearrange("p a (b h d) -> p (a b) h d", b=2, h=MH)
        Xw = scratch[1][:, 2:4].rearrange("p a (b h d) -> p (a b) h d", b=2, h=MH)
        Bt = sb("Bt", [P, 4, NS])
        Gm = sb("Gm", [P, 4, P])
        St = sb("St", [NS, 4, MH, MP])
        gT = ct[1:3]
        gq = zt
        mh = moT[:].rearrange("p (j c) -> p j c", j=4)
        sq = sb("sq", [P, P])
        ssq = sb("ssq", [P, 4])
        m_hn = zt[0][:].rearrange("p (j c) -> p j c", j=4)
        gb = tg
        gt = sg
        ga = ya
        mlT = moT

        names = """
            setup_chain const_loaded attn_w_loaded weights_loaded setup_weights setup_pool
            setup_dve setup_act setup_dve2 x_loaded0 x_loaded1 x_free0 x_free1 out_stored a_link
            a_mid_copied a_u a_var a_rstd a_hn a_cT a_rope a_high a_mid a_low a_shift a_pv a_osb
            a_proj a_u1 a_filled a_freed0 a_freed1 a_freed2 a_pad e_link e_head_link e_pick_link
            e_var e_rstd e_hn e_pick e_tanh e_down e_moT e_x w_filled w_freed0 w_freed1 w_freed2
            m_link m_var m_rstd m_u m_conv m_ctanh m_xs m_BC m_ztanh m_dtexpin m_dtexp m_a m_MV
            m_Xw m_Lg m_Ce m_Y m_yd m_gT m_gq m_var2 m_rstd2 m_mh m_ssq m_var3 m_rstd3 m_hn
            m_gtanh m_ga m_mlp m_mlT m_tmp m_x
        """.split()
        s = {n: ctx.enter_context(nc.semaphore(n)) for n in names}
        a_freed = [s[f"a_freed{k}"] for k in range(SLOTS)]
        w_freed = [s[f"w_freed{k}"] for k in range(SLOTS)]
        x_loaded, x_free = [s["x_loaded0"], s["x_loaded1"]], [s["x_free0"], s["x_free1"]]
        PAIRS = NB // 2
        block = ctx.enter_context(nc.Block())

        def used(eng, freed, lap, steps, fill=None):
            for slot in range(SLOTS):
                counts = [t // SLOTS + 2 for t in steps if t % SLOTS == slot]
                if fill is not None and fill % SLOTS == slot:
                    counts.append(fill // SLOTS + 1)
                if counts:
                    eng.wait_ge(freed[slot], lap + max(counts))

        def a_used(eng, n, *tasks, fill=None):
            used(eng, a_freed, n * A_LAP, [A_STEP[task] for task in tasks], fill)

        def w_used(eng, place, *steps, fill=None):
            pair, at = place
            used(eng, w_freed, pair * W_LAP, [at + t for t in steps], None if fill is None else at + fill)

        def w_slot(place, t):
            pair, at = place
            return wring[(at + t) % SLOTS], w_freed[(at + t) % SLOTS], pair * PAIR_FILLS + at + t + 1

        def copy_stacks(copy, task, ring):
            src = ring[:].bitcast(BF16).rearrange("p (h t) -> p h t", h=2)
            side, quarter = divmod(task[1], 4) if task[0] == "qkT" else (0, task[1])
            heads = slice(2 * quarter, 2 * quarter + 2)
            if side == 0:
                copy(stq[0][0:STACK, heads, :], src[0:STACK])
                return copy(stq[1][STACK:P, heads, :], src[STACK:P])
            return copy(stkT[:, heads, :], src)

        loads = [(ident, A["consts"][:, 0:P]), (upto, A["consts"][:, P:2 * P]), (after, A["consts"][:, 2 * P:3 * P]),
                 (cos, A["consts"][:, 3 * P:3 * P + 4 * HD].rearrange("p (j d) -> p j d", d=HD)),
                 (sin, A["consts"][:, 3 * P + 4 * HD:3 * P + 8 * HD].rearrange("p (j d) -> p j d", d=HD)),
                 (vec, A["packed"])]
        wloads = [(wv, A["wv"].rearrange("e c n -> c e n")),
                  (ep, A["ep"].rearrange("e (k f) c -> f e k c", f=P)), (W_in, A["W_in"]),
                  (W_out, A["W_out"].rearrange("(k f) c -> f k c", f=P)), (w1, A["w1"]),
                  (w2, A["w2"].rearrange("(k f) c -> f k c", f=P))]

        @block.sync
        def _(sp):
            for dst, src in loads:
                sp.dma_start(dst[:], src).then_inc(s["const_loaded"], 16)
            def load(i, k):
                sp.dma_start(x0[k][:], x_v[bass.ds(2 * i + k, 1)].rearrange("b p j c -> p (b j) c")).then_inc(x_loaded[k], 16)

            def store(i, k):
                sp.wait_ge(s["e_x"], 4 * i + 3 + k)
                sp.dma_start(out_v[bass.ds(2 * i + k, 1)].rearrange("b p j c -> p (b j) c"), x3[:]).then_inc(s["out_stored"], 16)

            sp.sem_inc(s["out_stored"], 16)
            load(0, 0)
            sp.dma_start(attn_w[:], A["attn_w"]).then_inc(s["attn_w_loaded"], 16)
            sp.dma_start(proj_w[:], A["proj_w"]).then_inc(s["attn_w_loaded"], 16)
            for dst, src in wloads:
                sp.dma_start(dst[:], src).then_inc(s["weights_loaded"], 16)
            load(0, 1)
            with sp.Fori(0, PAIRS - 1) as i:
                for k in range(2):
                    sp.wait_ge(x_free[k], i + 1)
                    load(i + 1, k)
                for k in range(2):
                    store(i, k)
            for k in range(2):
                store(PAIRS - 1, k)
            sp.wait_ge(s["out_stored"], 16 * (NB + 1))

        @block.tensor
        def _(pe):
            def transpose4(dst, src, ind):
                for j in range(4):
                    last = pe.transpose(dst(j), src(j), ind)
                return last

            def attention(n, par):
                def blocks(k, a):
                    if k < 2:
                        return [(k, a, 0, 0, 512)]
                    if k < 4:
                        return [(k - 2, a, 1, 0, 384), (k - 2, a, 3, 384, 128)]
                    return [(q, a, 2, 256 * q, 256) for q in range(2)]

                def pv(g, part):
                    fills = PRODUCTS[part][0]
                    a_used(pe, n, *[("exp", g, x) for x in fills])
                    if part == 0 and g > 0:
                        pe.wait_ge(s["a_osb"], n * GROUPS + g)
                    parts = [(b, 2 * q + a, x, kb, c, w) for x in fills for b, (q, a, kb, c, w) in enumerate(blocks(x // 2, x % 2))]
                    for b, hl, x, kb, c, w in sorted(parts if part < 2 else [(0,) + q[1:] for q in parts]):
                        last = pe.matmul(obank[32 * hl:32 * hl + 32, 512 - w:512], vx[:, kb, GROUP * g + hl, :],
                                         probs[x][:, c:c + w], start=(part == 0), stop=(part == 2), skip_group_check=True)
                    last.then_inc(s["a_pv"], 1)

                def both_heads(j, hp, side):
                    return stk[side][:, 16 * j + 2 * hp:16 * j + 2 * hp + 2, :].rearrange("p h k -> p (h k)")

                for t, task in A_TASKS:
                    kind = task[0]
                    if t is None:
                        if kind == "proj":
                            a_used(pe, n, ("yT",))
                            for j in range(4):
                                last = pe.matmul(obank[:, j * P:(j + 1) * P], yT[:, j * P:(j + 1) * P], proj_w[:],
                                                 start=True, stop=True)
                            last.then_inc(s["a_proj"], 1)
                        elif kind == "pv_last":
                            pv(GROUPS - 1, 1)
                            pv(GROUPS - 1, 2)
                        yield
                        continue
                    ring = aring[t % SLOTS]
                    rb16 = ring[:].bitcast(BF16)
                    reads = {("max", 0, 3, 0): [("qkT", i) for i in range(8)], ("yT",): [("back", GROUPS - 1)],
                             ("logits",): [("e_hT",)]}.get(task, [])
                    if kind == "exp" and task[2] == 0:
                        reads = [("shift", task[1])]
                    a_used(pe, n, *reads, fill=t)
                    if kind == "hT":
                        pe.wait_ge(s["a_hn"], n + 1)
                        last = transpose4(lambda j: ring[:, j * P:(j + 1) * P], lambda j: hn[:, j, :], ident[:])
                    elif kind == "qkv":
                        j = task[1]
                        if j == 0:
                            pe.wait_ge(s["a_cT"], n + 1)
                            pe.wait_ge(s["attn_w_loaded"], 32)
                        last = pe.matmul(ring[:, 0:3 * P], cT[:, j * P:(j + 1) * P], attn_w[:], start=True, stop=True)
                    elif kind == "qkT":
                        side, quarter = divmod(task[1], 4)
                        pe.wait_ge(s["a_low"], 2 * n + side + 1)
                        for b in range(2):
                            last = transpose4(lambda j: rb16[:, b * 512 + j * P:b * 512 + (j + 1) * P],
                                              lambda j: both_heads(j, 2 * quarter + b, side), identb[:])
                    elif kind == "max":
                        _, g, j, k = task
                        w = P * (j + 1)
                        heads = [divmod(k, 2)] if j >= 2 else [(q, k) for q in range(2)] if j == 1 else [divmod(h, 2) for h in range(4)]
                        for c, (q, a) in enumerate(heads):
                            hp = 2 * g + q
                            pe.matmul(ring[:, c * w:(c + 1) * w], stq[a][:, hp, j * P:(j + 1) * P], stkT[:, hp, 0:w],
                                      start=True, stop=False)
                            last = pe.matmul(ring[:, (c + 1) * w - P:(c + 1) * w], identb[:], neg_keys[:], start=False, stop=True)
                    elif kind == "shift":
                        g = task[1]
                        pe.wait_ge(s["a_shift"], n * GROUPS + g + 1)
                        for b in range(2):
                            last = transpose4(lambda j: rb16[:, b * 512 + j * P:b * 512 + (j + 1) * P],
                                              lambda j: both_heads(j, 2 * g + b, 0), identb[:])
                    elif kind == "exp":
                        _, g, k = task
                        for q, a, kb, c, w in blocks(k // 2, k % 2):
                            hp = 2 * g + q
                            pe.matmul(ring[:, c:c + w], stkT[:, hp, kb * P:(kb + 1) * P], stq[a][:, hp, T - w:T],
                                      start=True, stop=False)
                            last = pe.matmul(ring[:, c:c + P], identb[:], neg_queries[:], start=False, stop=True)
                    elif kind == "back":
                        g = task[1]
                        pe.wait_ge(s["a_osb"], n * GROUPS + g + 1)
                        last = transpose4(lambda j: ring[:, j * P:(j + 1) * P], lambda j: osb[:, j * P:(j + 1) * P], ident[:])
                    elif kind == "yT":
                        last = transpose4(lambda j: ring[:, j * P:(j + 1) * P], lambda j: y[:, j, :], ident[:])
                    elif kind == "e_hT":
                        pe.wait_ge(s["e_hn"], n + 1)
                        last = transpose4(lambda j: ring[:, j * P:(j + 1) * P], lambda j: e_hn[:, j, :], ident[:])
                    elif kind == "logits":
                        for j in range(4):
                            last = pe.matmul(ring[:, EXPERTS * j:EXPERTS * (j + 1)], e_hT[par][:, j * P:(j + 1) * P],
                                             v("router", 0, EXPERTS),
                                             start=True, stop=True)
                    last.then_inc(s["a_filled"], 1)
                    if kind == "exp":
                        for part, (_, fill) in enumerate(PRODUCTS):
                            if fill % EXPS == task[2] and task[1] >= fill // EXPS:
                                pv(task[1] - fill // EXPS, part)
                    yield

            def experts(n, par, place):
                def down(e, c):
                    k = 4 * e + c
                    w_used(pe, place, E_STEP["value", e, c])
                    pe.matmul(acc[:], ep[:, e, c, :], ya[k % 2][:], start=(k == 0), stop=(k == 15)).then_inc(s["e_down"], 1)

                for t, task in E_TASKS:
                    kind = task[0]
                    if kind == "last_down":
                        down(3, 3)
                        yield
                        continue
                    ring, _, _ = w_slot(place, t)
                    reads = []
                    if kind == "gate" and task[2] == 0:
                        reads = [E_STEP["mask", task[1]]]
                    w_used(pe, place, *reads, fill=t)
                    if kind == "mask":
                        e = task[1]
                        if e == 0:
                            pe.wait_ge(s["e_pick"], n + 1)
                        for j in range(4):
                            last = pe.matmul(ring[:, j * P:(j + 1) * P], pick[par][:, j, e:e + 1].to_broadcast([P, P]), identb[:],
                                             start=True, stop=True)
                    elif kind in ("gate", "value"):
                        _, e, c = task
                        o = (DFF if kind == "value" else 0) + c * P
                        last = pe.matmul(ring[:], wv[:, e, o:o + P], hm[e % 2][:], start=True, stop=True)
                    elif kind == "back":
                        pe.wait_ge(s["e_moT"], n + 1)
                        last = transpose4(lambda j: ring[:, j * P:(j + 1) * P], lambda j: moT[:, j * P:(j + 1) * P], ident[:])
                    last.then_inc(s["w_filled"], 1)
                    if kind == "value" and 4 * e + c >= 1:
                        down(*divmod(4 * e + c - 1, 4))
                    yield

            def mamba(i, par, place):
                def chunk(ring, w, src, n0, m=P):
                    return pe.matmul(ring, w[:, n0:n0 + m], src[:], start=True, stop=True)

                def outputs(bank, c, j):
                    for a in range(2):
                        h = 2 * c + a
                        dst = bank[MP * a:MP * a + MP, j * P:(j + 1) * P]
                        last = pe.matmul(dst, Xd[:, j, h, :], Ld[:, j, h, :], start=True, stop=(j == 0), skip_group_check=True)
                        if j > 0:
                            last = pe.matmul(dst, St[:, j, h, :], Ed[:, j, h, :], start=False, stop=True, skip_group_check=True)
                    return last

                def mlp_down(c):
                    pe.wait_ge(s["m_ga"], 4 * i + c + 1)
                    pe.matmul(acc[:], w2[:, c, :], ga[c % 2][:], start=(c == 0), stop=(c == 3)).then_inc(s["m_mlp"], 1)

                for t, task in M_TASKS:
                    kind = task[0]
                    if t is None:
                        if kind == "Y0":
                            j = task[1]
                            pe.wait_ge(s["m_Lg"], 4 * i + j + 1)
                            if j == 0:
                                w_used(pe, place, M_STEP["xsT", 1])
                            else:
                                pe.wait_ge(s["m_Ce"], 3 * i + j)
                                w_used(pe, place, M_STEP["state", j - 1])
                            last = outputs(acc, 0, j)
                            if j == 3:
                                last.then_inc(s["m_Y"], 1)
                        elif kind == "last_down":
                            mlp_down(3)
                        yield
                        continue
                    ring, _, _ = w_slot(place, t)
                    reads = {"xbc": [M_STEP["uT",]], "up": [M_STEP["hT",]]}.get(kind, [])
                    if task == ("state", 0):
                        reads = [M_STEP["BT",]]
                    w_used(pe, place, *reads, fill=t)
                    if kind == "uT":
                        pe.wait_ge(s["m_u"], i + 1)
                        last = transpose4(lambda j: ring[:, j * P:(j + 1) * P], lambda j: mu[:, j, :], ident[:])
                    elif kind == "xbc":
                        last = chunk(ring[:], W_in, uT, DIN + task[1] * P)
                    elif kind == "z":
                        last = chunk(ring[:], W_in, uT, task[1] * P)
                    elif kind == "dt":
                        for j in range(4):
                            last = pe.matmul(ring[:, MH * j:MH * (j + 1)], uT[:, j * P:(j + 1) * P], W_in[:, 2 * DIN + 2 * NS:],
                                             start=True, stop=True)
                    elif kind == "sums":
                        pe.wait_ge(s["m_a"], i + 1)
                        av = sm["a"][:].rearrange("p j h -> p (j h)")
                        pe.matmul(ring[:, 0:16], after[:], av, start=True, stop=True)
                        last = pe.matmul(ring[:, 16:32], ones[:], av, start=True, stop=True)
                    elif kind == "xsT":
                        c = task[1]
                        pe.wait_ge(s["m_xs"], 2 * i + c + 1)
                        last = transpose4(lambda j: ring[:, j * P:(j + 1) * P], lambda j: xs[c][:, j * P:(j + 1) * P], ident[:])
                    elif kind == "BT":
                        pe.wait_ge(s["m_BC"], 2 * i + 1)
                        for j in range(4):
                            last = pe.matmul(ring[:, j * NS:(j + 1) * NS], BT[:, j * P:(j + 1) * P], ident[0:NS, 0:NS],
                                             start=True, stop=True)
                    elif kind == "G":
                        pe.wait_ge(s["m_BC"], 2 * i + 2)
                        for j in range(4):
                            last = pe.matmul(ring[:, j * P:(j + 1) * P], BT[:, j * P:(j + 1) * P],
                                             CT[:, j * P:(j + 1) * P], start=True, stop=True)
                    elif kind == "decay":
                        j = task[1]
                        pe.wait_ge(s["m_MV"], 4 * i + j + 1)
                        last = pe.matmul(ring[:], after[:], MV[:, j].rearrange("p h t -> p (h t)"), start=True, stop=True)
                    elif kind == "head_decay":
                        j = task[1]
                        last = pe.matmul(ring[0:NS, :], ones[:, 0:NS], MV[:, j].rearrange("p h t -> p (h t)"), start=True, stop=True)
                    elif kind == "state":
                        j = task[1]
                        if j == 0:
                            pe.wait_ge(s["m_Xw"], i + 1)
                        last = pe.matmul(ring[0:NS, 0:MH * MP], Bt[:, j, :], Xw[:, j].rearrange("p h d -> p (h d)"),
                                         start=True, stop=True)
                    elif kind == "Y1":
                        for j in range(4):
                            last = outputs(ring, 1, j)
                    elif kind == "sumsq":
                        pe.wait_ge(s["m_gq"], 2 * i + 2)
                        for j in range(4):
                            for c in range(2):
                                last = pe.matmul(ring[:, j:j + 1], gq[c][:, j * P:(j + 1) * P], ones[:, 0:1],
                                                 start=(c == 0), stop=(c == 1))
                    elif kind == "out":
                        for j in range(4):
                            for c in range(2):
                                last = pe.matmul(ring[:, j * P:(j + 1) * P], gT[c][:, j * P:(j + 1) * P], W_out[:, c, :],
                                                 start=(c == 0), stop=(c == 1))
                    elif kind == "hT":
                        pe.wait_ge(s["m_hn"], i + 1)
                        last = transpose4(lambda j: ring[:, j * P:(j + 1) * P], lambda j: m_hn[:, j, :], ident[:])
                    elif kind == "up":
                        last = chunk(ring[:], w1, e_hT[par], task[1] * P)
                    elif kind == "back":
                        pe.wait_ge(s["m_mlT"], i + 1)
                        last = transpose4(lambda j: ring[:, j * P:(j + 1) * P], lambda j: mlT[:, j * P:(j + 1) * P], ident[:])
                    last.then_inc(s["w_filled"], 1)
                    if kind == "up" and task[1] > 0:
                        mlp_down(task[1] - 1)
                    yield

            pe.wait_ge(s["const_loaded"], 16 * len(loads))
            pe.wait_ge(s["setup_dve2"], 1)
            schedule(PAIRS, pe.Fori,
                     lambda i, k: attention(4 * i + k, k), lambda i, k: attention(4 * i + 2 + k, k),
                     lambda i, k: experts(4 * i + k, k, (i, E1_AT[k])),
                     lambda i, k: experts(4 * i + 2 + k, k, (i, E2_AT[k])),
                     lambda i, k: mamba(2 * i + k, k, (i, M_AT[k])),
                     lambda: pe.wait_ge(s["setup_weights"], 1))

        @block.scalar
        def _(act):
            def copy(dst, src):
                return act.activation(dst, src, ACT.Copy)

            def attention(n, par):
                def copy_out(g):
                    act.wait_ge(s["a_pv"], (n * GROUPS + g + 1) * len(PRODUCTS))
                    if g > 0:
                        a_used(act, n, ("back", g - 1))
                    copy(osb[:], obank[:]).then_inc(s["a_osb"], 1)

                def high():
                    for side in range(2):
                        st = stk[side][:, :, 0:MROW].rearrange("p h (k d) -> p h k d", d=HD)
                        hi = st[:, :, 0:3, :] if side == 0 else st[:, :, 2:5, :]
                        if side == 0:
                            act.wait_ge(s["a_rope"], 4 * n + 4)
                            act.wait_ge(s["a_pad"], n + 1)
                        copy(hi, rqk[side].unsqueeze(2).to_broadcast([P, 64, 3, HD])).then_inc(s["a_high"], 1)

                def middle():
                    for side in range(2):
                        st = stk[side][:, :, 0:MROW].rearrange("p h (k d) -> p h k d", d=HD)
                        md = st[:, :, 3:6:2, :] if side == 0 else st[:, :, 1:6:4, :]
                        act.wait_ge(s["a_mid"], 2 * n + side + 1)
                        copy(md, mid[side].unsqueeze(2).to_broadcast([P, 64, 2, HD])).then_inc(s["a_mid_copied"], 1)

                x = 0
                for t, task in A_TASKS:
                    kind = task[0]
                    if t is not None:
                        ring = aring[t % SLOTS]
                    if kind == "hT":
                        act.wait_ge(s["a_filled"], n * NA + t + 1)
                        act.activation(hT[:, 2:], ring[:], ACT.Identity, scale=v("ln1_w"),
                                       bias=v("ln1_b")).then_inc(a_freed[t % SLOTS], 1)
                    elif kind == "high":
                        high()
                    elif kind == "mid":
                        middle()
                    elif kind == "shift" or (kind == "qkT" and task[1] % 2 == 0):
                        act.wait_ge(s["a_filled"], n * NA + t + 1)
                        copy_stacks(copy, task, ring).then_inc(a_freed[t % SLOTS], 1)
                    elif kind == "exp":
                        act.wait_ge(s["a_filled"], n * NA + t + 1)
                        if x >= EXPS:
                            part = [x % EXPS in fills for fills, _ in PRODUCTS].index(True)
                            act.wait_ge(s["a_pv"], (n * GROUPS + x // EXPS - 1) * len(PRODUCTS) + part + 1)
                        act.activation(probs[x % EXPS], ring[:], ACT.Exp, scale=float(HD) ** -0.5).then_inc(a_freed[t % SLOTS], 1)
                        if x % EXPS == PRODUCTS[-1][1] - EXPS and x > EXPS:
                            copy_out(x // EXPS - 1)
                        x += 1
                    elif kind == "pv_last":
                        copy_out(GROUPS - 1)
                    elif kind == "yT":
                        act.wait_ge(s["a_filled"], n * NA + t + 1)
                        copy(yT[:], ring[:]).then_inc(a_freed[t % SLOTS], 1)
                    elif kind == "e_hT":
                        act.wait_ge(s["a_filled"], n * NA + t + 1)
                        act.activation(e_hT[par][:], ring[:], ACT.Identity, scale=v("ln2_w"),
                                       bias=v("ln2_b")).then_inc(a_freed[t % SLOTS], 1)
                    yield

            def experts(n, par, place):
                for t, task in E_TASKS:
                    kind = task[0]
                    if t is not None:
                        ring, freed, filled = w_slot(place, t)
                    if kind == "gate":
                        _, e, c = task
                        k = 4 * e + c
                        act.wait_ge(s["w_filled"], filled)
                        if k >= 2:
                            w_used(act, place, E_STEP[("gate",) + divmod(k - 2, 4)])
                        act.activation(tg[k % 2][:], ring[:], ACT.Tanh).then_inc(s["e_tanh"], 1)
                    elif kind == "last_down":
                        act.wait_ge(s["e_down"], n * 16 + 16)
                        copy(moT[:], acc[:]).then_inc(s["e_moT"], 1)
                    yield

            def mamba(i, par, place):
                for t, task in M_TASKS:
                    kind = task[0]
                    if t is not None:
                        ring, freed, filled = w_slot(place, t)
                    if kind in ("uT", "xbc", "z", "sums", "BT", "decay", "head_decay", "hT", "up"):
                        act.wait_ge(s["w_filled"], filled)
                    if kind == "uT":
                        copy(uT[:], ring[:]).then_inc(freed, 1)
                    elif kind == "xbc":
                        c = task[1]
                        copy(cpad[c][:, 3:], ring[:])
                        act.activation(cacc[c], ring[:], ACT.Identity, scale=v("mconv", TAPS * c + TAPS - 1),
                                       bias=v("mconv_b", c)).then_inc(freed, 1)
                    elif kind == "z":
                        act.activation(zt[task[1]][:], ring[:], ACT.Tanh).then_inc(s["m_ztanh"], 1)
                        if task[1] == 0:
                            act.wait_ge(s["m_dtexpin"], i + 1)
                            act.activation(sm["e"][:], sm["n"][:], ACT.Exp).then_inc(s["m_dtexp"], 1)
                    elif kind in ("conv", "step_size") and task != ("conv", 2):
                        k, c = {("conv", 0): (0, 2), ("conv", 1): (1, 0), ("step_size",): (2, 1)}[task]
                        act.wait_ge(s["m_conv"], 3 * i + k + 1)
                        act.activation(ct[c][:], cacc[c][:], ACT.Tanh).then_inc(s["m_ctanh"], 1)
                    elif kind == "sums":
                        act.activation(edec[:].rearrange("p a j h -> p (a j h)"), ring[:, 0:32], ACT.Exp).then_inc(freed, 1)
                    elif kind == "BT":
                        copy(Bt[:].rearrange("p j n -> p (j n)"), ring[:, 0:4 * NS]).then_inc(freed, 1)
                    elif kind == "decay":
                        j = task[1]
                        act.activation(Ld[:, j].rearrange("p h t -> p (h t)"), ring[:], ACT.Exp).then_inc(freed, 1)
                    elif kind == "head_decay":
                        j = task[1]
                        act.activation(Ed[:, j].rearrange("p h t -> p (h t)"), ring[0:NS, :], ACT.Exp).then_inc(freed, 1)
                    elif task in (("Y0", 3), ("Y1",)):
                        c = int(kind == "Y1")
                        act.wait_ge(s["m_gT"], 2 * i + c + 1)
                        act.activation(gq[c][:], gT[c][:], ACT.Square).then_inc(s["m_gq"], 1)
                    elif kind == "out":
                        for j in range(4):
                            act.wait_ge(s["m_mh"], 4 * i + j + 1)
                            if j > 0:
                                act.wait_ge(s["m_ssq"], 4 * i + j)
                            act.activation(sq[:], mh[:, j, :], ACT.Square, accum_out=ssq[:, j:j + 1]).then_inc(s["m_ssq"], 1)
                    elif kind == "hT":
                        copy(e_hT[par][:], ring[:]).then_inc(freed, 1)
                    elif kind == "up":
                        c = task[1]
                        if c >= 2:
                            act.wait_ge(s["m_ga"], 4 * i + c - 1)
                        act.activation(gb[c % 2][:], ring[:], ACT.Identity, bias=v("b1", c)).then_inc(freed, 1)
                        w_used(act, place, t)
                        act.activation(gt[c % 2][:], gb[c % 2][:], ACT.Tanh).then_inc(s["m_gtanh"], 1)
                    elif kind == "last_down":
                        act.wait_ge(s["m_mlp"], 4 * i + 4)
                        act.activation(mlT[:], acc[:], ACT.Identity, bias=v("b2")).then_inc(s["m_mlT"], 1)
                    yield

            act.wait_ge(s["const_loaded"], 16 * len(loads))
            act.wait_ge(s["setup_dve"], 1)
            act.activation(negA[:], negA[:], ACT.Exp).then_inc(s["setup_act"], 1)
            act.wait_ge(s["setup_dve2"], 1)
            for k in range(SLOTS):
                act.sem_inc(a_freed[k], 1)
                act.sem_inc(w_freed[k], 1)
            schedule(PAIRS, act.Fori,
                     lambda i, k: attention(4 * i + k, k), lambda i, k: attention(4 * i + 2 + k, k),
                     lambda i, k: experts(4 * i + k, k, (i, E1_AT[k])),
                     lambda i, k: experts(4 * i + 2 + k, k, (i, E2_AT[k])),
                     lambda i, k: mamba(2 * i + k, k, (i, M_AT[k])))

        @block.gpsimd
        def _(pool):
            def rsqrt(dst, src, ready, count, done):
                pool.wait_ge(ready, count)
                w = dst.shape[1]
                pool.tensor_tensor(dst[:], src[:], half[:, 0:w], ALU.pow).then_inc(done, 1)

            def attention(n, par, src):
                for _, task in A_TASKS:
                    kind = task[0]
                    if kind == "stats":
                        rsqrt(a_r, a_pw, s["a_var"], n + 1, s["a_rstd"])
                        pool.memset(stk[1][:, :, MROW:MROW + 3], 1.0)
                        pool.memset(stk[1][:, :, MROW + 3:], 0.0)
                        pool.memset(stk[0][:, :, MROW:MROW + 3], 0.0).then_inc(s["a_pad"], 1)
                    elif kind == "high":
                        pool.wait_ge(s["a_rstd"], n + 1)
                        pool.tensor_tensor(pool_pause[:], half[:, 0:1], half[:, 0:1], ALU.mult)
                        for j in range(4):
                            last = pool.tensor_scalar(u[:, j, :], src[:, j, :], a_mv[:, j, 0:1], a_r[:, j:j + 1],
                                                      ALU.subtract, ALU.mult)
                        last.then_inc(s["a_u"], 1)
                    elif kind == "e_stats":
                        rsqrt(e_r, e_pw, s["e_var"], n + 1, s["e_rstd"])
                    yield

            def experts(n, par):
                for _ in E_TASKS:
                    yield

            def mamba(i, par, place, x1):
                for t, task in M_TASKS:
                    kind = task[0]
                    if kind == "stats":
                        rsqrt(m_r, m_pw, s["m_var"], i + 1, s["m_rstd"])
                    elif kind == "sums":
                        pool.wait_ge(s["m_a"], i + 1)
                        for j in range(4):
                            pool.tensor_tensor(MV[:, j], upto[:].unsqueeze(1).to_broadcast([P, MH, P]),
                                               sm["a"][:, j, :].unsqueeze(2).to_broadcast([P, MH, P]),
                                               ALU.mult).then_inc(s["m_MV"], 1)
                    elif kind == "xsT" and task[1] == 1:
                        w_used(pool, place, M_STEP["sums",], M_STEP["xsT", 0], M_STEP["xsT", 1])
                        pool.tensor_tensor(Xw.rearrange("p j h d -> p (j h) d"), Xd.rearrange("p j h d -> p (j h) d"),
                                           edec[:, 0].rearrange("p j h -> p (j h)").unsqueeze(2).to_broadcast([P, 16, MP]), ALU.mult).then_inc(s["m_Xw"], 1)
                    elif kind == "decay":
                        j = task[1]
                        w_used(pool, place, M_STEP["G",], t)
                        pool.tensor_tensor(Ld[:, j], Ld[:, j], Gm[:, j].unsqueeze(1).to_broadcast([P, MH, P]),
                                           ALU.mult).then_inc(s["m_Lg"], 1)
                    elif kind == "head_decay":
                        j = task[1]
                        w_used(pool, place, t)
                        pool.tensor_tensor(Ed[:, j], Ed[:, j],
                                           CT[:, j * P:(j + 1) * P].unsqueeze(1).to_broadcast([NS, MH, P]),
                                           ALU.mult).then_inc(s["m_Ce"], 1)
                    elif kind == "sumsq":
                        rsqrt(m_r, m_pw, s["m_var2"], i + 1, s["m_rstd2"])
                    elif kind == "mh_var":
                        rsqrt(m_r, m_pw, s["m_var3"], i + 1, s["m_rstd3"])
                        pool.tensor_tensor(tmp[:], mh[:], x1[:], ALU.add).then_inc(s["m_tmp"], 1)
                    yield

            pool.memset(half[:], -0.5).then_inc(s["setup_pool"], 1)
            pool.memset(ones[:], 1.0).then_inc(s["setup_pool"], 1)
            for e in range(EXPERTS):
                pool.memset(tie[:, e:e + 1], float(EXPERTS - e)).then_inc(s["setup_pool"], 1)
            pool.memset(hT[:, 0:2], 0.0).then_inc(s["setup_pool"], 1)
            for c in range(3):
                pool.memset(cpad[c][:, 0:3], 0.0).then_inc(s["setup_pool"], 1)
            pool.memset(vx[:, :, :, HD:HD + 1], 1.0).then_inc(s["setup_pool"], 1)
            pool.memset(vx[:, :, :, HD + 1:], 0.0).then_inc(s["setup_pool"], 1)
            pool.memset(stk[0][:, :, MROW:], 0.0).then_inc(s["setup_pool"], 1)
            pool.wait_ge(s["setup_pool"], 13)
            schedule(PAIRS, pool.Fori,
                     lambda i, k: attention(4 * i + k, k, x0[k]), lambda i, k: attention(4 * i + 2 + k, k, x2[k]),
                     lambda i, k: experts(4 * i + k, k), lambda i, k: experts(4 * i + 2 + k, k),
                     lambda i, k: mamba(2 * i + k, k, (i, M_AT[k]), x1[k]))

        @block.vector
        def _(dve):
            def linker(sem, per, n):
                count = [0]

                def link(ins):
                    count[0] += 1
                    ins.then_inc(sem, 1)
                    dve.wait_ge(sem, n * per + count[0])
                return link, count

            def statistics(link, src, st, mv):
                for j in range(4):
                    last = dve.bn_stats(st[:, j, :], src[:, j, :])
                link(last)
                dve.memset(pause[:], 0.0)
                for j in range(4):
                    last = dve.bn_aggr(mv[:, j, :], st[:, j, :])
                link(last)

            def attention(n, par, src, src_ready, src_count, u1):
                link, count = linker(s["a_link"], A_LINKS, n)
                head_link, head_count = linker(s["e_head_link"], H_LINKS, n)
                pick_link, pick_count = linker(s["e_pick_link"], P_LINKS, n)
                dve.wait_ge(src_ready, src_count)
                statistics(link, src, a_st, a_mv)
                var, mean = a_mv[:, :, 1], a_mv[:, :, 0]
                link(dve.tensor_scalar(a_pw[:, 0:4], var, EPS, None, ALU.add))
                link(dve.reciprocal(a_rc[:], a_pw[:, 0:4]))
                link(dve.tensor_tensor(a_pw[:, 4:8], var, a_rc[:], ALU.mult))
                dve.tensor_scalar(a_pw[:, 4:8], a_pw[:, 4:8], EPS, None, ALU.add).then_inc(s["a_var"], 1)
                yield
                dve.wait_ge(s["a_rstd"], n + 1)
                link(dve.tensor_tensor(a_rc[:], a_r[:, 0:4], a_r[:, 4:8], ALU.mult))
                for j in range(4):
                    last = dve.tensor_scalar(hn[:, j, :], src[:, j, :], a_mv[:, j, 0:1], a_rc[:, j:j + 1], ALU.subtract, ALU.mult)
                last.then_inc(s["a_hn"], 1)
                yield
                for t, task in A_TASKS[2:]:
                    kind = task[0]
                    if t is not None:
                        ring, filled = aring[t % SLOTS], n * NA + t + 1
                    if kind == "hT":
                        a_used(dve, n, task)
                        link(dve.tensor_scalar(cT[:], hT[:, 0:T], v("aconv", 0), None, ALU.mult))
                        link(dve.scalar_tensor_tensor(out=cT[:], in0=hT[:, 1:T + 1], scalar=v("aconv", 1), in1=cT[:],
                                                      op0=ALU.mult, op1=ALU.add))
                        dve.scalar_tensor_tensor(out=cT[:], in0=hT[:, 2:T + 2], scalar=v("aconv", 2), in1=cT[:],
                                                 op0=ALU.mult, op1=ALU.add).then_inc(s["a_cT"], 1)
                    elif kind == "qkv":
                        dve.wait_ge(s["a_filled"], filled)
                        j = task[1]
                        qk = ring[:, 0:2 * P].rearrange("p (h d) -> p h d", d=HD)
                        hf = HD // 2
                        if j > 0:
                            dve.wait_ge(s["a_rope"], 4 * n + j)
                        dve.tensor_tensor(ra[:], qk, cos[:, j, :].unsqueeze(1).to_broadcast([P, 32, HD]), ALU.mult)
                        dve.tensor_tensor(rb[:, :, 0:hf], qk[:, :, hf:],
                                          sin[:, j, 0:hf].unsqueeze(1).to_broadcast([P, 32, hf]), ALU.mult)
                        dve.tensor_tensor(rb[:, :, hf:], qk[:, :, 0:hf],
                                          sin[:, j, hf:].unsqueeze(1).to_broadcast([P, 32, hf]), ALU.mult)
                        dve.tensor_copy(vx[:, j, :, 0:HD],
                                        ring[:, 2 * P:3 * P].rearrange("p (h d) -> p h d", d=HD)).then_inc(a_freed[t % SLOTS], 1)
                        a_used(dve, n, task)
                        dve.tensor_tensor(rqk[0][:, 16 * j:16 * j + 16, :], ra[:, 0:16, :], rb[:, 0:16, :], ALU.add)
                        dve.tensor_tensor(rqk[1][:, 16 * j:16 * j + 16, :], ra[:, 16:32, :], rb[:, 16:32, :],
                                          ALU.add).then_inc(s["a_rope"], 1)
                    elif kind == "qkT" and task[1] % 2:
                        dve.wait_ge(s["a_filled"], filled)
                        copy_stacks(dve.tensor_copy, task, ring).then_inc(a_freed[t % SLOTS], 1)
                    elif kind == "mid":
                        dve.wait_ge(s["a_rope"], 4 * n + 4)
                        for side in range(2):
                            dve.wait_ge(s["a_high"], 2 * n + side + 1)
                            hi = stk[side][:, :, 2 * HD:3 * HD]
                            dve.tensor_tensor(mid[side], rqk[side], hi, ALU.subtract).then_inc(s["a_mid"], 1)
                    elif kind == "low":
                        for side in range(2):
                            dve.wait_ge(s["a_mid_copied"], 2 * n + side + 1)
                            dve.wait_ge(s["a_mid"], 2 * n + side + 1)
                            lo, md = (stk[0][:, :, 4 * HD:5 * HD], stk[0][:, :, 3 * HD:4 * HD]) if side == 0 else \
                                (stk[1][:, :, 0:HD], stk[1][:, :, HD:2 * HD])
                            dve.tensor_tensor(lo, mid[side], md, ALU.subtract).then_inc(s["a_low"], 1)
                    elif kind == "max":
                        _, g, j, k = task
                        w = P * (j + 1)
                        dve.wait_ge(s["a_filled"], filled)
                        h0 = GROUP * g
                        if j >= 2:
                            src_ap, dst = ring[:, 0:w], mx[:, j, h0 + k:h0 + k + 1]
                        elif j == 1:
                            src_ap, dst = ring[:, 0:2 * w].rearrange("p (q w) -> p q w", w=w), mx[:, j, h0 + k:h0 + k + 3:2]
                        else:
                            src_ap, dst = ring[:].rearrange("p (h w) -> p h w", w=w), mx[:, j, h0:h0 + 4]
                        dve.tensor_reduce(dst, src_ap, AX_X, ALU.max).then_inc(a_freed[t % SLOTS], 1)
                        if j == 0:
                            a_used(dve, n, task, ("max", g, 1, 0), ("max", g, 1, 1))
                            rows = stk[0][:].rearrange("p (j h) k -> p j h k", j=4)[:, :, h0:h0 + GROUP, :]
                            hi, md, lo = (rows[:, :, :, MROW + k] for k in range(3))
                            m_g, t_g = mx[:, :, h0:h0 + GROUP], mt[:, :, h0:h0 + GROUP]
                            link(dve.tensor_scalar(hi, m_g, -1.0, None, ALU.mult))
                            link(dve.tensor_scalar(t_g, m_g, -1.0, None, ALU.mult))
                            link(dve.tensor_tensor(t_g, t_g, hi, ALU.subtract))
                            link(dve.tensor_copy(md, t_g))
                            dve.tensor_tensor(lo, t_g, md, ALU.subtract).then_inc(s["a_shift"], 1)
                    elif kind == "back":
                        g = task[1]
                        dve.wait_ge(s["a_filled"], filled)
                        o = ring[:].rearrange("p (j h k) -> p j h k", j=4, k=32)
                        link(dve.reciprocal(rden[:], o[:, :, :, HD]))
                        for j in range(4):
                            last = dve.tensor_tensor(y[:, j, 32 * g:32 * g + 32].rearrange("p (h d) -> p h d", d=HD),
                                                     o[:, j, :, 0:HD],
                                                     rden[:, j, :].unsqueeze(2).to_broadcast([P, GROUP, HD]), ALU.mult)
                        last.then_inc(a_freed[t % SLOTS], 1)
                    elif kind == "proj":
                        dve.wait_ge(s["a_proj"], n + 1)
                        dve.wait_ge(s["a_u"], n + 1)
                        dve.tensor_tensor(u1[:], u[:], obank[:].rearrange("p (j c) -> p j c", j=4), ALU.add).then_inc(s["a_u1"], 1)
                        assert count[0] == A_LINKS, count
                    elif kind == "e_stats":
                        dve.wait_ge(s["a_u1"], n + 1)
                        statistics(head_link, u1, e_st, e_mv)
                        assert head_count[0] == H_LINKS, head_count
                        dve.tensor_scalar(e_pw[:], e_mv[:, :, 1], EPS, None, ALU.add).then_inc(s["e_var"], 1)
                    elif kind == "e_norm":
                        dve.wait_ge(s["e_rstd"], n + 1)
                        for j in range(4):
                            last = dve.tensor_scalar(e_hn[:, j, :], u1[:, j, :], e_mv[:, j, 0:1], e_r[:, j:j + 1],
                                                     ALU.subtract, ALU.mult)
                        last.then_inc(s["e_hn"], 1)
                    elif kind == "logits":
                        dve.wait_ge(s["a_filled"], filled)
                        lg = ring[:, 0:4 * EXPERTS].rearrange("p (j e) -> p j e", e=EXPERTS)
                        pick_link(dve.tensor_reduce(lmax[:], lg, AX_X, ALU.max))
                        pick_link(dve.tensor_tensor(lsel[:], lg, lmax[:].unsqueeze(2).to_broadcast([P, 4, EXPERTS]), ALU.is_equal))
                        dve.sem_inc(a_freed[t % SLOTS], 1)
                        pick_link(dve.tensor_tensor(lsel[:], lsel[:], tie[:].unsqueeze(1).to_broadcast([P, 4, EXPERTS]), ALU.mult))
                        pick_link(dve.tensor_reduce(lmax[:], lsel[:], AX_X, ALU.max))
                        dve.tensor_tensor(pick[par][:], lsel[:], lmax[:].unsqueeze(2).to_broadcast([P, 4, EXPERTS]),
                                          ALU.is_equal).then_inc(s["e_pick"], 1)
                        assert pick_count[0] == P_LINKS, pick_count
                    yield

            def experts(n, par, place, u1, src, dst, result):
                link, count = linker(s["e_link"], E_LINKS, n)

                for t, task in E_TASKS:
                    kind = task[0]
                    if t is not None:
                        ring, freed, filled = w_slot(place, t)
                    if kind in ("mask", "back"):
                        dve.wait_ge(s["w_filled"], filled)
                    if kind == "mask":
                        e = task[1]
                        a_used(dve, n, ("e_hT",))
                        dve.tensor_tensor(hm[e % 2][:], e_hT[par][:], ring[:], ALU.mult).then_inc(freed, 1)
                    elif kind == "value":
                        _, e, c = task
                        k = 4 * e + c
                        gate = E_STEP["gate", e, c]
                        gate_ring, gate_freed, _ = w_slot(place, gate)
                        dve.wait_ge(s["e_tanh"], n * 16 + k + 1)
                        dve.scalar_tensor_tensor(out=sg[k % 2][:], in0=tg[k % 2][:], scalar=1.0, in1=gate_ring[:], op0=ALU.add,
                                                 op1=ALU.mult).then_inc(gate_freed, 1)
                        if k >= 2:
                            dve.wait_ge(s["e_down"], n * 16 + k - 1)
                        w_used(dve, place, gate)
                        dve.wait_ge(s["w_filled"], filled)
                        dve.tensor_tensor(ya[k % 2][:], sg[k % 2][:], ring[:], ALU.mult).then_inc(freed, 1)
                    elif kind == "back":
                        link(dve.tensor_tensor(tmp[:], u1[:], ring[:].rearrange("p (j c) -> p j c", j=4), ALU.add))
                        dve.sem_inc(freed, 1)
                        if result is not None:
                            dve.wait_ge(s["out_stored"], 16 * result + 16)
                        dve.scalar_tensor_tensor(out=dst[:].rearrange("p j c -> p (j c)"),
                                                 in0=tmp[:].rearrange("p j c -> p (j c)"), scalar=0.5,
                                                 in1=src[:].rearrange("p j c -> p (j c)"), op0=ALU.mult,
                                                 op1=ALU.add).then_inc(s["e_x"], 1)
                        dve.wait_ge(s["e_x"], n + 1)
                        if result is None:
                            dve.sem_inc(x_free[x0.index(src)], 1)
                        assert count[0] == E_LINKS, count
                    yield

            def mamba(i, par, place, x1, x2):
                link, count = linker(s["m_link"], M_LINKS, i)

                statistics(link, x1, m_st, m_mv)
                dve.tensor_scalar(m_pw[:], m_mv[:, :, 1], EPS, None, ALU.add).then_inc(s["m_var"], 1)
                yield
                dve.wait_ge(s["m_rstd"], i + 1)
                for j in range(4):
                    last = dve.tensor_scalar(mu[:, j, :], x1[:, j, :], m_mv[:, j, 0:1], m_r[:, j:j + 1], ALU.subtract, ALU.mult)
                last.then_inc(s["m_u"], 1)
                yield

                def convolve(c):
                    w_used(dve, place, M_STEP["xbc", c])
                    for q in range(TAPS - 1):
                        ins = dve.scalar_tensor_tensor(out=cacc[c][:], in0=cpad[c][:, q:q + T],
                                                       scalar=v("mconv", TAPS * c + q), in1=cacc[c][:],
                                                       op0=ALU.mult, op1=ALU.add)
                        if q < TAPS - 2:
                            link(ins)
                    ins.then_inc(s["m_conv"], 1)

                def silu(dst, th, h):
                    return dve.scalar_tensor_tensor(out=dst, in0=th, scalar=1.0, in1=h, op0=ALU.add, op1=ALU.mult)

                def step_size():
                    S = {k: sm[k][:] for k in sm}
                    flat = {k: sm[k][:].rearrange("p j h -> p (j h)") for k in sm}
                    dve.wait_ge(s["m_dtexp"], i + 1)
                    link(dve.tensor_scalar(S["d"], S["e"], 2.0, None, ALU.add))
                    link(dve.reciprocal(S["r"], S["d"]))
                    link(dve.tensor_tensor(S["z"], S["e"], S["r"], ALU.mult))
                    link(dve.tensor_tensor(S["z2"], S["z"], S["z"], ALU.mult))
                    link(dve.tensor_scalar(S["p"], S["z2"], 1.0 / (2 * ATANH_TERMS - 1), None, ALU.mult))
                    for k in range(ATANH_TERMS - 2, 0, -1):
                        link(dve.scalar_tensor_tensor(out=flat["p"], in0=flat["p"], scalar=1.0 / (2 * k + 1),
                                                      in1=flat["z2"], op0=ALU.add, op1=ALU.mult))
                    link(dve.scalar_tensor_tensor(out=flat["q"], in0=flat["p"], scalar=1.0, in1=flat["z"], op0=ALU.add, op1=ALU.mult))
                    link(dve.tensor_scalar(S["w"], S["x"], 0.0, None, ALU.max))
                    link(dve.scalar_tensor_tensor(out=flat["dt"], in0=flat["q"], scalar=2.0, in1=flat["w"], op0=ALU.mult,
                                                  op1=ALU.add))
                    link(dve.tensor_tensor(S["w"], S["dt"], negA[:].unsqueeze(1).to_broadcast([P, 4, MH]), ALU.mult))
                    dve.tensor_scalar(S["a"], S["w"], -1000.0, None, ALU.max).then_inc(s["m_a"], 1)

                for t, task in M_TASKS[2:]:
                    kind = task[0]
                    if t is not None:
                        ring, freed, filled = w_slot(place, t)
                    if task in (("Y0", 3), ("Y1",)):
                        c = int(kind == "Y1")
                        if c == 0:
                            dve.wait_ge(s["m_Y"], i + 1)
                        else:
                            dve.wait_ge(s["m_gT"], 2 * i + 1)
                            dve.wait_ge(s["w_filled"], filled)
                        dve.scalar_tensor_tensor(out=e_hT[par][:], in0=xs[c][:], scalar=v("D", c),
                                                 in1=(ring if c else acc)[:], op0=ALU.mult,
                                                 op1=ALU.add).then_inc(s["m_yd"], 1)
                        dve.wait_ge(s["m_yd"], 2 * i + c + 1)
                        dve.tensor_tensor(gT[c][:], e_hT[par][:], zs[c][:], ALU.mult).then_inc(s["m_gT"], 1)
                        if c == 1:
                            dve.sem_inc(freed, 1)
                    if kind in ("dt", "z", "xsT", "G", "state", "sumsq", "out", "back"):
                        dve.wait_ge(s["w_filled"], filled)
                    if kind == "dt":
                        link(dve.tensor_tensor(sm["x"][:], ring[:, 0:4 * MH].rearrange("p (j h) -> p j h", h=MH),
                                               v("dt_bias", 0, MH).unsqueeze(1).to_broadcast([P, 4, MH]), ALU.add))
                        dve.sem_inc(freed, 1)
                        fx = sm["x"][:].rearrange("p j h -> p (j h)")
                        dve.scalar_tensor_tensor(out=sm["n"][:].rearrange("p j h -> p (j h)"), in0=fx, scalar=-1.0, in1=fx,
                                                 op0=ALU.mult, op1=ALU.min).then_inc(s["m_dtexpin"], 1)
                    elif kind == "z":
                        c = task[1]
                        dve.wait_ge(s["m_ztanh"], 2 * i + c + 1)
                        silu(zs[c][:], zt[c][:], ring[:]).then_inc(freed, 1)
                    elif kind == "conv":
                        convolve(task[1])
                    elif kind == "step_size":
                        step_size()
                    elif kind == "BC":
                        dve.wait_ge(s["m_ctanh"], 3 * i + 1)
                        silu(BT[:], ct[2][0:NS, :], cacc[2][0:NS, :]).then_inc(s["m_BC"], 1)
                        silu(CT[:], ct[2][NS:P, :], cacc[2][NS:P, :]).then_inc(s["m_BC"], 1)
                    elif kind == "xs":
                        c = task[1]
                        dve.wait_ge(s["m_ctanh"], 3 * i + c + 2)
                        silu(xs[c][:], ct[c][:], cacc[c][:]).then_inc(s["m_xs"], 1)
                    elif kind == "xsT":
                        c = task[1]
                        r4 = ring[:].rearrange("p (j a d) -> p j a d", j=4, a=2)
                        for j in range(4):
                            last = dve.tensor_tensor(Xd[:, j, 2 * c:2 * c + 2, :], r4[:, j],
                                                     sm["dt"][:, j, 2 * c:2 * c + 2].unsqueeze(2).to_broadcast([P, 2, MP]), ALU.mult)
                        last.then_inc(freed, 1)
                    elif kind == "G":
                        dve.tensor_tensor(Gm[:], ring[:].rearrange("p (j t) -> p j t", j=4),
                                          upto[:].unsqueeze(1).to_broadcast([P, 4, P]), ALU.mult).then_inc(freed, 1)
                    elif kind == "state":
                        j = task[1]
                        new = ring[0:NS, 0:MH * MP].rearrange("p (h d) -> p h d", d=MP)
                        if j == 0:
                            dve.tensor_copy(St[:, 1], new).then_inc(freed, 1)
                        else:
                            w_used(dve, place, M_STEP["sums",], t - 1)
                            link(dve.tensor_tensor(St[:, 0], St[:, j],
                                                   edec[0:NS, 1, j, :].unsqueeze(2).to_broadcast([NS, MH, MP]), ALU.mult))
                            dve.tensor_tensor(St[:, j + 1], St[:, 0], new, ALU.add).then_inc(freed, 1)
                    elif kind == "sumsq":
                        link(dve.tensor_scalar(m_pw[:], ring[:, 0:4], 1.0 / DIN, EPS, ALU.mult, ALU.add))
                        dve.sem_inc(freed, 1)
                        dve.sem_inc(s["m_var2"], 1)
                    elif kind == "out":
                        dve.wait_ge(s["m_rstd2"], i + 1)
                        for j in range(4):
                            dve.scalar_tensor_tensor(out=mh[:, j, :], in0=ring[:, j * P:(j + 1) * P],
                                                     scalar=m_r[:, j:j + 1], in1=mu[:, j, :],
                                                     op0=ALU.mult, op1=ALU.add).then_inc(s["m_mh"], 1)
                        dve.wait_ge(s["m_mh"], 4 * i + 4)
                        dve.sem_inc(freed, 1)
                    elif kind == "mh_var":
                        dve.wait_ge(s["m_ssq"], 4 * i + 4)
                        dve.tensor_scalar(m_pw[:], ssq[:], 1.0 / P, EPS, ALU.mult, ALU.add).then_inc(s["m_var3"], 1)
                    elif kind == "mh_norm":
                        dve.wait_ge(s["m_rstd3"], i + 1)
                        for j in range(4):
                            last = dve.tensor_scalar(m_hn[:, j, :], mh[:, j, :], m_r[:, j:j + 1], None, ALU.mult)
                        last.then_inc(s["m_hn"], 1)
                    elif kind == "up":
                        c = task[1]
                        dve.wait_ge(s["m_gtanh"], 4 * i + c + 1)
                        if c >= 2:
                            dve.wait_ge(s["m_mlp"], 4 * i + c - 1)
                        silu(ga[c % 2][:], gt[c % 2][:], gb[c % 2][:]).then_inc(s["m_ga"], 1)
                    elif kind == "back":
                        dve.wait_ge(s["m_tmp"], i + 1)
                        dve.tensor_tensor(x2[:], tmp[:], ring[:].rearrange("p (j c) -> p j c", j=4), ALU.add).then_inc(s["m_x"], 1)
                        dve.wait_ge(s["m_x"], i + 1)
                        dve.sem_inc(freed, 1)
                        assert count[0] == M_LINKS, count
                    yield

            sc = 0

            def step(ins):
                nonlocal sc
                sc += 1
                ins.then_inc(s["setup_chain"], 1)

            dve.wait_ge(s["const_loaded"], 16 * len(loads))
            dve.tensor_scalar(negA[:], v("A_log", 0, MH), 88.0, None, ALU.min).then_inc(s["setup_dve"], 1)
            step(dve.tensor_copy(identb[:], ident[:]))
            step(dve.tensor_scalar(neg_queries[:], after[:], NEG, None, ALU.mult))
            step(dve.tensor_scalar(v("mconv", 0, 12), v("mconv", 0, 12), 0.5, None, ALU.mult))
            step(dve.tensor_scalar(v("mconv_b", 0, 3), v("mconv_b", 0, 3), 0.5, None, ALU.mult))
            step(dve.tensor_scalar(v("b1", 0, 4), v("b1", 0, 4), 0.5, None, ALU.mult))
            dve.wait_ge(s["setup_chain"], sc)
            step(dve.memset(stq[0][STACK:P], 0.0))
            step(dve.memset(stq[1][0:STACK], 0.0))
            step(dve.tensor_tensor(tmp[:, 0, :], upto[:], ident[:], ALU.subtract))
            dve.wait_ge(s["setup_chain"], sc)
            step(dve.tensor_scalar(neg_keys[:], tmp[:, 0, :], NEG, None, ALU.mult))
            dve.wait_ge(s["setup_act"], 1)
            step(dve.tensor_scalar(negA[:], negA[:], -1.0, None, ALU.mult))
            dve.wait_ge(s["setup_chain"], sc)
            dve.wait_ge(s["setup_pool"], 13)
            dve.sem_inc(s["setup_dve2"], 1)

            def weights():
                dve.wait_ge(s["weights_loaded"], 16 * len(wloads))
                for e in range(EXPERTS):
                    step(dve.tensor_scalar(wv[:, e, 0:DFF], wv[:, e, 0:DFF], 0.5, None, ALU.mult))
                step(dve.tensor_scalar(W_in[:, 0:DIN], W_in[:, 0:DIN], 0.5, None, ALU.mult))
                step(dve.tensor_scalar(w1[:], w1[:], v("rms_w"), 0.5, ALU.mult, ALU.mult))
                for c in range(2):
                    step(dve.tensor_scalar(W_out[:, c, :], W_out[:, c, :], v("norm_w", c), None, ALU.mult))
                dve.wait_ge(s["setup_chain"], sc)
                dve.sem_inc(s["setup_weights"], 1)

            schedule(PAIRS, dve.Fori,
                     lambda i, k: attention(4 * i + k, k, x0[k], x_loaded[k], 16 * i + 16, u1[k]),
                     lambda i, k: attention(4 * i + 2 + k, k, x2[k], s["m_x"], 2 * i + k + 1, u1[k]),
                     lambda i, k: experts(4 * i + k, k, (i, E1_AT[k]), u1[k], x0[k], x1[k], None),
                     lambda i, k: experts(4 * i + 2 + k, k, (i, E2_AT[k]), u1[k], x2[k], x3, 2 * i + k),
                     lambda i, k: mamba(2 * i + k, k, (i, M_AT[k]), x1[k], x2[k]), weights)


_WEIGHTS = {"attn_w": "L0_ffn_attn_w", "proj_w": "L0_ffn_proj_w", "wv": "L0_ffn_expert_wv", "ep": "L0_ffn_expert_proj",
            "W_in": "L0_attn_W_in", "W_out": "L0_attn_W_out", "w1": "L0_attn_mlp_w1", "w2": "L0_attn_mlp_w2"}


def packed_vectors(inputs):
    import numpy as np

    def get(name):
        return np.asarray(inputs[name])

    def rows(a):
        return np.broadcast_to(a[None, :], (P, a.shape[0]))

    cols = {
        "ln1_w": get("L0_ffn_ln1_w")[:, None], "ln1_b": get("L0_ffn_ln1_b")[:, None],
        "ln2_w": get("L0_ffn_ln2_w")[:, None], "ln2_b": get("L0_ffn_ln2_b")[:, None],
        "aconv": get("L0_ffn_conv_w")[:, 0, :], "router": get("L0_ffn_router_w"),
        "mconv": get("L0_attn_conv_w").reshape(3, P, TAPS).transpose(1, 0, 2).reshape(P, 3 * TAPS),
        "mconv_b": get("L0_attn_conv_b").reshape(3, P).T,
        "dt_bias": rows(get("L0_attn_dt_bias")), "A_log": rows(get("L0_attn_A_log")),
        "D": np.repeat(get("L0_attn_D_param"), MP).reshape(2, P).T,
        "norm_w": get("L0_attn_norm_w").reshape(2, P).T, "rms_w": get("L0_attn_rms_w")[:, None],
        "b1": get("L0_attn_mlp_b1").reshape(4, P).T, "b2": get("L0_attn_mlp_b2")[:, None],
    }
    return np.ascontiguousarray(np.concatenate([cols[name] for name in PACK], axis=1))


def shape_constants(T):
    import numpy as np
    r = np.arange(P)
    upto = (r[:, None] <= r[None, :]).astype(np.float32)
    after = (r[:, None] > r[None, :]).astype(np.float32)
    inv = (np.float32(1.0) / np.float32(10000.0) ** (np.arange(0, HD, 2, dtype=np.float32) / np.float32(HD))).astype(np.float32)
    ang = np.arange(T, dtype=np.float32)[:, None] * inv[None, :]
    ang = np.concatenate([ang, ang], axis=1)
    sign = np.where(np.arange(HD) < HD // 2, np.float32(-1), np.float32(1))
    cos = np.cos(ang).astype(np.float32).reshape(T // P, P, HD).transpose(1, 0, 2).reshape(P, -1)
    sin = (np.sin(ang) * sign).astype(np.float32).reshape(T // P, P, HD).transpose(1, 0, 2).reshape(P, -1)
    return np.ascontiguousarray(np.concatenate([np.eye(P, dtype=np.float32), upto, after, cos, sin], axis=1))


def kernel(**inputs):
    import numpy as np
    import concourse.bacc as bacc
    from concourse.bass_utils import run_bass_kernel_spmd

    x = np.ascontiguousarray(inputs["L0_attn_hidden_tokens"])
    host = {"x": x, "packed": packed_vectors(inputs), "consts": shape_constants(x.shape[1])}
    host.update({k: np.ascontiguousarray(inputs[n]) for k, n in _WEIGHTS.items()})
    nc = bacc.Bacc("TRN2", target_bir_lowering=False, num_devices=1)
    A = {k: nc.dram_tensor(f"in_{k}", a.shape, F32, kind="ExternalInput").ap() for k, a in host.items()}
    A["out"] = nc.dram_tensor("out_x", x.shape, F32, kind="ExternalOutput").ap()
    build_program(nc, A)
    r = run_bass_kernel_spmd(nc, [{f"in_{k}": a for k, a in host.items()}], core_ids=[0])
    return r.results[0]["out_x"]
```
